# Optimizing a Trainium2 kernel written in Bass

```python
import numpy as np
import jax
import jax.numpy as jnp

def _softmax(x, axis=-1):
    return jax.nn.softmax(x, axis=axis)

def _gelu(x):
    return jax.nn.gelu(x, approximate=True)

def _silu(x):
    return jax.nn.silu(x)

def _sigmoid(x):
    return jax.nn.sigmoid(x)

def _layernorm(x, axis=-1, eps=1e-05):
    m = jnp.mean(x, axis=axis, keepdims=True)
    v = jnp.var(x, axis=axis, keepdims=True)
    return (x - m) / jnp.sqrt(v + eps)

def _scatter_add(tgt, idx, src, axis=0):
    return tgt.at[idx].add(src)

def _segment_sum(src, seg, n):
    return jax.ops.segment_sum(src, seg, n)
kernel_name = 'mk_xattn_ffn_d2_seqx_r4_2aaeaa'

def setup_inputs(seed: int=0):
    np.random.seed(seed)
    _w = jnp.asarray

    def _rec_inputs():
        import jax
        import jax.numpy as jnp
        _rk = jax.random.key(seed)
        x = -0.0003929 + 0.9999 * jax.random.normal(jax.random.fold_in(_rk, 1), (2, 512, 1024), jnp.float32)
        _lenS = 512 - jax.random.randint(jax.random.fold_in(_rk, 7), (2,), 0, max(1, 512 // 4) + 1, jnp.int32)
        _lenS2 = 1024 - jax.random.randint(jax.random.fold_in(_rk, 8), (2,), 0, max(1, 1024 // 4) + 1, jnp.int32)
        _ctx_4096P = jax.random.normal(jax.random.fold_in(_rk, 11), (2, 16, 1024), jnp.float32)
        _ctx_4096c = jax.random.dirichlet(jax.random.fold_in(_rk, 511), 0.3 * jnp.ones((16,), jnp.float32), (2, 1024))
        _ctx_4096t = jnp.einsum('bsk,bkd->bsd', _ctx_4096c, _ctx_4096P)
        _ctx_4096t = _ctx_4096t * jax.lax.rsqrt(jnp.mean(jnp.square(_ctx_4096t)) + 1e-12) * 0.953939
        ctx_4096 = 2.81802e-05 + 1.00001 * (_ctx_4096t + 0.3 * jax.random.normal(jax.random.fold_in(_rk, 611), (2, 1024, 1024), jnp.float32))
        _validS = jnp.arange(512)[None, :] < _lenS[:, None]
        _validS2 = jnp.arange(1024)[None, :] < _lenS2[:, None]
        _causal = jnp.tril(jnp.ones((512, 512), dtype=bool))
        mask_BxSxS2_ff0 = jnp.where(jnp.ones((2, 512, 1024), dtype=bool), 0.0, -1000000000.0).astype(jnp.float32)
        return (x, ctx_4096, mask_BxSxS2_ff0)
    x, ctx_4096, mask_BxSxS2_ff0 = _rec_inputs()

    def _L0_xattn_setup():
        import jax, jax.numpy as jnp
        import numpy as np
        BS, SEQ, D_MODEL = (4, 256, 1024)
        N_Q_HEADS, N_KV_HEADS, D_K, D_V = (32, 8, 128, 128)
        ROPE_BASE = 10000.0

        def _rotate_half(x):
            x1, x2 = jnp.split(x, 2, axis=-1)
            return jnp.concatenate([-x2, x1], axis=-1)

        def _apply_rope(x, pos0):
            d = x.shape[-1]
            seq = x.shape[2]
            inv_freq = 1.0 / ROPE_BASE ** (jnp.arange(0, d, 2, dtype=jnp.float32) / d)
            pos = (pos0 + jnp.arange(seq)).astype(jnp.float32)
            ang = pos[:, None] * inv_freq[None, :]
            cos = jnp.concatenate([jnp.cos(ang), jnp.cos(ang)], axis=-1)
            sin = jnp.concatenate([jnp.sin(ang), jnp.sin(ang)], axis=-1)
            return x * cos[None, None] + _rotate_half(x) * sin[None, None]
        key = jax.random.key(seed)
        ks = jax.random.split(key, 8)
        w_scale = 0.02
        return {'query': jax.random.normal(ks[0], (BS, SEQ, D_MODEL), dtype=jnp.float32), 'key': jax.random.normal(ks[1], (BS, SEQ, D_MODEL), dtype=jnp.float32), 'value': jax.random.normal(ks[2], (BS, SEQ, D_MODEL), dtype=jnp.float32), 'mask': jnp.zeros((BS, SEQ, SEQ), dtype=jnp.float32), 'wq': jax.random.normal(ks[3], (D_MODEL, N_Q_HEADS * D_K), dtype=jnp.float32) * w_scale, 'wk': jax.random.normal(ks[4], (D_MODEL, N_KV_HEADS * D_K), dtype=jnp.float32) * w_scale, 'wv': jax.random.normal(ks[5], (D_MODEL, N_KV_HEADS * D_V), dtype=jnp.float32) * w_scale, 'wo': jax.random.normal(ks[6], (N_Q_HEADS * D_V, D_MODEL), dtype=jnp.float32) * w_scale, 'curr_seq_pos': 0}
    _L0_xattn_all = _L0_xattn_setup()
    _L0_xattn_in = {k: v for k, v in _L0_xattn_all.items() if k in ('wq', 'wk', 'wv', 'wo')}
    del _L0_xattn_all

    def _L0_ffn_setup():
        import jax, jax.numpy as jnp
        import numpy as np
        K_TOP = 8
        key = jax.random.key(seed)
        k1, k2, k3 = jax.random.split(key, 3)
        B, S, H, E = (4, 1024, 1024, 64)
        hidden_states = jax.random.normal(k1, (B, S, H), dtype=jnp.float32)
        router_weight = jax.random.normal(k2, (E, H), dtype=jnp.float32)
        router_bias = jnp.zeros((E,), dtype=jnp.float32)
        expert_bias = jax.random.normal(k3, (E, H), dtype=jnp.float32) * 0.1
        return {'hidden_states': hidden_states, 'router_weight': router_weight, 'router_bias': router_bias, 'expert_bias': expert_bias}
    _L0_ffn_all = _L0_ffn_setup()
    _L0_ffn_in = {k: v for k, v in _L0_ffn_all.items() if k in ('router_weight', 'router_bias', 'expert_bias')}
    del _L0_ffn_all

    def _L1_xattn_setup():
        import jax, jax.numpy as jnp
        import numpy as np
        QMIN = 0.0
        QMAX = 255.0

        def fake_quant(x, scale, zp):
            s = scale.reshape(())
            z = zp.reshape(())
            q = jnp.clip(jnp.round(x / s + z), QMIN, QMAX)
            return (q - z) * s
        key = jax.random.key(seed)
        k1, k2 = jax.random.split(key)
        B, M, K, N = (4, 512, 1024, 1024)
        x1 = jax.random.normal(k1, (B, M, K), dtype=jnp.float32)
        x2 = jax.random.normal(k2, (B, K, N), dtype=jnp.float32)
        x1_scale = jnp.full((1,), 8.0 / 255.0, dtype=jnp.float32)
        x1_zp = jnp.full((1,), 128.0, dtype=jnp.float32)
        x2_scale = jnp.full((1,), 8.0 / 255.0, dtype=jnp.float32)
        x2_zp = jnp.full((1,), 128.0, dtype=jnp.float32)
        return {'x1': x1, 'x2': x2, 'x1_scale': x1_scale, 'x1_zp': x1_zp, 'x2_scale': x2_scale, 'x2_zp': x2_zp}
    _L1_xattn_all = _L1_xattn_setup()
    _L1_xattn_in = {k: v for k, v in _L1_xattn_all.items() if k in ('x1_scale', 'x1_zp', 'x2_scale', 'x2_zp')}
    del _L1_xattn_all

    def _L1_ffn_setup():
        import jax, jax.numpy as jnp
        import numpy as np
        NF4_CODE = jnp.array([-1.0, -0.6961928009986877, -0.5250730514526367, -0.39491748809814453, -0.28444138169288635, -0.18477343022823334, -0.09105003625154495, 0.0, 0.07958029955625534, 0.16093020141124725, 0.24611230194568634, 0.33791524171829224, 0.44070982933044434, 0.5626170039176941, 0.7229568362236023, 1.0], dtype=jnp.float32)
        BLOCKSIZE = 64

        def nf4_quant_dequant(w):
            shape = w.shape
            flat = w.reshape(-1, BLOCKSIZE)
            absmax = jnp.max(jnp.abs(flat), axis=1, keepdims=True)
            normalized = flat / jnp.where(absmax == 0, 1.0, absmax)
            bounds = (NF4_CODE[:-1] + NF4_CODE[1:]) * 0.5
            idx = jnp.searchsorted(bounds, normalized)
            return (NF4_CODE[idx] * absmax).reshape(shape)
        key = jax.random.key(seed)
        k1, k2, k3, kx = jax.random.split(key, 4)
        D, H = (1024, 2752)
        scale = 0.02
        w1 = jax.random.normal(k1, (H, D), jnp.float32) * scale
        w2 = jax.random.normal(k2, (H, D), jnp.float32) * scale
        w3 = jax.random.normal(k3, (D, H), jnp.float32) * scale
        x = jax.random.normal(kx, (2, 512, D), jnp.float32)
        return {'x': x, 'w1': w1, 'w2': w2, 'w3': w3}
    _L1_ffn_all = _L1_ffn_setup()
    _L1_ffn_in = {k: v for k, v in _L1_ffn_all.items() if k in ('w1', 'w2', 'w3')}
    del _L1_ffn_all
    return {'x': x, 'ctx_4096': ctx_4096, 'mask_BxSxS2_ff0': mask_BxSxS2_ff0, 'L0_xattn_wq': _L0_xattn_in['wq'], 'L0_xattn_wk': _L0_xattn_in['wk'], 'L0_xattn_wv': _L0_xattn_in['wv'], 'L0_xattn_wo': _L0_xattn_in['wo'], 'L0_ffn_router_weight': _L0_ffn_in['router_weight'], 'L0_ffn_router_bias': _L0_ffn_in['router_bias'], 'L0_ffn_expert_bias': _L0_ffn_in['expert_bias'], 'L1_xattn_x1_scale': _L1_xattn_in['x1_scale'], 'L1_xattn_x1_zp': _L1_xattn_in['x1_zp'], 'L1_xattn_x2_scale': _L1_xattn_in['x2_scale'], 'L1_xattn_x2_zp': _L1_xattn_in['x2_zp'], 'L1_ffn_w1': _L1_ffn_in['w1'], 'L1_ffn_w2': _L1_ffn_in['w2'], 'L1_ffn_w3': _L1_ffn_in['w3']}

def reference(x, ctx_4096, mask_BxSxS2_ff0, L0_xattn_wq, L0_xattn_wk, L0_xattn_wv, L0_xattn_wo, L0_ffn_router_weight, L0_ffn_router_bias, L0_ffn_expert_bias, L1_xattn_x1_scale, L1_xattn_x1_zp, L1_xattn_x2_scale, L1_xattn_x2_zp, L1_ffn_w1, L1_ffn_w2, L1_ffn_w3):
    import jax
    import jax.numpy as jnp

    def _L0_xattn_ref(query, key, value, mask, wq, wk, wv, wo, curr_seq_pos):
        import jax, jax.numpy as jnp
        import numpy as np
        BS, SEQ, D_MODEL = (4, 256, 1024)
        N_Q_HEADS, N_KV_HEADS, D_K, D_V = (32, 8, 128, 128)
        ROPE_BASE = 10000.0

        def _rotate_half(x):
            x1, x2 = jnp.split(x, 2, axis=-1)
            return jnp.concatenate([-x2, x1], axis=-1)

        def _apply_rope(x, pos0):
            d = x.shape[-1]
            seq = x.shape[2]
            inv_freq = 1.0 / ROPE_BASE ** (jnp.arange(0, d, 2, dtype=jnp.float32) / d)
            pos = (pos0 + jnp.arange(seq)).astype(jnp.float32)
            ang = pos[:, None] * inv_freq[None, :]
            cos = jnp.concatenate([jnp.cos(ang), jnp.cos(ang)], axis=-1)
            sin = jnp.concatenate([jnp.sin(ang), jnp.sin(ang)], axis=-1)
            return x * cos[None, None] + _rotate_half(x) * sin[None, None]
        bs, sq, _ = query.shape
        n_groups = N_Q_HEADS // N_KV_HEADS
        q = (query @ wq).reshape(bs, sq, N_Q_HEADS, D_K).transpose((0, 2, 1, 3))
        sk = key.shape[1]
        k = (key @ wk).reshape(bs, sk, N_KV_HEADS, 1, D_K)
        k = jnp.repeat(k, n_groups, axis=3).reshape(bs, sk, N_Q_HEADS, D_K).transpose((0, 2, 1, 3))
        v = (value @ wv).reshape(bs, sk, N_KV_HEADS, 1, D_V)
        v = jnp.repeat(v, n_groups, axis=3).reshape(bs, sk, N_Q_HEADS, D_V).transpose((0, 2, 1, 3))
        scale = jnp.sqrt(jnp.float32(D_K))
        q = _apply_rope(q, curr_seq_pos)
        k = _apply_rope(k, curr_seq_pos)
        raw = jnp.einsum('bhqd,bhkd->bhqk', q, k) / scale
        masked = raw + mask[:bs, None, curr_seq_pos:curr_seq_pos + sq, :sk]
        attn = jax.nn.softmax(masked, axis=-1)
        out = jnp.einsum('bhqk,bhkd->bhqd', attn, v)
        out = out.transpose((0, 2, 1, 3)).reshape(bs, sq, N_Q_HEADS * D_V)
        return out @ wo

    def _L0_ffn_ref(hidden_states, router_weight, router_bias, expert_bias):
        import jax, jax.numpy as jnp
        import numpy as np
        K_TOP = 8
        B, S, H = hidden_states.shape
        E = router_weight.shape[0]
        T = B * S
        flat = hidden_states.reshape(T, H)
        logits = jnp.einsum('th,eh->te', flat, router_weight) + router_bias
        scores = jax.nn.softmax(logits, axis=-1)
        topk_w, topk_idx = jax.lax.top_k(scores, K_TOP)
        w_sum = topk_w.sum(axis=-1, keepdims=True)
        w_dense = jnp.zeros((T, E), dtype=scores.dtype).at[jnp.arange(T)[:, None], topk_idx].add(topk_w)
        bias_mix = jnp.einsum('te,eh->th', w_dense, expert_bias)
        out = flat * w_sum + bias_mix
        return out.reshape(B, S, H)

    def _L1_xattn_ref(x1, x2, x1_scale, x1_zp, x2_scale, x2_zp):
        import jax, jax.numpy as jnp
        import numpy as np
        QMIN = 0.0
        QMAX = 255.0

        def fake_quant(x, scale, zp):
            s = scale.reshape(())
            z = zp.reshape(())
            q = jnp.clip(jnp.round(x / s + z), QMIN, QMAX)
            return (q - z) * s
        q1 = fake_quant(x1, x1_scale, x1_zp)
        q2 = fake_quant(x2, x2_scale, x2_zp)
        return jnp.matmul(q1, q2)

    def _L1_ffn_ref(x, w1, w2, w3):
        import jax, jax.numpy as jnp
        import numpy as np
        NF4_CODE = jnp.array([-1.0, -0.6961928009986877, -0.5250730514526367, -0.39491748809814453, -0.28444138169288635, -0.18477343022823334, -0.09105003625154495, 0.0, 0.07958029955625534, 0.16093020141124725, 0.24611230194568634, 0.33791524171829224, 0.44070982933044434, 0.5626170039176941, 0.7229568362236023, 1.0], dtype=jnp.float32)
        BLOCKSIZE = 64

        def nf4_quant_dequant(w):
            shape = w.shape
            flat = w.reshape(-1, BLOCKSIZE)
            absmax = jnp.max(jnp.abs(flat), axis=1, keepdims=True)
            normalized = flat / jnp.where(absmax == 0, 1.0, absmax)
            bounds = (NF4_CODE[:-1] + NF4_CODE[1:]) * 0.5
            idx = jnp.searchsorted(bounds, normalized)
            return (NF4_CODE[idx] * absmax).reshape(shape)
        dq1 = nf4_quant_dequant(w1)
        dq2 = nf4_quant_dequant(w2)
        dq3 = nf4_quant_dequant(w3)
        gate = jnp.einsum('bsd,hd->bsh', x, dq1)
        up = jnp.einsum('bsd,hd->bsh', x, dq2)
        h = jax.nn.silu(gate) * up
        return jnp.einsum('bsh,dh->bsd', h, dq3)
    x = x + _L0_xattn_ref(_layernorm(x, axis=-1), ctx_4096, ctx_4096, mask_BxSxS2_ff0, L0_xattn_wq, L0_xattn_wk, L0_xattn_wv, L0_xattn_wo, 0)
    x = x + _L0_ffn_ref(_layernorm(x, axis=-1), L0_ffn_router_weight, L0_ffn_router_bias, L0_ffn_expert_bias)
    x = x + _L1_xattn_ref(_layernorm(x, axis=-1), ctx_4096, L1_xattn_x1_scale, L1_xattn_x1_zp, L1_xattn_x2_scale, L1_xattn_x2_zp)
    x = x + _L1_ffn_ref(_layernorm(x, axis=-1), L1_ffn_w1, L1_ffn_w2, L1_ffn_w3)
    return x

_drawn_inputs = setup_inputs


def setup_inputs(seed=0):
    import zlib

    import numpy as np

    out = dict(_drawn_inputs(seed))
    spreads = {'L0_ffn_router_bias': (0.0, 0.8)}
    factors = {'L1_ffn_w1': 6.947, 'L1_ffn_w2': 6.729, 'L1_ffn_w3': 6.698}
    for name, (base, spread) in spreads.items():
        noise = np.random.default_rng([zlib.crc32(name.encode()), seed]).standard_normal(out[name].shape)
        drawn = base * np.exp(spread * noise) if base else spread * noise
        out[name] = jnp.asarray(drawn.astype(out[name].dtype))
    for name, factor in factors.items():
        out[name] = (out[name] * factor).astype(out[name].dtype)
    return out
```

```python
from contextlib import ExitStack

import numpy as np
import concourse.bass as bass
from concourse import mybir
from concourse.alu_op_type import AluOpType as ALU

F32 = mybir.dt.float32
F32R = mybir.dt.float32r
BF16 = mybir.dt.bfloat16
ACT = mybir.ActivationFunctionType
AX = mybir.AxisListType

P = 128
B, SQ, SK, D = 2, 512, 1024, 1024
T = B * SQ
TT = T // P
DC = D // P
HQ, HKV, DH = 32, 8, 128
GRP = HQ // HKV
KT = SK // P
QT = SQ // P
E, TOPK = 64, 8
HF = 2752
HC = -(-HF // P)
BLK = 64
EPS = 1e-5
ROUND = 1.5 * 2.0 ** 23
QMAX = 255.0
QMID = 128.0
NEG = -3.0e38

CODE = np.array([-1.0, -0.6961928009986877, -0.5250730514526367, -0.39491748809814453,
                 -0.28444138169288635, -0.18477343022823334, -0.09105003625154495, 0.0,
                 0.07958029955625534, 0.16093020141124725, 0.24611230194568634,
                 0.33791524171829224, 0.44070982933044434, 0.5626170039176941,
                 0.7229568362236023, 1.0], np.float32)
BOUNDS = (CODE[:-1] + CODE[1:]) * np.float32(0.5)


def exact_step(a, b):
    d = np.float32(b - a)
    for c in (d, np.nextafter(d, np.float32(9)), np.nextafter(d, np.float32(-9))):
        if np.float32(a + c) == b:
            return float(c)
    raise AssertionError


ZERO = int(np.argmin(np.abs(CODE)))
STEPS_UP = [(float(BOUNDS[j]), ALU.is_gt, exact_step(CODE[j], CODE[j + 1]))
            for j in range(ZERO, len(CODE) - 1)]
STEPS_DOWN = [(float(BOUNDS[j]), ALU.is_le, exact_step(CODE[j + 1], CODE[j]))
              for j in range(ZERO - 1, -1, -1)]


spent = []


class Event:

    def __init__(self, ctx, nc, name, spare=0):
        self.sem = ctx.enter_context(nc.semaphore(name))
        spent.append(self.sem)
        self.spare = spare

    def open(self, eng):
        eng.sem_inc(self.sem, self.spare)

    def done(self, n):
        return n + 1 + self.spare

    def free(self, n, ring):
        return n + 1 - ring + self.spare


def make_tools(ctx, nc, tag):
    def sb(name, shape, dt):
        return ctx.enter_context(nc.sbuf_tensor(f"{tag}_{name}", shape, dt))

    def ps(name, shape, dt=F32):
        return ctx.enter_context(nc.psum_tensor(f"{tag}_{name}", shape, dt))

    def sem(name):
        spent.append(ctx.enter_context(nc.semaphore(f"{tag}_{name}")))
        return spent[-1]

    def event(name, spare=0):
        return Event(ctx, nc, f"{tag}_{name}", spare)

    return sb, ps, sem, event


def f32(ap):
    return ap.bitcast(F32)


def split_matmul(pe, out, w, x, start, stop):
    pe.matmul(out, w[0], x[0], start=start, stop=False)
    pe.matmul(out, w[0], x[1], start=False, stop=False)
    return pe.matmul(out, w[1], x[0], start=False, stop=stop)


def clear_stage(nc):
    with nc.Block() as block:
        @block.sync
        def _(sp):
            for s in spent:
                sp.sem_clear(s)
    spent.clear()


def load_stage(nc, x, X, ident, ident_bf):
    with ExitStack() as ctx:
        sb, ps, sem, event = make_tools(ctx, nc, "ld")
        x_in, zeroed, made = sem("x_in"), sem("zeroed"), sem("made")
        block = ctx.enter_context(nc.Block())

        @block.sync
        def _(sp):
            sp.dma_start(X[:], x.rearrange("b (t p) d -> p (b t) d", p=P)).then_inc(x_in, 16)
            sp.wait_ge(x_in, 16)

        @block.gpsimd
        def _(pool):
            pool.memset(ident[:], 0.0).then_inc(zeroed, 1)
            pool.wait_ge(zeroed, 1)
            pool.affine_select(out=ident[:], in_=ident[:], compare_op=ALU.not_equal, fill=1.0,
                               base=0, pattern=[[-1, P]], channel_multiplier=1).then_inc(made, 1)
            pool.wait_ge(made, 1)
            pool.tensor_copy(ident_bf[:], ident[:]).then_inc(made, 1)


def norm_stage(nc, tag, X, ident, xT=None, xn_all=None, stats=None):
    with ExitStack() as ctx:
        sb, ps, sem, event = make_tools(ctx, nc, tag)
        st = sb("st", [P, TT, 2, 6], F32)
        mv = sb("mv", [P, TT, 2], F32)
        s = sb("s", [P, 5, TT], F32)
        xn = xn_all if xn_all is not None else sb("xn", [P, 2, D], F32)
        slots = TT if xn_all is not None else 2
        seq, var_ready, root_ready, normed = sem("seq"), sem("var"), sem("root"), sem("normed")
        turned, hi_out, lo_out = sem("turned"), sem("hi"), sem("lo")
        if xT is not None:
            tp = ps("tp", [P, 2, DC, P])
        block = ctx.enter_context(nc.Block())

        @block.scalar
        def _(act):
            act.wait_ge(var_ready, 1)
            act.activation(s[:, 1, :], s[:, 0, :], ACT.Sqrt).then_inc(root_ready, 1)
            if xT is not None:
                for t in range(TT):
                    act.wait_ge(turned, t + 1)
                    act.activation(xT[0][:, :, t * P:(t + 1) * P], tp[:, t % 2], ACT.Copy).then_inc(hi_out, 1)

        @block.vector
        def _(dve):
            steps = [0]

            def after(ins):
                steps[0] += 1
                ins.then_inc(seq, 1)
                dve.wait_ge(seq, steps[0])

            for t in range(TT):
                for h in range(2):
                    last = dve.bn_stats(st[:, t, h, :], X[:, t, h * 512:(h + 1) * 512])
            after(last)
            for t in range(TT):
                last = dve.bn_aggr(mv[:, t, :], st[:, t, :, :].rearrange("p a b -> p (a b)"))
            after(last)
            dve.tensor_scalar(s[:, 0, :], mv[:, :, 1], EPS, None, ALU.add).then_inc(var_ready, 1)
            dve.wait_ge(root_ready, 1)
            after(dve.reciprocal(s[:, 2, :], s[:, 1, :]))
            after(dve.tensor_tensor(s[:, 3, :], s[:, 0, :], s[:, 2, :], ALU.mult))
            after(dve.tensor_tensor(s[:, 3, :], s[:, 3, :], s[:, 1, :], ALU.add))
            after(dve.tensor_scalar(s[:, 2, :], s[:, 3, :], 0.5, None, ALU.mult))
            after(dve.reciprocal(s[:, 4, :], s[:, 2, :]))

            def norm(t):
                if xT is not None and t >= 2:
                    dve.wait_ge(turned, t - 1)
                dve.tensor_scalar(xn[:, t % slots, :], X[:, t, :], mv[:, t, 0:1], s[:, 4, t:t + 1],
                                  ALU.subtract, ALU.mult).then_inc(normed, 1)

            def low(t):
                dve.wait_ge(hi_out, t + 1)
                sl = slice(t * P, (t + 1) * P)
                dve.tensor_tensor(xT[1][:, :, sl], tp[:, t % 2], f32(xT[0][:, :, sl]), ALU.subtract).then_inc(lo_out, 1)

            norm(0)
            for t in range(TT):
                if t + 1 < TT:
                    norm(t + 1)
                if xT is not None:
                    low(t)

        if xT is not None:
            @block.tensor
            def _(pe):
                for t in range(TT):
                    pe.wait_ge(normed, t + 1)
                    if t >= 2:
                        pe.wait_ge(lo_out, t - 1)
                    for c in range(DC):
                        last = pe.transpose(tp[:, t % 2, c, :], xn[:, t % 2, c * P:(c + 1) * P], ident[:])
                    last.then_inc(turned, 1)


def project_stage(nc, tag, xT, w, heads, store, cos_d, sin_d, rows):
    with ExitStack() as ctx:
        sb, ps, sem, event = make_tools(ctx, nc, tag)
        width = max(stop for _, stop in rows)
        cos = sb("cos", [P, width], F32)
        sin = sb("sin", [P, width], F32)
        raw = sb("raw", [P, 2, DC, DH], F32)
        wh = sb("wh", [P, 2, DC, DH], F32R)
        wl = sb("wl", [P, 2, DC, DH], F32R)
        ta = sb("ta", [P, 2, 512], F32)
        tb = sb("tb", [P, 2, 512], F32)
        res = sb("res", [P, 2, 1024], F32)
        pj = ps("pj", [P, 2, 2, 512])
        tab_in = sem("tab_in")
        raw_in = [sem("raw_in0"), sem("raw_in1")]
        stored = [sem("stored0"), sem("stored1")]
        hi_out = event("hi")
        lo_out = event("lo", 2)
        tiles = event("tiles", 4)
        read = event("read", 4)
        summed = event("summed", 2)
        wv_ = w.rearrange("(c p) n -> p c n", p=P)
        block = ctx.enter_context(nc.Block())

        @block.sync
        def _(sp):
            for s in range(2):
                sp.sem_inc(stored[s], 16)
            sp.dma_start(cos[:], cos_d).then_inc(tab_in, 16)
            sp.dma_start(sin[:], sin_d).then_inc(tab_in, 16)
            with sp.Fori(0, heads // 2) as i:
                for s in range(2):
                    sp.wait_ge(lo_out.sem, lo_out.free(2 * i + s, 2))
                    sp.dma_start(raw[:, s], wv_[:, :, bass.ds(i * (2 * DH) + s * DH, DH)]).then_inc(raw_in[s], 16)
                for s in range(2):
                    sp.wait_ge(summed.sem, summed.done(4 * i + 2 * s + 1))
                    sp.dma_start(store(2 * i + s), res[:, s, :]).then_inc(stored[s], 16)
            for s in range(2):
                sp.wait_ge(stored[s], 16 * (heads // 2 + 1))

        @block.scalar
        def _(act):
            with act.Fori(0, heads // 2) as i:
                for s in range(2):
                    act.wait_ge(raw_in[s], i * 16 + 16)
                    act.wait_ge(tiles.sem, tiles.free(4 * i + 2 * s + 1, 4))
                    act.activation(wh[:, s], raw[:, s], ACT.Copy).then_inc(hi_out.sem, 1)

        @block.vector
        def _(dve):
            lo_out.open(dve)
            read.open(dve)
            dve.wait_ge(tab_in, 32)
            with dve.Fori(0, heads // 2) as i:
                for s in range(2):
                    dve.wait_ge(hi_out.sem, hi_out.done(2 * i + s))
                    dve.tensor_tensor(wl[:, s], raw[:, s], f32(wh[:, s]), ALU.subtract).then_inc(lo_out.sem, 1)
                for s in range(2):
                    for j in range(2):
                        n = 4 * i + 2 * s + j
                        a, b = rows[j]
                        src = pj[:, s, j, :]
                        dve.wait_ge(tiles.sem, tiles.done(n))
                        dve.wait_ge(summed.sem, summed.free(n, 2))
                        dve.tensor_tensor(ta[:, j], src, cos[:, a:b], ALU.mult)
                        dve.tensor_tensor(tb[0:64, j], src[64:128], sin[64:128, a:b], ALU.mult)
                        dve.tensor_tensor(tb[64:128, j], src[0:64], sin[0:64, a:b], ALU.mult).then_inc(read.sem, 1)

        @block.gpsimd
        def _(pool):
            summed.open(pool)
            with pool.Fori(0, heads // 2) as i:
                for s in range(2):
                    for j in range(2):
                        n = 4 * i + 2 * s + j
                        if j == 0:
                            pool.wait_ge(stored[s], i * 16 + 16)
                        pool.wait_ge(read.sem, read.done(n))
                        pool.tensor_tensor(res[:, s, j * 512:(j + 1) * 512], ta[:, j], tb[:, j],
                                           ALU.add).then_inc(summed.sem, 1)

        @block.tensor
        def _(pe):
            tiles.open(pe)
            with pe.Fori(0, heads // 2) as i:
                for s in range(2):
                    pe.wait_ge(lo_out.sem, lo_out.done(2 * i + s))
                    for j in range(2):
                        pe.wait_ge(read.sem, read.free(4 * i + 2 * s + j, 4))
                        for c in range(DC):
                            last = split_matmul(pe, pj[:, s, j, :], (wh[:, s, c, :], wl[:, s, c, :]),
                                                [x[:, c, j * 512:(j + 1) * 512] for x in xT],
                                                c == 0, c == DC - 1)
                        last.then_inc(tiles.sem, 1)


def context_stage(nc, tag, ctx_b, ident, cT):
    with ExitStack() as ctx:
        sb, ps, sem, event = make_tools(ctx, nc, tag)
        rows = sb("rows", [P, 3, D], F32)
        tp = ps("tp", [P, 2, DC, P])
        rows_in = [sem(f"rows_in{k}") for k in range(3)]
        turned, hi_out, lo_out = sem("turned"), sem("hi"), sem("lo")
        block = ctx.enter_context(nc.Block())

        @block.sync
        def _(sp):
            for t in range(KT):
                if t >= 3:
                    sp.wait_ge(turned, t - 2)
                sp.dma_start(rows[:, t % 3], ctx_b[t * P:(t + 1) * P, :]).then_inc(rows_in[t % 3], 16)

        @block.tensor
        def _(pe):
            for t in range(KT):
                pe.wait_ge(rows_in[t % 3], 16 * (t // 3 + 1))
                if t >= 2:
                    pe.wait_ge(lo_out, t - 1)
                for c in range(DC):
                    last = pe.transpose(tp[:, t % 2, c, :], rows[:, t % 3, c * P:(c + 1) * P], ident[:])
                last.then_inc(turned, 1)

        @block.scalar
        def _(act):
            for t in range(KT):
                act.wait_ge(turned, t + 1)
                act.activation(cT[0][:, :, t * P:(t + 1) * P], tp[:, t % 2], ACT.Copy).then_inc(hi_out, 1)

        @block.vector
        def _(dve):
            for t in range(KT):
                sl = slice(t * P, (t + 1) * P)
                dve.wait_ge(hi_out, t + 1)
                dve.tensor_tensor(cT[1][:, :, sl], tp[:, t % 2], f32(cT[0][:, :, sl]), ALU.subtract).then_inc(lo_out, 1)


def value_stage(nc, tag, cT, w, store):
    with ExitStack() as ctx:
        sb, ps, sem, event = make_tools(ctx, nc, tag)
        raw = sb("raw", [P, DC, 512], F32)
        wh = sb("wh", [P, DC, 512], F32R)
        wl = sb("wl", [P, DC, 512], F32R)
        res = sb("res", [P, 2, 512], F32)
        acc = ps("acc", [P, 2, 512])
        raw_in, hi_out, lo_out, tiles, copied = sem("raw_in"), sem("hi"), sem("lo"), sem("tiles"), sem("copied")
        stored = [sem("stored0"), sem("stored1")]
        block = ctx.enter_context(nc.Block())
        halves = D // 512

        @block.sync
        def _(sp):
            for h in range(halves):
                if h:
                    sp.wait_ge(lo_out, h)
                sp.dma_start(raw[:], w.rearrange("(c p) n -> p c n", p=P)[:, :, h * 512:(h + 1) * 512]).then_inc(raw_in, 16)
                for t in range(KT):
                    n = h * KT + t
                    sp.wait_ge(copied, n + 1)
                    sp.dma_start(store(t, h), res[:, n % 2]).then_inc(stored[n % 2], 16)
            for s in range(2):
                sp.wait_ge(stored[s], 16 * (halves * KT // 2))

        @block.scalar
        def _(act):
            for h in range(halves):
                act.wait_ge(raw_in, 16 * (h + 1))
                if h:
                    act.wait_ge(tiles, h * KT)
                act.activation(wh[:], raw[:], ACT.Copy).then_inc(hi_out, 1)
                for t in range(KT):
                    n = h * KT + t
                    act.wait_ge(tiles, n + 1)
                    if n >= 2:
                        act.wait_ge(stored[n % 2], 16 * (n // 2))
                    act.activation(res[:, n % 2], acc[:, n % 2], ACT.Copy).then_inc(copied, 1)

        @block.vector
        def _(dve):
            for h in range(halves):
                dve.wait_ge(hi_out, h + 1)
                dve.tensor_tensor(wl[:], raw[:], f32(wh[:]), ALU.subtract).then_inc(lo_out, 1)

        @block.tensor
        def _(pe):
            for h in range(halves):
                pe.wait_ge(lo_out, h + 1)
                for t in range(KT):
                    n = h * KT + t
                    if n >= 2:
                        pe.wait_ge(copied, n - 1)
                    for c in range(DC):
                        last = split_matmul(pe, acc[:, n % 2], [x[:, c, t * P:(t + 1) * P] for x in cT],
                                            (wh[:, c, :], wl[:, c, :]), c == 0, c == DC - 1)
                    last.then_inc(tiles, 1)


def attention_stage(nc, q_d, k_d, v_d, o_d, mask, ident):
    with ExitStack() as ctx:
        sb, ps, sem, event = make_tools(ctx, nc, "at")
        KG = 2
        HP = KG * GRP
        NS = HP * QT
        PASSES = HKV // KG
        HALF = KT // 2

        mk = sb("mk", [P, B * QT, SK], F32)
        kraw = sb("kraw", [P, SK], F32)
        vraw = sb("vraw", [P, KT, DH], F32)
        kk = [sb(f"k{x}", [P, KG, SK], F32R) for x in ("h", "l")]
        vv = [sb(f"v{x}", [P, KG, KT, DH], F32R) for x in ("h", "l")]
        qraw = sb("qraw", [P, 2, SQ], F32)
        qq = [sb(f"q{x}", [P, 2, SQ], F32R) for x in ("h", "l")]
        sc = sb("sc", [P, 2, SK], F32)
        pr = sb("pr", [P, 2, SK], F32)
        pt = [sb(f"pt{x}", [P, 2, KT, SQ], F32R) for x in ("h", "l")]
        ot = sb("ot", [P, 2, SQ], F32)
        sm = sb("sm", [P, 2, 4], F32)
        turnstile = sb("turnstile", [P, 1], F32)
        s_ps = ps("s", [P, 2, SK])
        t_ps = ps("t", [P, 2, HALF, P])
        o_ps = ps("o", [P, 2, SQ])

        mask_in, k_in, v_in = sem("mask_in"), sem("k_in"), sem("v_in")
        q_in = [sem("q_in0"), sem("q_in1")]
        o_st = [sem("o_st0"), sem("o_st1")]
        k_hi, v_hi, q_hi = event("k_hi"), event("v_hi"), event("q_hi")
        k_lo, v_lo = event("k_lo", 1), event("v_lo", 1)
        q_lo = event("q_lo", 2)
        scored = event("scored", NS)
        masked = event("masked", 2)
        maxed = event("maxed")
        expd = event("expd", 2)
        recipd = event("recipd")
        normed = event("normed")
        turned = event("turned", 4)
        t_hi = event("t_hi")
        t_lo = event("t_lo", 2)
        mixed = event("mixed", HP)
        copied = event("copied", 2)
        block = ctx.enter_context(nc.Block())

        def group(b, i, g):
            return i * KG + (b * HKV + g)

        def head(b, i, h):
            return i * HP + (b * HQ + h)

        def step(b, i, n):
            return i * NS + (b * HQ * QT + n)

        FETCH = [(0, "k", 0), (0, "q", 0), (0, "v", 0)]
        FETCH += [(QT * (h - 1) + 1, "q", h) for h in range(1, HP)]
        FETCH += [(QT * (GRP - 2), "k", 1), (QT * (GRP - 2) + 2, "v", 1)]
        FETCH.sort(key=lambda f: f[0])

        @block.sync
        def _(sp):
            sp.dma_start(mk[:], mask.rearrange("b (t p) k -> p (b t) k", p=P)).then_inc(mask_in, 16)
            for b in range(B):
                with sp.Fori(0, PASSES) as i:
                    for _, kind, x in FETCH:
                        if kind == "k":
                            sp.wait_ge(k_lo.sem, k_lo.free(group(b, i, x), 1))
                            sp.dma_start(kraw[:], k_d[b, bass.ds(i * KG + x, 1)].rearrange("a p n -> p (a n)")).then_inc(k_in, 16)
                        elif kind == "v":
                            sp.wait_ge(v_lo.sem, v_lo.free(group(b, i, x), 1))
                            sp.dma_start(vraw[:], v_d[b].rearrange("t p n -> p t n")[:, :, bass.ds(i * (KG * DH) + x * DH, DH)]).then_inc(v_in, 16)
                        else:
                            sp.wait_ge(q_lo.sem, q_lo.free(head(b, i, x), 2))
                            sp.dma_start(qraw[:, x % 2], q_d[bass.ds(i * HP + x, 1)].rearrange("a p n -> p (a n)")[:, b * SQ:(b + 1) * SQ]).then_inc(q_in[x % 2], 16)

        @block.gpsimd
        def _(pool):
            k_lo.open(pool)
            v_lo.open(pool)
            q_lo.open(pool)
            for b in range(B):
                with pool.Fori(0, PASSES) as i:
                    for _, kind, x in FETCH:
                        if kind == "k":
                            pool.wait_ge(k_hi.sem, k_hi.done(group(b, i, x)))
                            pool.tensor_tensor(kk[1][:, x], kraw[:], f32(kk[0][:, x]), ALU.subtract).then_inc(k_lo.sem, 1)
                        elif kind == "v":
                            pool.wait_ge(v_hi.sem, v_hi.done(group(b, i, x)))
                            pool.tensor_tensor(vv[1][:, x], vraw[:], f32(vv[0][:, x]), ALU.subtract).then_inc(v_lo.sem, 1)
                        else:
                            pool.wait_ge(q_hi.sem, q_hi.done(head(b, i, x)))
                            pool.tensor_tensor(qq[1][:, x % 2], qraw[:, x % 2], f32(qq[0][:, x % 2]), ALU.subtract).then_inc(q_lo.sem, 1)

        @block.scalar
        def _(act):
            def fetch(b, i, kind, x):
                if kind == "k":
                    act.wait_ge(k_in, group(b, i, x) * 16 + 16)
                    act.wait_ge(scored.sem, scored.free(step(b, i, (x + 1) * GRP * QT - 1), NS))
                    act.activation(kk[0][:, x], kraw[:], ACT.Copy).then_inc(k_hi.sem, 1)
                elif kind == "v":
                    act.wait_ge(v_in, group(b, i, x) * 16 + 16)
                    act.wait_ge(mixed.sem, mixed.free(head(b, i, (x + 1) * GRP - 1), HP))
                    act.activation(vv[0][:, x], vraw[:], ACT.Copy).then_inc(v_hi.sem, 1)
                else:
                    act.wait_ge(q_in[x % 2], i * (16 * HP // 2) + 16 * (b * HQ // 2 + x // 2 + 1))
                    act.wait_ge(scored.sem, scored.free(step(b, i, QT * (x + 1) - 1), 2 * QT))
                    act.activation(qq[0][:, x % 2], qraw[:, x % 2], ACT.Copy).then_inc(q_hi.sem, 1)

            def exponentials(b, i, n):
                act.wait_ge(maxed.sem, maxed.done(step(b, i, n)))
                act.wait_ge(turned.sem, turned.free(2 * step(b, i, n) + 1, 4))
                act.activation(pr[:, n % 2], sc[:, n % 2], ACT.Exp, bias=sm[:, n % 2, 1:2],
                               accum_out=sm[:, n % 2, 2:3]).then_inc(expd.sem, 1)

            def turn_high(b, i, n):
                h = n // QT
                if n % QT == 0:
                    act.wait_ge(mixed.sem, mixed.free(head(b, i, h), 2))
                for j in range(2):
                    act.wait_ge(turned.sem, turned.done(2 * step(b, i, n) + j))
                    act.activation(pt[0][:, h % 2, j * HALF:(j + 1) * HALF, (n % QT) * P:(n % QT + 1) * P],
                                   t_ps[:, j], ACT.Copy).then_inc(t_hi.sem, 1)

            def copy_out(b, i, h):
                act.wait_ge(mixed.sem, mixed.done(head(b, i, h)))
                act.wait_ge(o_st[h % 2], i * (16 * HP // 2) + 16 * (b * HQ // 2 + h // 2 + 1))
                act.activation(ot[:, h % 2], o_ps[:, h % 2], ACT.Copy).then_inc(copied.sem, 1)

            def store_out(b, i, h):
                act.wait_ge(copied.sem, copied.done(head(b, i, h)))
                act.dma_start(o_d[bass.ds(i * HP + h, 1)].rearrange("a p n -> p (a n)")[:, b * SQ:(b + 1) * SQ],
                              ot[:, h % 2]).then_inc(o_st[h % 2], 16)

            expd.open(act)
            copied.open(act)
            for s in range(2):
                act.sem_inc(o_st[s], 16)
            for b in range(B):
                with act.Fori(0, PASSES) as i:
                    for n in range(NS + 5):
                        for at, kind, x in FETCH:
                            if at == n:
                                fetch(b, i, kind, x)
                        if n < NS:
                            exponentials(b, i, n)
                        if 2 <= n < NS + 2:
                            turn_high(b, i, n - 2)
                        if n >= QT + 3 and (n - 3) % QT == 0:
                            copy_out(b, i, (n - 3) // QT - 1)
                        if n >= QT + 4 and (n - 4) % QT == 0:
                            store_out(b, i, (n - 4) // QT - 1)
            for s in range(2):
                act.wait_ge(o_st[s], 16 * (B * HQ // 2 + 1))

        @block.vector
        def _(dve):
            def mask_and_max(b, i, n):
                dve.wait_ge(scored.sem, scored.done(step(b, i, n)))
                dve.wait_ge(expd.sem, expd.free(step(b, i, n), 2))
                dve.memset(turnstile[:], 0.0)
                dve.tensor_tensor_reduce(sc[:, n % 2], s_ps[:, n % 2], mk[:, b * QT + n % QT], 1.0, NEG,
                                         ALU.add, ALU.max, sm[:, n % 2, 0:1]).then_inc(masked.sem, 1)
                dve.wait_ge(masked.sem, masked.done(step(b, i, n)))
                dve.tensor_scalar(sm[:, n % 2, 1:2], sm[:, n % 2, 0:1], -1.0, None, ALU.mult).then_inc(maxed.sem, 1)

            def normalise(b, i, n):
                dve.wait_ge(expd.sem, expd.done(step(b, i, n)))
                dve.reciprocal(sm[:, n % 2, 3:4], sm[:, n % 2, 2:3]).then_inc(recipd.sem, 1)
                dve.wait_ge(recipd.sem, recipd.done(step(b, i, n)))
                dve.tensor_scalar(pr[:, n % 2], pr[:, n % 2], sm[:, n % 2, 3:4], None, ALU.mult).then_inc(normed.sem, 1)

            def turn_low(b, i, n):
                h = n // QT
                for j in range(2):
                    sl = (slice(None), h % 2, slice(j * HALF, (j + 1) * HALF), slice((n % QT) * P, (n % QT + 1) * P))
                    dve.wait_ge(t_hi.sem, t_hi.done(2 * step(b, i, n) + j))
                    dve.tensor_tensor(pt[1][sl], t_ps[:, j], f32(pt[0][sl]), ALU.subtract).then_inc(t_lo.sem, 1)

            masked.open(dve)
            t_lo.open(dve)
            dve.wait_ge(mask_in, 16)
            for b in range(B):
                with dve.Fori(0, PASSES) as i:
                    for n in range(NS + 2):
                        if n < NS:
                            mask_and_max(b, i, n)
                        if 1 <= n < NS + 1:
                            normalise(b, i, n - 1)
                        if n >= 2:
                            turn_low(b, i, n - 2)

        @block.tensor
        def _(pe):
            def scores(b, i, n):
                h = n // QT
                g = h // GRP
                if n % (QT * GRP) == 0:
                    pe.wait_ge(k_lo.sem, k_lo.done(group(b, i, g)))
                if n % QT == 0:
                    pe.wait_ge(q_lo.sem, q_lo.done(head(b, i, h)))
                pe.wait_ge(masked.sem, masked.free(step(b, i, n), 2))
                for j in range(SK // 512):
                    last = split_matmul(pe, s_ps[:, n % 2, j * 512:(j + 1) * 512],
                                        [x[:, h % 2, (n % QT) * P:(n % QT + 1) * P] for x in qq],
                                        [x[:, g, j * 512:(j + 1) * 512] for x in kk], True, True)
                last.then_inc(scored.sem, 1)

            def turn(b, i, n):
                pe.wait_ge(normed.sem, normed.done(step(b, i, n)))
                for j in range(2):
                    pe.wait_ge(t_lo.sem, t_lo.free(2 * step(b, i, n) + j, 2))
                    for c in range(HALF):
                        k = j * HALF + c
                        last = pe.transpose(t_ps[:, j, c, :], pr[:, n % 2, k * P:(k + 1) * P], ident[:])
                    last.then_inc(turned.sem, 1)

            def mix(b, i, h):
                g = h // GRP
                if h % GRP == 0:
                    pe.wait_ge(v_lo.sem, v_lo.done(group(b, i, g)))
                pe.wait_ge(t_lo.sem, t_lo.done(2 * step(b, i, QT * (h + 1) - 1) + 1))
                pe.wait_ge(copied.sem, copied.free(head(b, i, h), 2))
                for c in range(KT):
                    last = split_matmul(pe, o_ps[:, h % 2], [x[:, g, c, :] for x in vv],
                                        [x[:, h % 2, c, :] for x in pt], c == 0, c == KT - 1)
                last.then_inc(mixed.sem, 1)

            scored.open(pe)
            turned.open(pe)
            mixed.open(pe)
            for b in range(B):
                with pe.Fori(0, PASSES) as i:
                    for n in range(NS + 3):
                        if n < NS:
                            scores(b, i, n)
                        if 2 <= n < NS + 2:
                            turn(b, i, n - 2)
                        if n >= QT + 2 and (n - 2) % QT == 0:
                            mix(b, i, (n - 2) // QT - 1)


def output_stage(nc, o_d, wo, X):
    with ExitStack() as ctx:
        sb, ps, sem, event = make_tools(ctx, nc, "ou")
        oraw = sb("oraw", [P, GRP, T], F32)
        wraw = sb("wraw", [P, GRP, D], F32)
        oo = [sb(f"o{x}", [P, 2, GRP, T], F32R) for x in ("h", "l")]
        ww = [sb(f"w{x}", [P, 2, GRP, D], F32R) for x in ("h", "l")]
        acc = ps("acc", [P, 4, 512])
        NT = TT * (D // 512)
        o_in = [sem(f"o_in{r}") for r in range(GRP)]
        w_in = [sem(f"w_in{r}") for r in range(GRP)]
        o_hi, w_hi = event("o_hi"), event("w_hi")
        o_lo, w_lo = event("o_lo", GRP), event("w_lo", GRP)
        tiles = event("tiles", 2 * NT)
        added = event("added", 4)
        block = ctx.enter_context(nc.Block())
        GROUPS = HQ // GRP

        @block.sync
        def _(sp):
            with sp.Fori(0, GROUPS // 2) as i:
                for s in range(2):
                    for r in range(GRP):
                        h = i * (2 * GRP) + (s * GRP + r)
                        sp.wait_ge(o_lo.sem, o_lo.free(h, GRP))
                        sp.dma_start(oraw[:, r], o_d[bass.ds(h, 1)].rearrange("a p n -> p (a n)")).then_inc(o_in[r], 16)
                        sp.wait_ge(w_lo.sem, w_lo.free(h, GRP))
                        sp.dma_start(wraw[:, r], wo[bass.ds(i * (2 * GRP * DH) + (s * GRP + r) * DH, DH), :]).then_inc(w_in[r], 16)

        @block.scalar
        def _(act):
            with act.Fori(0, GROUPS // 2) as i:
                for s in range(2):
                    act.wait_ge(tiles.sem, tiles.free(i * (2 * NT) + (s + 1) * NT - 1, 2 * NT))
                    for r in range(GRP):
                        act.wait_ge(o_in[r], i * 32 + 16 * (s + 1))
                        act.activation(oo[0][:, s, r], oraw[:, r], ACT.Copy).then_inc(o_hi.sem, 1)
                        act.wait_ge(w_in[r], i * 32 + 16 * (s + 1))
                        act.activation(ww[0][:, s, r], wraw[:, r], ACT.Copy).then_inc(w_hi.sem, 1)

        @block.vector
        def _(dve):
            def split(i, s, r):
                h = i * (2 * GRP) + (s * GRP + r)
                dve.wait_ge(o_hi.sem, o_hi.done(h))
                dve.tensor_tensor(oo[1][:, s, r], oraw[:, r], f32(oo[0][:, s, r]), ALU.subtract).then_inc(o_lo.sem, 1)
                dve.wait_ge(w_hi.sem, w_hi.done(h))
                dve.tensor_tensor(ww[1][:, s, r], wraw[:, r], f32(ww[0][:, s, r]), ALU.subtract).then_inc(w_lo.sem, 1)

            o_lo.open(dve)
            w_lo.open(dve)
            added.open(dve)
            with dve.Fori(0, GROUPS // 2) as i:
                for r in range(GRP):
                    split(i, 0, r)
                for s in range(2):
                    for k in range(NT):
                        if s == 0 and k % 4 == 0:
                            split(i, 1, k // 4)
                        m = i * (2 * NT) + (s * NT + k)
                        t, n = k // 2, k % 2
                        dve.wait_ge(tiles.sem, tiles.done(m))
                        dve.tensor_tensor(X[:, t, n * 512:(n + 1) * 512], acc[:, k % 4],
                                          X[:, t, n * 512:(n + 1) * 512], ALU.add).then_inc(added.sem, 1)

        @block.tensor
        def _(pe):
            tiles.open(pe)
            with pe.Fori(0, GROUPS // 2) as i:
                for s in range(2):
                    h = i * (2 * GRP) + (s * GRP + GRP - 1)
                    pe.wait_ge(o_lo.sem, o_lo.done(h))
                    pe.wait_ge(w_lo.sem, w_lo.done(h))
                    for k in range(NT):
                        t, n = k // 2, k % 2
                        pe.wait_ge(added.sem, added.free(i * (2 * NT) + (s * NT + k), 4))
                        for r in range(GRP):
                            last = split_matmul(pe, acc[:, k % 4], [x[:, s, r, t * P:(t + 1) * P] for x in oo],
                                                [x[:, s, r, n * 512:(n + 1) * 512] for x in ww],
                                                r == 0, r == GRP - 1)
                        last.then_inc(tiles.sem, 1)


def router_stage(nc, X, xn, ident, router_w, router_b, expert_b):
    with ExitStack() as ctx:
        sb, ps, sem, event = make_tools(ctx, nc, "ro")
        rw = sb("rw", [E, D], F32)
        rwT = sb("rwT", [P, DC, E], F32)
        rb = sb("rb", [P, E], F32)
        eb = sb("eb", [E, D], F32)
        xT = sb("xT", [P, 2, DC, P], F32)
        lg = sb("lg", [P, 2, E], F32)
        ex = sb("ex", [P, 2, E], F32)
        rest = sb("rest", [P, 2, E], F32)
        top = sb("top", [P, 2, TOPK], F32)
        sm = sb("sm", [P, 2, 6], F32)
        wT = sb("wT", [E, 2, P], F32)
        tmp = sb("tmp", [P, D], F32)
        t_ps = ps("t", [P, DC, P])
        l_ps = ps("l", [P, 512])
        w_ps = ps("w", [P, 512])
        m_ps = ps("m", [P, 2, D])
        w_in, rw_turned, rw_copied = sem("w_in"), sem("rw_turned"), sem("rw_copied")
        turned, copied, logits, seq, picked = sem("turned"), sem("copied"), sem("logits"), sem("seq"), sem("picked")
        maxed, expd = sem("maxed"), sem("expd")
        w_turned, w_copied, mixed, added = sem("w_turned"), sem("w_copied"), sem("mixed"), sem("added")
        block = ctx.enter_context(nc.Block())

        @block.sync
        def _(sp):
            sp.dma_start(rw[:], router_w).then_inc(w_in, 16)
            sp.dma_start(eb[:], expert_b).then_inc(w_in, 16)
            sp.dma_start(rb[:], router_b.rearrange("(a e) -> a e", a=1).broadcast_to((P, E))).then_inc(w_in, 16)

        @block.tensor
        def _(pe):
            pe.wait_ge(w_in, 48)
            for c in range(DC):
                last = pe.transpose(t_ps[:, c, 0:E], rw[:, c * P:(c + 1) * P], ident[0:E, 0:E])
            last.then_inc(rw_turned, 1)

            def turn(t):
                if t == 0:
                    pe.wait_ge(rw_copied, 1)
                else:
                    pe.wait_ge(copied, t)
                for c in range(DC):
                    last = pe.transpose(t_ps[:, c, :], xn[:, t, c * P:(c + 1) * P], ident[:])
                last.then_inc(turned, 1)

            turn(0)
            for t in range(TT):
                pe.wait_ge(copied, t + 1)
                if t:
                    pe.wait_ge(picked, t)
                for c in range(DC):
                    last = pe.matmul(l_ps[:, 0:E], xT[:, t % 2, c, :], rwT[:, c, :], start=c == 0, stop=c == DC - 1)
                last.then_inc(logits, 1)
                if t + 1 < TT:
                    turn(t + 1)
                pe.wait_ge(picked, t + 1)
                if t:
                    pe.wait_ge(w_copied, t)
                pe.transpose(w_ps[0:E, 0:P], rest[:, t % 2, :], ident[:]).then_inc(w_turned, 1)
                pe.wait_ge(w_copied, t + 1)
                if t >= 2:
                    pe.wait_ge(added, t - 1)
                for n in range(2):
                    last = pe.matmul(m_ps[:, t % 2, n * 512:(n + 1) * 512], wT[:, t % 2, :],
                                     eb[:, n * 512:(n + 1) * 512], start=True, stop=True)
                last.then_inc(mixed, 1)

        @block.scalar
        def _(act):
            act.wait_ge(rw_turned, 1)
            act.activation(rwT[:], t_ps[:, :, 0:E], ACT.Copy).then_inc(rw_copied, 1)
            for t in range(TT):
                act.wait_ge(turned, t + 1)
                if t >= 2:
                    act.wait_ge(logits, t - 1)
                act.activation(xT[:, t % 2], t_ps[:], ACT.Copy).then_inc(copied, 1)
                act.wait_ge(maxed, t + 1)
                act.activation(ex[:, t % 2], lg[:, t % 2], ACT.Exp, bias=sm[:, t % 2, 1:2],
                               accum_out=sm[:, t % 2, 2:3]).then_inc(expd, 1)
                act.wait_ge(w_turned, t + 1)
                if t >= 2:
                    act.wait_ge(mixed, t - 1)
                act.activation(wT[:, t % 2, :], w_ps[0:E, 0:P], ACT.Copy).then_inc(w_copied, 1)

        @block.vector
        def _(dve):
            steps = [0]

            def after(ins):
                steps[0] += 1
                ins.then_inc(seq, 1)
                dve.wait_ge(seq, steps[0])

            dve.wait_ge(w_in, 48)
            for t in range(TT):
                s = t % 2
                col = [sm[:, s, k:k + 1] for k in range(6)]
                dve.wait_ge(logits, t + 1)
                after(dve.tensor_tensor_reduce(lg[:, s], l_ps[:, 0:E], rb[:], 1.0, NEG, ALU.add, ALU.max, col[0]))
                dve.tensor_scalar(col[1], col[0], -1.0, None, ALU.mult).then_inc(maxed, 1)
                dve.wait_ge(expd, t + 1)
                after(dve.reciprocal(col[3], col[2]))
                after(dve.tensor_scalar(ex[:, s], ex[:, s], col[3], None, ALU.mult))
                after(dve.max(top[:, s], ex[:, s]))
                if t >= 2:
                    dve.wait_ge(w_turned, t - 1)
                after(dve.match_replace(rest[:, s], top[:, s], ex[:, s], 0.0))
                after(dve.reduce_sum(col[4], top[:, s], AX.X))
                dve.tensor_tensor(rest[:, s], ex[:, s], rest[:, s], ALU.subtract).then_inc(picked, 1)
                after(dve.scalar_tensor_tensor(tmp[:], xn[:, t], col[4], X[:, t], ALU.mult, ALU.add))
                dve.wait_ge(mixed, t + 1)
                dve.tensor_tensor(X[:, t], m_ps[:, s], tmp[:], ALU.add).then_inc(added, 1)


def quantised_stage(nc, X, xn, ident_bf, context, scales):
    with ExitStack() as ctx:
        sb, ps, sem, event = make_tools(ctx, nc, "qn")
        par = sb("par", [P, 4], F32)
        k = sb("k", [P, 6], F32)
        rows = sb("rows", [P, 3, D], F32)
        work = sb("work", [P, 2, D], F32)
        qa = sb("qa", [P, 2, D], BF16)
        qaT = sb("qaT", [P, TT, DC, P], BF16)
        rowsum = sb("rowsum", [P, 2, TT], F32)
        qb = sb("qb", [P, B, KT, D], BF16)
        ones = sb("ones", [P, P], BF16)
        colsum = sb("colsum", [P, B, D], F32)
        tmp = sb("tmp", [P, 512], F32)
        t_ps = ps("t", [P, 2, DC, P], BF16)
        c_ps = ps("c", [P, D])
        acc = ps("acc", [P, 4, 512])
        par_in, k_ready, ones_made = sem("par_in"), sem("k_ready"), sem("ones_made")
        rows_in = [sem(f"rows_in{r}") for r in range(3)]
        seq, qa_done, qb_done, scaled = sem("seq"), sem("qa_done"), sem("qb_done"), sem("scaled")
        turned, copied, col_done, col_read, tiles, added = (
            sem("turned"), sem("copied"), sem("col_done"), sem("col_read"), sem("tiles"), sem("added"))
        block = ctx.enter_context(nc.Block())

        @block.sync
        def _(sp):
            for j, v in enumerate(scales):
                sp.dma_start(par[:, j:j + 1], v.rearrange("(a b) -> a b", a=1).broadcast_to((P, 1))).then_inc(par_in, 16)
            for n in range(B * KT):
                if n >= 3:
                    sp.wait_ge(scaled, TT + n - 2)
                sp.dma_start(rows[:, n % 3], context[n // KT, (n % KT) * P:(n % KT + 1) * P, :]).then_inc(rows_in[n % 3], 16)

        @block.scalar
        def _(act):
            act.wait_ge(k_ready, 1)
            for n in range(TT + B * KT):
                a = n < TT
                if n >= 2:
                    act.wait_ge(qa_done if n - 2 < TT else qb_done, n - 1 if n - 2 < TT else n - 1 - TT)
                if not a:
                    m = n - TT
                    act.wait_ge(rows_in[m % 3], 16 * (m // 3 + 1))
                src = xn[:, n] if a else rows[:, (n - TT) % 3]
                act.activation(work[:, n % 2], src, ACT.Identity, bias=par[:, 1:2] if a else par[:, 3:4],
                               scale=k[:, 0:1] if a else k[:, 1:2]).then_inc(scaled, 1)
                if a:
                    act.wait_ge(turned, n + 1)
                    act.activation(qaT[:, n], t_ps[:, n % 2], ACT.Copy).then_inc(copied, 1)

        @block.gpsimd
        def _(pool):
            pool.memset(ones[:], 1.0).then_inc(ones_made, 1)

        @block.vector
        def _(dve):
            steps = [0]

            def after(ins):
                steps[0] += 1
                ins.then_inc(seq, 1)
                dve.wait_ge(seq, steps[0])

            dve.wait_ge(par_in, 64)
            dve.reciprocal(k[:, 0:1], par[:, 0:1])
            dve.reciprocal(k[:, 1:2], par[:, 2:3])
            dve.tensor_scalar(k[:, 2:3], par[:, 1:2], -1.0, QMID, ALU.mult, ALU.add)
            dve.tensor_tensor(k[:, 4:5], par[:, 0:1], par[:, 2:3], ALU.mult)
            after(dve.tensor_scalar(k[:, 3:4], par[:, 3:4], -1.0, QMID, ALU.mult, ALU.add))
            dve.tensor_scalar(k[:, 5:6], k[:, 3:4], float(D), None, ALU.mult).then_inc(k_ready, 1)

            def quantise(n, out, done):
                dve.wait_ge(scaled, n + 1)
                after(dve.tensor_scalar(work[:, n % 2], work[:, n % 2], QMAX, 0.0, ALU.min, ALU.max))
                dve.tensor_scalar(out, work[:, n % 2], ROUND, ROUND + QMID, ALU.add, ALU.subtract).then_inc(done, 1)

            for t in range(TT):
                if t >= 2:
                    dve.wait_ge(turned, t - 1)
                quantise(t, qa[:, t % 2], qa_done)
                dve.wait_ge(qa_done, t + 1)
                last = dve.reduce_sum(rowsum[:, 0, t:t + 1], qa[:, t % 2], AX.X)
            after(last)
            after(dve.tensor_scalar(rowsum[:, 1], rowsum[:, 0], k[:, 3:4], None, ALU.mult))

            def finish(b):
                dve.wait_ge(col_done, b + 1)
                dve.tensor_scalar(colsum[:, b], c_ps[:], k[:, 5:6], k[:, 2:3], ALU.add, ALU.mult).then_inc(col_read, 1)
                dve.wait_ge(col_read, b + 1)
                for j in range(2 * QT):
                    n = b * 2 * QT + j
                    t, h = n // 2, n % 2
                    sl = slice(h * 512, (h + 1) * 512)
                    dve.wait_ge(tiles, n + 1)
                    after(dve.scalar_tensor_tensor(tmp[:], acc[:, n % 4], rowsum[:, 1, t:t + 1], colsum[:, b, sl], ALU.add, ALU.add))
                    after(dve.scalar_tensor_tensor(X[:, t, sl], tmp[:], k[:, 4:5], X[:, t, sl], ALU.mult, ALU.add))
                    dve.sem_inc(added, 1)

            for n in range(B * KT):
                quantise(TT + n, qb[:, n // KT, n % KT], qb_done)
            for b in range(B):
                finish(b)

        @block.tensor
        def _(pe):
            for t in range(TT):
                pe.wait_ge(qa_done, t + 1)
                if t >= 2:
                    pe.wait_ge(copied, t - 1)
                for c in range(DC):
                    last = pe.transpose(t_ps[:, t % 2, c, :], qa[:, t % 2, c * P:(c + 1) * P], ident_bf[:])
                last.then_inc(turned, 1)
            pe.wait_ge(copied, TT)
            pe.wait_ge(ones_made, 1)
            for b in range(B):
                pe.wait_ge(qb_done, (b + 1) * KT)
                if b:
                    pe.wait_ge(col_read, b)
                for h in range(2):
                    for c in range(KT):
                        last = pe.matmul(c_ps[:, h * 512:(h + 1) * 512], ones[:], qb[:, b, c, h * 512:(h + 1) * 512],
                                         start=c == 0, stop=c == KT - 1)
                last.then_inc(col_done, 1)
                for j in range(2 * QT):
                    n = b * 2 * QT + j
                    t, h = n // 2, n % 2
                    if n >= 4:
                        pe.wait_ge(added, n - 3)
                    for c in range(DC):
                        last = pe.matmul(acc[:, n % 4], qaT[:, t, c, :], qb[:, b, c, h * 512:(h + 1) * 512],
                                         start=c == 0, stop=c == DC - 1)
                    last.then_inc(tiles, 1)


def nf4_stage(nc, w1, w2, w3, wq_d):
    with ExitStack() as ctx:
        sb, ps, sem, event = make_tools(ctx, nc, "nf")
        NB = 3 * D // BLK
        raw = sb("raw", [P, 2, 3, D], F32)
        nrm = sb("nrm", [P, 3, D], F32)
        hit = sb("hit", [P, 2, 3 * D], F32)
        val = sb("val", [P, 2, 3 * D], F32)
        am = sb("am", [P, 4, NB], F32)
        loaded = [sem("loaded0"), sem("loaded1")]
        stored = [sem("stored0"), sem("stored1")]
        zeroed, seq = sem("zeroed"), event("seq")
        scaled = event("scaled", 2)
        decoded = event("decoded", 1)
        block = ctx.enter_context(nc.Block())
        PAIRS = HC // 2
        REST = HF - (HC - 1) * P
        w3v = w3.rearrange("(c p) h -> p c h", p=P)
        STEPS = 4 + 2 * (len(STEPS_UP) + len(STEPS_DOWN)) - 1

        def blocks(ap):
            return ap.rearrange("p (n b) -> p n b", b=BLK)

        @block.sync
        def _(sp):
            for s in range(2):
                sp.sem_inc(stored[s], 16)

            def load(i, s, rows):
                m = 2 * i + s
                sp.wait_ge(scaled.sem, scaled.free(m, 2))
                sp.dma_start(raw[0:rows, s, 0], w1[bass.ds(m * P, rows), :]).then_inc(loaded[s], 16)
                sp.dma_start(raw[0:rows, s, 1], w2[bass.ds(m * P, rows), :]).then_inc(loaded[s], 16)
                sp.dma_start(raw[:, s, 2].rearrange("p (c h) -> p c h", h=P)[:, :, 0:rows],
                             w3v[:, :, bass.ds(m * P, rows)]).then_inc(loaded[s], 16)

            def store(i, s):
                sp.wait_ge(decoded.sem, decoded.done(2 * i + s))
                sp.dma_start(wq_d[bass.ds(2 * i + s, 1)].rearrange("a p n -> p (a n)"), val[:, s]).then_inc(stored[s], 16)

            with sp.Fori(0, PAIRS - 1) as i:
                for s in range(2):
                    load(i, s, P)
                for s in range(2):
                    store(i, s)
            sp.wait_ge(zeroed, 1)
            load(PAIRS - 1, 0, P)
            load(PAIRS - 1, 1, REST)
            for s in range(2):
                store(PAIRS - 1, s)
                sp.wait_ge(stored[s], 16 * (PAIRS + 1))

        @block.gpsimd
        def _(pool):
            pool.wait_ge(scaled.sem, scaled.free(HC - 1, 2))
            pool.memset(raw[:, 1], 0.0).then_inc(zeroed, 1)

        @block.vector
        def _(dve):
            scaled.open(dve)
            decoded.open(dve)

            def chunk(i, s):
                m = 2 * i + s
                count = [0]

                def after(ins):
                    ins.then_inc(seq.sem, 1)
                    dve.wait_ge(seq.sem, seq.done(m * STEPS + count[0]))
                    count[0] += 1

                src = raw[:, s].rearrange("p a b -> p (a b)")
                n = nrm[:].rearrange("p a b -> p (a b)")
                v = val[:, s]
                dve.wait_ge(decoded.sem, decoded.free(m, 1))
                dve.wait_ge(loaded[s], i * 48 + 48)
                after(dve.tensor_reduce(am[:, 0], blocks(src), AX.X, ALU.max, apply_absolute_value=True))
                after(dve.scalar_tensor_tensor(am[:, 1], am[:, 0], 0.0, am[:, 0], ALU.is_equal, ALU.add))
                after(dve.reciprocal(am[:, 2], am[:, 1]))
                after(dve.tensor_tensor(blocks(n), blocks(src), am[:, 2].unsqueeze(2).broadcast_to((P, NB, BLK)), ALU.mult))
                dve.sem_inc(scaled.sem, 1)
                dve.wait_ge(stored[s], i * 16 + 16)
                for j, (bound, compare, step) in enumerate(STEPS_UP + STEPS_DOWN):
                    out = v if j == 0 else hit[:, j % 2]
                    after(dve.tensor_scalar(out, n, bound, step, compare, ALU.mult))
                    if j:
                        after(dve.tensor_tensor(v, v, out, ALU.add))
                dve.tensor_tensor(blocks(v), blocks(v), am[:, 0].unsqueeze(2).broadcast_to((P, NB, BLK)), ALU.mult).then_inc(decoded.sem, 1)
                assert count[0] == STEPS, count[0]

            with dve.Fori(0, PAIRS) as i:
                for s in range(2):
                    chunk(i, s)


def ffn_stage(nc, xT, X, ident, wq_d):
    with ExitStack() as ctx:
        sb, ps, sem, event = make_tools(ctx, nc, "ff")
        raw = sb("raw", [P, 3, D], F32)
        gu = [sb(f"gu{x}", [P, 2, 2, D], F32R) for x in ("h", "l")]
        dn = [sb(f"dn{x}", [P, 4, D], F32R) for x in ("h", "l")]
        act_s = sb("act_s", [P, 2, 512], F32)
        hid = sb("hid", [P, 2, 512], F32)
        hT = [sb(f"h{x}", [P, 2, T], F32R) for x in ("h", "l")]
        t_ps = ps("t", [P, 2, 512])
        g_ps = ps("g", [P, 2, 2, 512])
        y_ps = ps("y", [P, 2, 512])
        PAIRS = HC // 2
        NT = TT * 2
        raw_in = [sem(f"raw_in{j}") for j in range(3)]
        turned = event("turned", 6)
        w_hi = event("w_hi")
        w_lo = event("w_lo", 2)
        gated = event("gated", 4)
        silu = event("silu", 2)
        gone = event("gone", 2)
        h_hi = event("h_hi")
        h_lo = event("h_lo", 2)
        tiles = event("tiles", 2 * NT)
        added = event("added", 2)
        block = ctx.enter_context(nc.Block())

        def weights_slot(q, s):
            return 2 * q + s

        def program(eng, body):
            with eng.Fori(0, PAIRS // 2) as i:
                for q in range(2):
                    body(2 * i + q, q)
            if PAIRS % 2:
                body(PAIRS - 1, 0)

        @block.sync
        def _(sp):
            def body(pr, q):
                for s in range(2):
                    m = pr * 2 + s
                    for j in range(3):
                        sp.wait_ge(turned.sem, turned.free(m * 6 + 2 * j + 1, 6))
                        sp.dma_start(raw[:, j], wq_d[bass.ds(m, 1)].rearrange("a p n -> p (a n)")[:, j * D:(j + 1) * D]).then_inc(raw_in[j], 16)

            program(sp, body)

        @block.tensor
        def _(pe):
            turned.open(pe)
            gated.open(pe)
            tiles.open(pe)

            def turn(pr, q, s):
                m = pr * 2 + s
                for j in range(3):
                    pe.wait_ge(raw_in[j], m * 16 + 16)
                    for k in range(2):
                        u = m * 6 + (2 * j + k)
                        pe.wait_ge(w_lo.sem, w_lo.free(u, 2))
                        for c in range(4):
                            o = (4 * k + c) * P
                            last = pe.transpose(t_ps[:, k, c * P:(c + 1) * P], raw[:, j, o:o + P], ident[:])
                        last.then_inc(turned.sem, 1)

            def gate_up(pr, s):
                m = pr * 2 + s
                pe.wait_ge(w_lo.sem, w_lo.done(m * 6 + 5))
                for j in range(2):
                    pe.wait_ge(gone.sem, gone.free(m * 2 + j, 2))
                    for u in range(2):
                        for c in range(DC):
                            last = split_matmul(pe, g_ps[:, j, u], [x[:, s, u, c * P:(c + 1) * P] for x in gu],
                                                [x[:, c, j * 512:(j + 1) * 512] for x in xT], c == 0, c == DC - 1)
                        last.then_inc(gated.sem, 1)

            def down(pr, q):
                pe.wait_ge(h_lo.sem, h_lo.done(pr * 4 + 3))
                for k in range(NT):
                    t, n = k // 2, k % 2
                    pe.wait_ge(added.sem, added.free(pr * NT + k, 2))
                    for s in range(2):
                        last = split_matmul(pe, y_ps[:, k % 2], [x[:, s, t * P:(t + 1) * P] for x in hT],
                                            [x[:, weights_slot(q, s), n * 512:(n + 1) * 512] for x in dn], s == 0, s == 1)
                    last.then_inc(tiles.sem, 1)

            def body(pr, q):
                for s in range(2):
                    turn(pr, q, s)
                    gate_up(pr, s)
                down(pr, q)

            program(pe, body)

        @block.scalar
        def _(act):
            silu.open(act)

            def body(pr, q):
                for s in range(2):
                    m = pr * 2 + s
                    act.wait_ge(gated.sem, gated.free(m * 4 + 3, 8))
                    act.wait_ge(tiles.sem, tiles.free(pr * NT + (NT - 1), 2 * NT))
                    for j in range(3):
                        for k in range(2):
                            act.wait_ge(turned.sem, turned.done(m * 6 + (2 * j + k)))
                            dst = gu[0][:, s, j, k * 512:(k + 1) * 512] if j < 2 else dn[0][:, weights_slot(q, s), k * 512:(k + 1) * 512]
                            act.activation(dst, t_ps[:, k], ACT.Copy).then_inc(w_hi.sem, 1)
                    for j in range(2):
                        a = m * 2 + j
                        act.wait_ge(gated.sem, gated.done(m * 4 + (2 * j)))
                        act.wait_ge(gone.sem, gone.free(a, 2))
                        act.activation(act_s[:, j], g_ps[:, j, 0], ACT.Silu).then_inc(silu.sem, 1)
                        act.wait_ge(gone.sem, gone.done(a))
                        act.wait_ge(tiles.sem, tiles.free(pr * NT + (NT - 1), NT))
                        act.activation(hT[0][:, s, j * 512:(j + 1) * 512], hid[:, j], ACT.Copy).then_inc(h_hi.sem, 1)

            program(act, body)

        @block.vector
        def _(dve):
            w_lo.open(dve)
            gone.open(dve)
            h_lo.open(dve)
            added.open(dve)

            def body(pr, q):
                for s in range(2):
                    m = pr * 2 + s
                    for j in range(3):
                        for k in range(2):
                            dve.wait_ge(w_hi.sem, w_hi.done(m * 6 + (2 * j + k)))
                            hi, lo = [x[:, s, j, k * 512:(k + 1) * 512] if j < 2 else y[:, weights_slot(q, s), k * 512:(k + 1) * 512]
                                      for x, y in zip(gu, dn)]
                            dve.tensor_tensor(lo, t_ps[:, k], f32(hi), ALU.subtract).then_inc(w_lo.sem, 1)
                    for j in range(2):
                        a = m * 2 + j
                        dve.wait_ge(gated.sem, gated.done(m * 4 + (2 * j + 1)))
                        dve.wait_ge(silu.sem, silu.done(a))
                        dve.wait_ge(h_lo.sem, h_lo.free(a, 2))
                        dve.tensor_tensor(hid[:, j], g_ps[:, j, 1], act_s[:, j], ALU.mult).then_inc(gone.sem, 1)
                        dve.wait_ge(h_hi.sem, h_hi.done(a))
                        sl = (slice(None), s, slice(j * 512, (j + 1) * 512))
                        dve.tensor_tensor(hT[1][sl], hid[:, j], f32(hT[0][sl]), ALU.subtract).then_inc(h_lo.sem, 1)
                for k in range(NT):
                    t, n = k // 2, k % 2
                    sl = slice(n * 512, (n + 1) * 512)
                    dve.wait_ge(tiles.sem, tiles.done(pr * NT + k))
                    dve.tensor_tensor(X[:, t, sl], y_ps[:, k % 2], X[:, t, sl], ALU.add).then_inc(added.sem, 1)

            program(dve, body)


def store_stage(nc, X, out):
    with ExitStack() as ctx:
        stored = ctx.enter_context(nc.semaphore("out_stored"))
        block = ctx.enter_context(nc.Block())

        @block.sync
        def _(sp):
            sp.dma_start(out.rearrange("b (t p) d -> p (b t) d", p=P), X[:]).then_inc(stored, 16)
            sp.wait_ge(stored, 16)


def build(nc, x, context, mask, wq, wk, wv, wo, router_w, router_b, expert_b, s1, z1, s2, z2,
          w1, w2, w3, cos_q, sin_q, cos_k, sin_k, out):
    def scratch(name, shape):
        return nc.dram_tensor(name, shape, F32, kind="Internal").ap()

    q_d = scratch("q_d", (HQ, DH, T))
    k_d = scratch("k_d", (B, HKV, DH, SK))
    v_d = scratch("v_d", (B, KT, P, D))
    o_d = scratch("o_d", (HQ, DH, T))
    wq_d = scratch("wq_d", (HC, P, 3 * D))
    spent.clear()
    with ExitStack() as ctx:
        X = ctx.enter_context(nc.sbuf_tensor("X", [P, TT, D], F32))
        ident = ctx.enter_context(nc.sbuf_tensor("ident", [P, P], F32))
        ident_bf = ctx.enter_context(nc.sbuf_tensor("ident_bf", [P, P], BF16))
        load_stage(nc, x, X, ident, ident_bf)
        nf4_stage(nc, w1, w2, w3, wq_d)
        with ExitStack() as c:
            xT = [c.enter_context(nc.sbuf_tensor(f"xT_{n}", [P, DC, T], F32R)) for n in ("h", "l")]
            norm_stage(nc, "n0", X, ident, xT=xT)
            project_stage(nc, "pq", xT, wq, HQ, lambda h: q_d[bass.ds(h, 1)].rearrange("a p n -> p (a n)"),
                          cos_q, sin_q, [(0, 512), (0, 512)])
        with ExitStack() as c:
            cT = [c.enter_context(nc.sbuf_tensor(f"cT_{n}", [P, DC, SK], F32R)) for n in ("h", "l")]
            for b in range(B):
                context_stage(nc, f"c{b}", context[b], ident, cT)
                project_stage(nc, f"pk{b}", cT, wk, HKV, lambda h: k_d[b, bass.ds(h, 1)].rearrange("a p n -> p (a n)"),
                              cos_k, sin_k, [(0, 512), (512, 1024)])
                value_stage(nc, f"v{b}", cT, wv, lambda t, h: v_d[b, t, :, h * 512:(h + 1) * 512])
        clear_stage(nc)
        attention_stage(nc, q_d, k_d, v_d, o_d, mask, ident)
        output_stage(nc, o_d, wo, X)
        with ExitStack() as c:
            xn = c.enter_context(nc.sbuf_tensor("xn", [P, TT, D], F32))
            norm_stage(nc, "n1", X, ident, xn_all=xn)
            router_stage(nc, X, xn, ident, router_w, router_b, expert_b)
            norm_stage(nc, "n2", X, ident, xn_all=xn)
            quantised_stage(nc, X, xn, ident_bf, context, (s1, z1, s2, z2))
        with ExitStack() as c:
            xT = [c.enter_context(nc.sbuf_tensor(f"yT_{n}", [P, DC, T], F32R)) for n in ("h", "l")]
            norm_stage(nc, "n3", X, ident, xT=xT)
            ffn_stage(nc, xT, X, ident, wq_d)
        store_stage(nc, X, out)


_INS = ["x", "ctx_4096", "mask_BxSxS2_ff0", "L0_xattn_wq", "L0_xattn_wk", "L0_xattn_wv", "L0_xattn_wo",
        "L0_ffn_router_weight", "L0_ffn_router_bias", "L0_ffn_expert_bias", "L1_xattn_x1_scale",
        "L1_xattn_x1_zp", "L1_xattn_x2_scale", "L1_xattn_x2_zp", "L1_ffn_w1", "L1_ffn_w2", "L1_ffn_w3"]


def rotary_tables():
    inv = np.float32(1.0) / np.float32(10000.0) ** (np.arange(0, DH, 2, dtype=np.float32) / np.float32(DH))
    ang = inv[:, None] * np.arange(SK, dtype=np.float32)[None, :]
    cos = np.concatenate([np.cos(ang)] * 2).astype(np.float32)
    sin = np.concatenate([np.sin(ang), -np.sin(ang)]).astype(np.float32)
    scale = np.float64(DH) ** -0.5
    return ((cos[:, :SQ] * scale).astype(np.float32), (sin[:, :SQ] * scale).astype(np.float32), cos, sin)


def kernel(**inputs):
    import concourse.bacc as bacc
    from concourse.bass_utils import run_bass_kernel_spmd

    nc = bacc.Bacc("TRN2", target_bir_lowering=False, num_devices=1)
    arrays = {n: np.ascontiguousarray(inputs[n]) for n in _INS}
    arrays.update(zip(("cos_q", "sin_q", "cos_k", "sin_k"), rotary_tables()))
    args = [nc.dram_tensor(f"in_{n}", a.shape, mybir.dt.from_np(a.dtype), kind="ExternalInput").ap()
            for n, a in arrays.items()]
    out = nc.dram_tensor("out_x", (B, SQ, D), F32, kind="ExternalOutput").ap()
    build(nc, *args, out)
    r = run_bass_kernel_spmd(nc, [{f"in_{n}": a for n, a in arrays.items()}], core_ids=[0])
    return r.results[0]["out_x"]
```

```python
from contextlib import ExitStack

import numpy as np
import concourse.bass as bass
from concourse import mybir
from concourse.alu_op_type import AluOpType as ALU

F32 = mybir.dt.float32
F32R = mybir.dt.float32r
BF16 = mybir.dt.bfloat16
ACT = mybir.ActivationFunctionType
AX = mybir.AxisListType

P = 128
B, SQ, SK, D = 2, 512, 1024, 1024
T = B * SQ
TT = T // P
DC = D // P
HQ, HKV, DH = 32, 8, 128
GRP = HQ // HKV
KT = SK // P
QT = SQ // P
E, TOPK = 64, 8
HF = 2752
HC = -(-HF // P)
BLK = 64
EPS = 1e-5
ROUND = 1.5 * 2.0 ** 23
QMAX = 255.0
QMID = 128.0
NEG = -3.0e38

CODE = np.array([-1.0, -0.6961928009986877, -0.5250730514526367, -0.39491748809814453,
                 -0.28444138169288635, -0.18477343022823334, -0.09105003625154495, 0.0,
                 0.07958029955625534, 0.16093020141124725, 0.24611230194568634,
                 0.33791524171829224, 0.44070982933044434, 0.5626170039176941,
                 0.7229568362236023, 1.0], np.float32)
BOUNDS = (CODE[:-1] + CODE[1:]) * np.float32(0.5)


def exact_step(a, b):
    d = np.float32(b - a)
    for c in (d, np.nextafter(d, np.float32(9)), np.nextafter(d, np.float32(-9))):
        if np.float32(a + c) == b:
            return float(c)
    raise AssertionError


STEPS = [exact_step(a, b) for a, b in zip(CODE[:-1], CODE[1:])]
NS4 = len(STEPS)
SHARP = 2.0 ** 40


spent = []


class Event:

    def __init__(self, ctx, nc, name, spare=0):
        self.sem = ctx.enter_context(nc.semaphore(name))
        spent.append(self.sem)
        self.spare = spare

    def open(self, eng):
        eng.sem_inc(self.sem, self.spare)

    def done(self, n):
        return n + 1 + self.spare

    def free(self, n, ring):
        return n + 1 - ring + self.spare


def make_tools(ctx, nc, tag):
    def sb(name, shape, dt):
        return ctx.enter_context(nc.sbuf_tensor(f"{tag}_{name}", shape, dt))

    def ps(name, shape, dt=F32):
        return ctx.enter_context(nc.psum_tensor(f"{tag}_{name}", shape, dt))

    def sem(name):
        spent.append(ctx.enter_context(nc.semaphore(f"{tag}_{name}")))
        return spent[-1]

    def event(name, spare=0):
        return Event(ctx, nc, f"{tag}_{name}", spare)

    return sb, ps, sem, event


def f32(ap):
    return ap.bitcast(F32)


def split_matmul(pe, out, w, x, start, stop):
    pe.matmul(out, w[0], x[0], start=start, stop=False)
    pe.matmul(out, w[0], x[1], start=False, stop=False)
    return pe.matmul(out, w[1], x[0], start=False, stop=stop)


class Nf4:
    NB = D // BLK

    def __init__(self, tools, sharp):
        sb, _, sem, event = tools
        self.sharp = sharp
        self.raw = sb("nf_raw", [P, 2, D], F32)
        self.above = sb("nf_above", [P, 2, D], F32)
        self.val = sb("nf_val", [P, 2, D], F32)
        self.am = sb("nf_am", [P, 2, 3, self.NB], F32)
        self.loaded = [sem("nf_loaded0"), sem("nf_loaded1")]
        self.stored = [sem("nf_stored0"), sem("nf_stored1")]
        self.seq = event("nf_seq")
        self.maxed = event("nf_maxed")
        self.normed = event("nf_normed")
        self.above_done = event("nf_above_done")
        self.stepped = event("nf_stepped", 2 * NS4)
        self.finished = event("nf_finished", 2)

    def blocks(self, ap, width):
        return ap[:, 0:width].rearrange("p (n b) -> p n b", b=BLK)

    def open_sync(self, sp):
        for s in range(2):
            sp.sem_inc(self.stored[s], 16)

    def open_vector(self, dve):
        self.stepped.open(dve)

    def open_gpsimd(self, pool):
        self.finished.open(pool)

    def load_sync(self, sp, n, s, parts, width=D):
        sp.wait_ge(self.finished.sem, self.finished.free(n, 2))
        w = width // len(parts)
        for k, part in enumerate(parts):
            sp.dma_start(self.raw[:, s, k * w:(k + 1) * w], part).then_inc(self.loaded[s], 16)

    def store_sync(self, sp, n, s, parts, width=D):
        sp.wait_ge(self.finished.sem, self.finished.done(n))
        w = width // len(parts)
        for k, part in enumerate(parts):
            sp.dma_start(part, self.val[:, s, k * w:(k + 1) * w]).then_inc(self.stored[s], 16)

    def close_sync(self, sp, counts):
        for s in range(2):
            sp.wait_ge(self.stored[s], 16 * (counts[s] + 1))

    def max_vector(self, dve, n, s, before, width=D, parts=1):
        am = self.am
        dve.wait_ge(self.finished.sem, self.finished.free(n, 2))
        dve.wait_ge(self.loaded[s], before * 16 + 16 * parts)
        dve.tensor_reduce(am[:, s, 0, 0:width // BLK], self.blocks(self.raw[:, s], width), AX.X, ALU.max,
                          apply_absolute_value=True).then_inc(self.seq.sem, 1)
        dve.wait_ge(self.seq.sem, self.seq.done(2 * n))
        w = slice(0, width // BLK)
        dve.scalar_tensor_tensor(am[:, s, 1, w], am[:, s, 0, w], 0.0, am[:, s, 0, w], ALU.is_equal, ALU.add).then_inc(self.seq.sem, 1)
        dve.wait_ge(self.seq.sem, self.seq.done(2 * n + 1))
        dve.reciprocal(am[:, s, 2, w], am[:, s, 1, w]).then_inc(self.maxed.sem, 1)

    def norm_gpsimd(self, pool, n, s, width=D):
        pool.wait_ge(self.maxed.sem, self.maxed.done(n))
        raw = self.blocks(self.raw[:, s], width)
        pool.tensor_tensor(raw, raw, self.am[:, s, 2, 0:width // BLK].unsqueeze(2).broadcast_to((P, width // BLK, BLK)),
                           ALU.mult).then_inc(self.normed.sem, 1)

    def above_scalar(self, act, n, s, steps, width=D):
        for j in steps:
            if j == 0:
                act.wait_ge(self.normed.sem, self.normed.done(n))
            act.wait_ge(self.stepped.sem, n * NS4 + (j - 1 + 2 * NS4))
            act.activation(self.above[:, (s + j) % 2, 0:width], self.raw[:, s, 0:width], ACT.Relu,
                           bias=self.sharp[:, j:j + 1], scale=SHARP).then_inc(self.above_done.sem, 1)

    def step_vector(self, dve, n, s, steps, before, width=D):
        for j in steps:
            v = self.val[:, s, 0:width]
            above = self.above[:, (s + j) % 2, 0:width]
            dve.wait_ge(self.above_done.sem, n * NS4 + (j + 1))
            if j == 0:
                dve.wait_ge(self.stored[s], before * 16 + 16)
                dve.tensor_scalar(v, above, STEPS[0], float(CODE[0]), ALU.min, ALU.add).then_inc(self.stepped.sem, 1)
            else:
                dve.wait_ge(self.stepped.sem, n * NS4 + (j + 2 * NS4))
                dve.scalar_tensor_tensor(v, above, STEPS[j], v, ALU.min, ALU.add).then_inc(self.stepped.sem, 1)

    def finish_gpsimd(self, pool, n, s, width=D):
        pool.wait_ge(self.stepped.sem, n * NS4 + 3 * NS4)
        v = self.blocks(self.val[:, s], width)
        pool.tensor_tensor(v, v, self.am[:, s, 0, 0:width // BLK].unsqueeze(2).broadcast_to((P, width // BLK, BLK)),
                           ALU.mult).then_inc(self.finished.sem, 1)


def share(total, k, n):
    return range(total * k // n, total * (k + 1) // n)


def clear_stage(nc):
    with nc.Block() as block:
        @block.sync
        def _(sp):
            for s in spent:
                sp.sem_clear(s)
    spent.clear()


def load_stage(nc, x, X, ident, ident_bf, sharp):
    with ExitStack() as ctx:
        sb, ps, sem, event = make_tools(ctx, nc, "ld")
        x_in, zeroed, made = sem("x_in"), sem("zeroed"), sem("made")
        block = ctx.enter_context(nc.Block())

        @block.sync
        def _(sp):
            sp.dma_start(X[:], x.rearrange("b (t p) d -> p (b t) d", p=P)).then_inc(x_in, 16)
            sp.wait_ge(x_in, 16)

        @block.gpsimd
        def _(pool):
            for j in range(NS4):
                pool.memset(sharp[:, j:j + 1], -SHARP * float(BOUNDS[j]))
            pool.memset(ident[:], 0.0).then_inc(zeroed, 1)
            pool.wait_ge(zeroed, 1)
            pool.affine_select(out=ident[:], in_=ident[:], compare_op=ALU.not_equal, fill=1.0,
                               base=0, pattern=[[-1, P]], channel_multiplier=1).then_inc(made, 1)
            pool.wait_ge(made, 1)
            pool.tensor_copy(ident_bf[:], ident[:]).then_inc(made, 1)


def norm_stage(nc, tag, X, ident, xT=None, xn_all=None, stats=None):
    with ExitStack() as ctx:
        sb, ps, sem, event = make_tools(ctx, nc, tag)
        st = sb("st", [P, TT, 2, 6], F32)
        mv = sb("mv", [P, TT, 2], F32)
        s = sb("s", [P, 5, TT], F32)
        xn = xn_all if xn_all is not None else sb("xn", [P, 2, D], F32)
        slots = TT if xn_all is not None else 2
        seq, var_ready, root_ready, normed = sem("seq"), sem("var"), sem("root"), sem("normed")
        turned, hi_out, lo_out = sem("turned"), sem("hi"), sem("lo")
        if xT is not None:
            tp = ps("tp", [P, 2, DC, P])
        block = ctx.enter_context(nc.Block())

        @block.scalar
        def _(act):
            act.wait_ge(var_ready, 1)
            act.activation(s[:, 1, :], s[:, 0, :], ACT.Sqrt).then_inc(root_ready, 1)
            if xT is not None:
                for t in range(TT):
                    act.wait_ge(turned, t + 1)
                    act.activation(xT[0][:, :, t * P:(t + 1) * P], tp[:, t % 2], ACT.Copy).then_inc(hi_out, 1)

        @block.vector
        def _(dve):
            steps = [0]

            def after(ins):
                steps[0] += 1
                ins.then_inc(seq, 1)
                dve.wait_ge(seq, steps[0])

            for t in range(TT):
                for h in range(2):
                    last = dve.bn_stats(st[:, t, h, :], X[:, t, h * 512:(h + 1) * 512])
            after(last)
            for t in range(TT):
                last = dve.bn_aggr(mv[:, t, :], st[:, t, :, :].rearrange("p a b -> p (a b)"))
            after(last)
            dve.tensor_scalar(s[:, 0, :], mv[:, :, 1], EPS, None, ALU.add).then_inc(var_ready, 1)
            dve.wait_ge(root_ready, 1)
            after(dve.reciprocal(s[:, 2, :], s[:, 1, :]))
            after(dve.tensor_tensor(s[:, 3, :], s[:, 0, :], s[:, 2, :], ALU.mult))
            after(dve.tensor_tensor(s[:, 3, :], s[:, 3, :], s[:, 1, :], ALU.add))
            after(dve.tensor_scalar(s[:, 2, :], s[:, 3, :], 0.5, None, ALU.mult))
            after(dve.reciprocal(s[:, 4, :], s[:, 2, :]))

            def norm(t):
                if xT is not None and t >= 2:
                    dve.wait_ge(turned, t - 1)
                dve.tensor_scalar(xn[:, t % slots, :], X[:, t, :], mv[:, t, 0:1], s[:, 4, t:t + 1],
                                  ALU.subtract, ALU.mult).then_inc(normed, 1)

            def low(t):
                dve.wait_ge(hi_out, t + 1)
                sl = slice(t * P, (t + 1) * P)
                dve.tensor_tensor(xT[1][:, :, sl], tp[:, t % 2], f32(xT[0][:, :, sl]), ALU.subtract).then_inc(lo_out, 1)

            norm(0)
            for t in range(TT):
                if t + 1 < TT:
                    norm(t + 1)
                if xT is not None:
                    low(t)

        if xT is not None:
            @block.tensor
            def _(pe):
                for t in range(TT):
                    pe.wait_ge(normed, t + 1)
                    if t >= 2:
                        pe.wait_ge(lo_out, t - 1)
                    for c in range(DC):
                        last = pe.transpose(tp[:, t % 2, c, :], xn[:, t % 2, c * P:(c + 1) * P], ident[:])
                    last.then_inc(turned, 1)


def project_stage(nc, tag, xT, w, heads, store, cos_d, sin_d, rows, sharp, unit_src, unit_dst):
    with ExitStack() as ctx:
        sb, ps, sem, event = tools = make_tools(ctx, nc, tag)
        width = max(stop for _, stop in rows)
        cos = sb("cos", [P, width], F32)
        sin = sb("sin", [P, width], F32)
        raw = sb("raw", [P, 2, DC, DH], F32)
        wh = sb("wh", [P, 2, DC, DH], F32R)
        wl = sb("wl", [P, 2, DC, DH], F32R)
        ta = sb("ta", [P, 2, 512], F32)
        tb = sb("tb", [P, 2, 512], F32)
        res = sb("res", [P, 2, 1024], F32)
        pj = ps("pj", [P, 2, 2, 512])
        nf = Nf4(tools, sharp)
        tab_in = sem("tab_in")
        raw_in = [sem("raw_in0"), sem("raw_in1")]
        stored = [sem("stored0"), sem("stored1")]
        hi_out = event("hi")
        lo_out = event("lo", 2)
        tiles = event("tiles", 4)
        read = event("read", 4)
        summed = event("summed", 2)
        wv_ = w.rearrange("(c p) n -> p c n", p=P)
        block = ctx.enter_context(nc.Block())
        PASSES = heads // 2

        def program(eng, body):
            with eng.Fori(0, PASSES // 2 - 1) as i:
                for u in range(2):
                    body(2 * i + u, u, i, False)
            for u in range(2):
                body(PASSES - 2 + u, u, PASSES // 2 - 1, u == 1)

        @block.sync
        def _(sp):
            def load_head(h, s):
                sp.wait_ge(lo_out.sem, lo_out.free(h, 2))
                sp.dma_start(raw[:, s], wv_[:, :, bass.ds(h * DH, DH)]).then_inc(raw_in[s], 16)

            def store_head(i, s):
                sp.wait_ge(summed.sem, summed.done(4 * i + 2 * s + 1))
                sp.dma_start(store(2 * i + s), res[:, s, :]).then_inc(stored[s], 16)

            def body(i, u, _, last):
                if not last:
                    load_head(2 * i + 2, 0)
                    nf.load_sync(sp, i + 1, 1 - u, [unit_src(i + 1)])
                    load_head(2 * i + 3, 1)
                for s in range(2):
                    store_head(i, s)
                nf.store_sync(sp, i, u, [unit_dst(i)])

            for s in range(2):
                sp.sem_inc(stored[s], 16)
            nf.open_sync(sp)
            lo_out.open(sp)
            load_head(0, 0)
            nf.load_sync(sp, 0, 0, [unit_src(0)])
            sp.dma_start(cos[:], cos_d).then_inc(tab_in, 16)
            sp.dma_start(sin[:], sin_d).then_inc(tab_in, 16)
            load_head(1, 1)
            program(sp, body)
            for s in range(2):
                sp.wait_ge(stored[s], 16 * (PASSES + 1))
            nf.close_sync(sp, [PASSES // 2] * 2)

        @block.scalar
        def _(act):
            def high(i, s):
                act.wait_ge(raw_in[s], i * 16 + 16)
                act.wait_ge(tiles.sem, tiles.free(4 * i + 2 * s + 1, 4))
                act.activation(wh[:, s], raw[:, s], ACT.Copy).then_inc(hi_out.sem, 1)

            def body(i, u, _, last):
                high(i, 1)
                nf.above_scalar(act, i, u, share(NS4, 0, 2))
                if not last:
                    high(i + 1, 0)
                nf.above_scalar(act, i, u, share(NS4, 1, 2))

            high(0, 0)
            program(act, body)

        @block.vector
        def _(dve):
            def low(i, s):
                dve.wait_ge(hi_out.sem, hi_out.done(2 * i + s))
                dve.tensor_tensor(wl[:, s], raw[:, s], f32(wh[:, s]), ALU.subtract).then_inc(lo_out.sem, 1)

            def rotate(i, s, j):
                n = 4 * i + 2 * s + j
                a, b = rows[j]
                src = pj[:, s, j, :]
                dve.wait_ge(tiles.sem, tiles.done(n))
                dve.wait_ge(summed.sem, summed.free(n, 2))
                dve.tensor_tensor(ta[:, j], src, cos[:, a:b], ALU.mult)
                dve.tensor_tensor(tb[0:64, j], src[64:128], sin[64:128, a:b], ALU.mult)
                dve.tensor_tensor(tb[64:128, j], src[0:64], sin[0:64, a:b], ALU.mult).then_inc(read.sem, 1)

            def body(i, u, before, last):
                nf.max_vector(dve, i, u, before)
                for s in range(2):
                    if s == 0:
                        low(i, 1)
                    elif not last:
                        low(i + 1, 0)
                    for j in range(2):
                        rotate(i, s, j)
                        nf.step_vector(dve, i, u, share(NS4, 2 * s + j, 4), before)

            read.open(dve)
            nf.open_vector(dve)
            low(0, 0)
            dve.wait_ge(tab_in, 32)
            program(dve, body)

        @block.gpsimd
        def _(pool):
            def body(i, u, before, last):
                nf.norm_gpsimd(pool, i, u)
                for s in range(2):
                    for j in range(2):
                        n = 4 * i + 2 * s + j
                        if j == 0:
                            pool.wait_ge(stored[s], i * 16 + 16)
                        pool.wait_ge(read.sem, read.done(n))
                        pool.tensor_tensor(res[:, s, j * 512:(j + 1) * 512], ta[:, j], tb[:, j],
                                           ALU.add).then_inc(summed.sem, 1)
                nf.finish_gpsimd(pool, i, u)

            summed.open(pool)
            nf.open_gpsimd(pool)
            program(pool, body)

        @block.tensor
        def _(pe):
            tiles.open(pe)
            with pe.Fori(0, PASSES) as i:
                for s in range(2):
                    pe.wait_ge(lo_out.sem, lo_out.done(2 * i + s))
                    for j in range(2):
                        pe.wait_ge(read.sem, read.free(4 * i + 2 * s + j, 4))
                        for c in range(DC):
                            last = split_matmul(pe, pj[:, s, j, :], (wh[:, s, c, :], wl[:, s, c, :]),
                                                [x[:, c, j * 512:(j + 1) * 512] for x in xT],
                                                c == 0, c == DC - 1)
                        last.then_inc(tiles.sem, 1)


def context_stage(nc, tag, ctx_b, ident, cT):
    with ExitStack() as ctx:
        sb, ps, sem, event = make_tools(ctx, nc, tag)
        rows = sb("rows", [P, 3, D], F32)
        tp = ps("tp", [P, 2, DC, P])
        rows_in = [sem(f"rows_in{k}") for k in range(3)]
        turned, hi_out, lo_out = sem("turned"), sem("hi"), sem("lo")
        block = ctx.enter_context(nc.Block())

        @block.sync
        def _(sp):
            for t in range(KT):
                if t >= 3:
                    sp.wait_ge(turned, t - 2)
                sp.dma_start(rows[:, t % 3], ctx_b[t * P:(t + 1) * P, :]).then_inc(rows_in[t % 3], 16)

        @block.tensor
        def _(pe):
            for t in range(KT):
                pe.wait_ge(rows_in[t % 3], 16 * (t // 3 + 1))
                if t >= 2:
                    pe.wait_ge(lo_out, t - 1)
                for c in range(DC):
                    last = pe.transpose(tp[:, t % 2, c, :], rows[:, t % 3, c * P:(c + 1) * P], ident[:])
                last.then_inc(turned, 1)

        @block.scalar
        def _(act):
            for t in range(KT):
                act.wait_ge(turned, t + 1)
                act.activation(cT[0][:, :, t * P:(t + 1) * P], tp[:, t % 2], ACT.Copy).then_inc(hi_out, 1)

        @block.vector
        def _(dve):
            for t in range(KT):
                sl = slice(t * P, (t + 1) * P)
                dve.wait_ge(hi_out, t + 1)
                dve.tensor_tensor(cT[1][:, :, sl], tp[:, t % 2], f32(cT[0][:, :, sl]), ALU.subtract).then_inc(lo_out, 1)


def value_stage(nc, tag, cT, w, store, sharp, units):
    with ExitStack() as ctx:
        sb, ps, sem, event = tools = make_tools(ctx, nc, tag)
        raw = sb("raw", [P, 2, 2, 512], F32)
        wh = sb("wh", [P, 2, DC, 512], F32R)
        wl = sb("wl", [P, 2, DC, 512], F32R)
        res = sb("res", [P, 2, 512], F32)
        acc = ps("acc", [P, 2, 512])
        nf = Nf4(tools, sharp)
        raw_in = [sem("raw_in0"), sem("raw_in1")]
        hi_out, lo_out, tiles, copied = sem("hi"), sem("lo"), sem("tiles"), sem("copied")
        stored = [sem("stored0"), sem("stored1")]
        block = ctx.enter_context(nc.Block())
        halves = D // 512
        CP = DC // 2
        wv_ = w.rearrange("(q c p) n -> q p c n", p=P, c=2)

        @block.sync
        def _(sp):
            def load_weights(m):
                h, q = m // CP, m % CP
                if m >= 2:
                    sp.wait_ge(lo_out, m - 1)
                sp.dma_start(raw[:, m % 2], wv_[q][:, :, h * 512:(h + 1) * 512]).then_inc(raw_in[m % 2], 16)

            def finish_unit(u):
                nf.store_sync(sp, u, u % 2, units[u][1], units[u][2])

            nf.open_sync(sp)
            for m in range(CP):
                load_weights(m)
                if m < 2:
                    nf.load_sync(sp, m, m, units[m][0], units[m][2])
            for m in range(CP, halves * CP):
                load_weights(m)
            for h in range(halves):
                for t in range(KT):
                    n = h * KT + t
                    sp.wait_ge(copied, n + 1)
                    sp.dma_start(store(t, h), res[:, n % 2]).then_inc(stored[n % 2], 16)
                    if n % 4 == 3 and n > 4:
                        u = n // 4 - 1
                        finish_unit(u)
                        if u + 2 < len(units):
                            nf.load_sync(sp, u + 2, u % 2, units[u + 2][0], units[u + 2][2])
            finish_unit(len(units) - 1)
            nf.close_sync(sp, [sum(len(u[0]) for u in units[s::2]) for s in range(2)])
            for s in range(2):
                sp.wait_ge(stored[s], 16 * (halves * KT // 2))

        @block.scalar
        def _(act):
            def high(m):
                h, q = m // CP, m % CP
                act.wait_ge(raw_in[m % 2], 16 * (m // 2 + 1))
                act.activation(wh[:, h, 2 * q:2 * q + 2], raw[:, m % 2], ACT.Copy).then_inc(hi_out, 1)

            for m in range(CP):
                high(m)
            for h in range(halves):
                for t in range(KT):
                    n = h * KT + t
                    act.wait_ge(tiles, n + 1)
                    if n >= 2:
                        act.wait_ge(stored[n % 2], 16 * (n // 2))
                    act.activation(res[:, n % 2], acc[:, n % 2], ACT.Copy).then_inc(copied, 1)
                    if n < CP:
                        high(CP + n)
                    nf.above_scalar(act, n // 4, n // 4 % 2, share(NS4, n % 4, 4), units[n // 4][2])

        @block.gpsimd
        def _(pool):
            nf.open_gpsimd(pool)
            for u in range(len(units)):
                nf.norm_gpsimd(pool, u, u % 2, units[u][2])
                nf.finish_gpsimd(pool, u, u % 2, units[u][2])

        @block.vector
        def _(dve):
            def low(m):
                h, q = m // CP, m % CP
                dve.wait_ge(hi_out, m + 1)
                dve.tensor_tensor(wl[:, h, 2 * q:2 * q + 2], raw[:, m % 2], f32(wh[:, h, 2 * q:2 * q + 2]), ALU.subtract).then_inc(lo_out, 1)

            nf.open_vector(dve)
            for m in range(CP):
                low(m)
            parts = [0, 0]
            for n in range(halves * KT):
                u = n // 4
                if n % 4 == 0:
                    nf.max_vector(dve, u, u % 2, parts[u % 2], units[u][2], len(units[u][0]))
                nf.step_vector(dve, u, u % 2, share(NS4, n % 4, 4), parts[u % 2], units[u][2])
                if n < CP:
                    low(CP + n)
                if n % 4 == 3:
                    parts[u % 2] += len(units[u][0])

        @block.tensor
        def _(pe):
            for h in range(halves):
                for t in range(KT):
                    n = h * KT + t
                    if n >= 2:
                        pe.wait_ge(copied, n - 1)
                    for c in range(DC):
                        if t == 0 and c % 2 == 0:
                            pe.wait_ge(lo_out, h * CP + c // 2 + 1)
                        last = split_matmul(pe, acc[:, n % 2], [x[:, c, t * P:(t + 1) * P] for x in cT],
                                            (wh[:, h, c, :], wl[:, h, c, :]), c == 0, c == DC - 1)
                    last.then_inc(tiles, 1)


def attention_stage(nc, q_d, k_d, v_d, o_d, mask, ident):
    with ExitStack() as ctx:
        sb, ps, sem, event = make_tools(ctx, nc, "at")
        KG = 2
        HP = KG * GRP
        NS = HP * QT
        PASSES = HKV // KG
        HALF = KT // 2

        mk = sb("mk", [P, B * QT, SK], F32)
        kraw = sb("kraw", [P, SK], F32)
        vraw = sb("vraw", [P, KT, DH], F32)
        kk = [sb(f"k{x}", [P, KG, SK], F32R) for x in ("h", "l")]
        vv = [sb(f"v{x}", [P, KG, KT, DH], F32R) for x in ("h", "l")]
        qraw = sb("qraw", [P, 2, SQ], F32)
        qq = [sb(f"q{x}", [P, 2, SQ], F32R) for x in ("h", "l")]
        sc = sb("sc", [P, 2, SK], F32)
        pr = sb("pr", [P, 2, SK], F32)
        pt = [sb(f"pt{x}", [P, 2, KT, SQ], F32R) for x in ("h", "l")]
        ot = sb("ot", [P, 2, SQ], F32)
        sm = sb("sm", [P, 2, 4], F32)
        turnstile = sb("turnstile", [P, 1], F32)
        s_ps = ps("s", [P, 2, SK])
        t_ps = ps("t", [P, 2, HALF, P])
        o_ps = ps("o", [P, 2, SQ])

        mask_in, k_in, v_in = sem("mask_in"), sem("k_in"), sem("v_in")
        q_in = [sem("q_in0"), sem("q_in1")]
        o_st = [sem("o_st0"), sem("o_st1")]
        k_hi, v_hi, q_hi = event("k_hi"), event("v_hi"), event("q_hi")
        k_lo, v_lo = event("k_lo", 1), event("v_lo", 1)
        q_lo = event("q_lo", 2)
        scored = event("scored", NS)
        masked = event("masked", 2)
        maxed = event("maxed")
        expd = event("expd", 2)
        recipd = event("recipd")
        normed = event("normed")
        turned = event("turned", 4)
        t_hi = event("t_hi")
        t_lo = event("t_lo", 2)
        mixed = event("mixed", HP)
        copied = event("copied", 2)
        block = ctx.enter_context(nc.Block())

        def group(b, i, g):
            return i * KG + (b * HKV + g)

        def head(b, i, h):
            return i * HP + (b * HQ + h)

        def step(b, i, n):
            return i * NS + (b * HQ * QT + n)

        FETCH = [(0, "k", 0), (0, "q", 0), (0, "v", 0)]
        FETCH += [(QT * (h - 1) + 1, "q", h) for h in range(1, HP)]
        FETCH += [(QT * (GRP - 2), "k", 1), (QT * (GRP - 2) + 2, "v", 1)]
        FETCH.sort(key=lambda f: f[0])

        @block.sync
        def _(sp):
            sp.dma_start(mk[:], mask.rearrange("b (t p) k -> p (b t) k", p=P)).then_inc(mask_in, 16)
            for b in range(B):
                with sp.Fori(0, PASSES) as i:
                    for _, kind, x in FETCH:
                        if kind == "k":
                            sp.wait_ge(k_lo.sem, k_lo.free(group(b, i, x), 1))
                            sp.dma_start(kraw[:], k_d[b, bass.ds(i * KG + x, 1)].rearrange("a p n -> p (a n)")).then_inc(k_in, 16)
                        elif kind == "v":
                            sp.wait_ge(v_lo.sem, v_lo.free(group(b, i, x), 1))
                            sp.dma_start(vraw[:], v_d[b].rearrange("t p n -> p t n")[:, :, bass.ds(i * (KG * DH) + x * DH, DH)]).then_inc(v_in, 16)
                        else:
                            sp.wait_ge(q_lo.sem, q_lo.free(head(b, i, x), 2))
                            sp.dma_start(qraw[:, x % 2], q_d[bass.ds(i * HP + x, 1)].rearrange("a p n -> p (a n)")[:, b * SQ:(b + 1) * SQ]).then_inc(q_in[x % 2], 16)

        @block.gpsimd
        def _(pool):
            k_lo.open(pool)
            v_lo.open(pool)
            q_lo.open(pool)
            for b in range(B):
                with pool.Fori(0, PASSES) as i:
                    for _, kind, x in FETCH:
                        if kind == "k":
                            pool.wait_ge(k_hi.sem, k_hi.done(group(b, i, x)))
                            pool.tensor_tensor(kk[1][:, x], kraw[:], f32(kk[0][:, x]), ALU.subtract).then_inc(k_lo.sem, 1)
                        elif kind == "v":
                            pool.wait_ge(v_hi.sem, v_hi.done(group(b, i, x)))
                            pool.tensor_tensor(vv[1][:, x], vraw[:], f32(vv[0][:, x]), ALU.subtract).then_inc(v_lo.sem, 1)
                        else:
                            pool.wait_ge(q_hi.sem, q_hi.done(head(b, i, x)))
                            pool.tensor_tensor(qq[1][:, x % 2], qraw[:, x % 2], f32(qq[0][:, x % 2]), ALU.subtract).then_inc(q_lo.sem, 1)

        @block.scalar
        def _(act):
            def fetch(b, i, kind, x):
                if kind == "k":
                    act.wait_ge(k_in, group(b, i, x) * 16 + 16)
                    act.wait_ge(scored.sem, scored.free(step(b, i, (x + 1) * GRP * QT - 1), NS))
                    act.activation(kk[0][:, x], kraw[:], ACT.Copy).then_inc(k_hi.sem, 1)
                elif kind == "v":
                    act.wait_ge(v_in, group(b, i, x) * 16 + 16)
                    act.wait_ge(mixed.sem, mixed.free(head(b, i, (x + 1) * GRP - 1), HP))
                    act.activation(vv[0][:, x], vraw[:], ACT.Copy).then_inc(v_hi.sem, 1)
                else:
                    act.wait_ge(q_in[x % 2], i * (16 * HP // 2) + 16 * (b * HQ // 2 + x // 2 + 1))
                    act.wait_ge(scored.sem, scored.free(step(b, i, QT * (x + 1) - 1), 2 * QT))
                    act.activation(qq[0][:, x % 2], qraw[:, x % 2], ACT.Copy).then_inc(q_hi.sem, 1)

            def exponentials(b, i, n):
                act.wait_ge(maxed.sem, maxed.done(step(b, i, n)))
                act.wait_ge(turned.sem, turned.free(2 * step(b, i, n) + 1, 4))
                act.activation(pr[:, n % 2], sc[:, n % 2], ACT.Exp, bias=sm[:, n % 2, 1:2],
                               accum_out=sm[:, n % 2, 2:3]).then_inc(expd.sem, 1)

            def turn_high(b, i, n):
                h = n // QT
                if n % QT == 0:
                    act.wait_ge(mixed.sem, mixed.free(head(b, i, h), 2))
                for j in range(2):
                    act.wait_ge(turned.sem, turned.done(2 * step(b, i, n) + j))
                    act.activation(pt[0][:, h % 2, j * HALF:(j + 1) * HALF, (n % QT) * P:(n % QT + 1) * P],
                                   t_ps[:, j], ACT.Copy).then_inc(t_hi.sem, 1)

            def copy_out(b, i, h):
                act.wait_ge(mixed.sem, mixed.done(head(b, i, h)))
                act.wait_ge(o_st[h % 2], i * (16 * HP // 2) + 16 * (b * HQ // 2 + h // 2 + 1))
                act.activation(ot[:, h % 2], o_ps[:, h % 2], ACT.Copy).then_inc(copied.sem, 1)

            def store_out(b, i, h):
                act.wait_ge(copied.sem, copied.done(head(b, i, h)))
                act.dma_start(o_d[bass.ds(i * HP + h, 1)].rearrange("a p n -> p (a n)")[:, b * SQ:(b + 1) * SQ],
                              ot[:, h % 2]).then_inc(o_st[h % 2], 16)

            expd.open(act)
            copied.open(act)
            for s in range(2):
                act.sem_inc(o_st[s], 16)
            for b in range(B):
                with act.Fori(0, PASSES) as i:
                    for n in range(NS + 5):
                        for at, kind, x in FETCH:
                            if at == n:
                                fetch(b, i, kind, x)
                        if 2 <= n < NS + 2:
                            turn_high(b, i, n - 2)
                        if n < NS:
                            exponentials(b, i, n)
                        if n >= QT + 3 and (n - 3) % QT == 0:
                            copy_out(b, i, (n - 3) // QT - 1)
                        if n >= QT + 4 and (n - 4) % QT == 0:
                            store_out(b, i, (n - 4) // QT - 1)
            for s in range(2):
                act.wait_ge(o_st[s], 16 * (B * HQ // 2 + 1))

        @block.vector
        def _(dve):
            def mask_and_max(b, i, n):
                dve.wait_ge(scored.sem, scored.done(step(b, i, n)))
                dve.wait_ge(expd.sem, expd.free(step(b, i, n), 2))
                dve.memset(turnstile[:], 0.0)
                dve.tensor_tensor_reduce(sc[:, n % 2], s_ps[:, n % 2], mk[:, b * QT + n % QT], 1.0, NEG,
                                         ALU.add, ALU.max, sm[:, n % 2, 0:1]).then_inc(masked.sem, 1)
                dve.wait_ge(masked.sem, masked.done(step(b, i, n)))
                dve.tensor_scalar(sm[:, n % 2, 1:2], sm[:, n % 2, 0:1], -1.0, None, ALU.mult).then_inc(maxed.sem, 1)

            def normalise(b, i, n):
                dve.wait_ge(expd.sem, expd.done(step(b, i, n)))
                dve.reciprocal(sm[:, n % 2, 3:4], sm[:, n % 2, 2:3]).then_inc(recipd.sem, 1)
                dve.wait_ge(recipd.sem, recipd.done(step(b, i, n)))
                dve.tensor_scalar(pr[:, n % 2], pr[:, n % 2], sm[:, n % 2, 3:4], None, ALU.mult).then_inc(normed.sem, 1)

            def turn_low(b, i, n):
                h = n // QT
                for j in range(2):
                    sl = (slice(None), h % 2, slice(j * HALF, (j + 1) * HALF), slice((n % QT) * P, (n % QT + 1) * P))
                    dve.wait_ge(t_hi.sem, t_hi.done(2 * step(b, i, n) + j))
                    dve.tensor_tensor(pt[1][sl], t_ps[:, j], f32(pt[0][sl]), ALU.subtract).then_inc(t_lo.sem, 1)

            masked.open(dve)
            t_lo.open(dve)
            dve.wait_ge(mask_in, 16)
            for b in range(B):
                with dve.Fori(0, PASSES) as i:
                    for n in range(NS + 2):
                        if n < NS:
                            mask_and_max(b, i, n)
                        if 1 <= n < NS + 1:
                            normalise(b, i, n - 1)
                        if n >= 2:
                            turn_low(b, i, n - 2)

        @block.tensor
        def _(pe):
            def scores(b, i, n):
                h = n // QT
                g = h // GRP
                if n % (QT * GRP) == 0:
                    pe.wait_ge(k_lo.sem, k_lo.done(group(b, i, g)))
                if n % QT == 0:
                    pe.wait_ge(q_lo.sem, q_lo.done(head(b, i, h)))
                pe.wait_ge(masked.sem, masked.free(step(b, i, n), 2))
                for j in range(SK // 512):
                    last = split_matmul(pe, s_ps[:, n % 2, j * 512:(j + 1) * 512],
                                        [x[:, h % 2, (n % QT) * P:(n % QT + 1) * P] for x in qq],
                                        [x[:, g, j * 512:(j + 1) * 512] for x in kk], True, True)
                last.then_inc(scored.sem, 1)

            def turn(b, i, n):
                pe.wait_ge(normed.sem, normed.done(step(b, i, n)))
                for j in range(2):
                    pe.wait_ge(t_lo.sem, t_lo.free(2 * step(b, i, n) + j, 2))
                    for c in range(HALF):
                        k = j * HALF + c
                        last = pe.transpose(t_ps[:, j, c, :], pr[:, n % 2, k * P:(k + 1) * P], ident[:])
                    last.then_inc(turned.sem, 1)

            def mix(b, i, h):
                g = h // GRP
                if h % GRP == 0:
                    pe.wait_ge(v_lo.sem, v_lo.done(group(b, i, g)))
                pe.wait_ge(t_lo.sem, t_lo.done(2 * step(b, i, QT * (h + 1) - 1) + 1))
                pe.wait_ge(copied.sem, copied.free(head(b, i, h), 2))
                for c in range(KT):
                    last = split_matmul(pe, o_ps[:, h % 2], [x[:, g, c, :] for x in vv],
                                        [x[:, h % 2, c, :] for x in pt], c == 0, c == KT - 1)
                last.then_inc(mixed.sem, 1)

            scored.open(pe)
            turned.open(pe)
            mixed.open(pe)
            for b in range(B):
                with pe.Fori(0, PASSES) as i:
                    for n in range(NS + 3):
                        if n < NS:
                            scores(b, i, n)
                        if 2 <= n < NS + 2:
                            turn(b, i, n - 2)
                        if n >= QT + 2 and (n - 2) % QT == 0:
                            mix(b, i, (n - 2) // QT - 1)


def output_stage(nc, o_d, wo, X, sharp, unit_src, unit_dst):
    with ExitStack() as ctx:
        sb, ps, sem, event = tools = make_tools(ctx, nc, "ou")
        oraw = sb("oraw", [P, 2, T], F32)
        wraw = sb("wraw", [P, 2, D], F32)
        oo = [sb(f"o{x}", [P, 2, GRP, T], F32R) for x in ("h", "l")]
        ww = [sb(f"w{x}", [P, 2, GRP, D], F32R) for x in ("h", "l")]
        acc = ps("acc", [P, 4, 512])
        nf = Nf4(tools, sharp)
        NT = TT * (D // 512)
        o_in = [sem(f"o_in{r}") for r in range(2)]
        w_in = [sem(f"w_in{r}") for r in range(2)]
        o_hi, w_hi = event("o_hi"), event("w_hi")
        o_lo, w_lo = event("o_lo", 2), event("w_lo", 2)
        tiles = event("tiles", 2 * NT)
        added = event("added", 4)
        block = ctx.enter_context(nc.Block())
        PASSES = HQ // GRP // 2

        def program(eng, body):
            with eng.Fori(0, PASSES - 1) as i:
                body(i, False)
            body(PASSES - 1, True)

        def head(i, s, r):
            return i * (2 * GRP) + (s * GRP + r)

        @block.sync
        def _(sp):
            def load(i, s, r):
                h = head(i, s, r)
                sp.wait_ge(o_lo.sem, o_lo.free(h, 2))
                sp.dma_start(oraw[:, r % 2], o_d[bass.ds(h, 1)].rearrange("a p n -> p (a n)")).then_inc(o_in[r % 2], 16)
                sp.wait_ge(w_lo.sem, w_lo.free(h, 2))
                sp.dma_start(wraw[:, r % 2], wo[bass.ds(h * DH, DH), :]).then_inc(w_in[r % 2], 16)

            def body(i, last):
                for r in range(GRP):
                    load(i, 1, r)
                nf.store_sync(sp, 2 * i, 0, [unit_dst(i, 0)])
                if not last:
                    nf.load_sync(sp, 2 * i + 2, 0, [unit_src(i + 1, 0)])
                    for r in range(GRP):
                        load(i + 1, 0, r)
                nf.store_sync(sp, 2 * i + 1, 1, [unit_dst(i, 1)])
                if not last:
                    nf.load_sync(sp, 2 * i + 3, 1, [unit_src(i + 1, 1)])

            nf.open_sync(sp)
            for r in range(GRP):
                load(0, 0, r)
            for s in range(2):
                nf.load_sync(sp, s, s, [unit_src(0, s)])
            program(sp, body)
            nf.close_sync(sp, [PASSES] * 2)

        @block.scalar
        def _(act):
            def high(i, s, r):
                h = head(i, s, r)
                if r == 0:
                    act.wait_ge(tiles.sem, tiles.free(i * (2 * NT) + ((s + 1) * NT - 1), 2 * NT))
                act.wait_ge(o_in[r % 2], i * 64 + (32 * s + 16 * (r // 2 + 1)))
                act.activation(oo[0][:, s, r], oraw[:, r % 2], ACT.Copy).then_inc(o_hi.sem, 1)
                act.wait_ge(w_in[r % 2], i * 64 + (32 * s + 16 * (r // 2 + 1)))
                act.activation(ww[0][:, s, r], wraw[:, r % 2], ACT.Copy).then_inc(w_hi.sem, 1)

            def body(i, last):
                for s in range(2):
                    for r in range(GRP):
                        if s == 0:
                            high(i, 1, r)
                        elif not last:
                            high(i + 1, 0, r)
                        nf.above_scalar(act, 2 * i + s, s, share(NS4, r, GRP))

            for r in range(GRP):
                high(0, 0, r)
            program(act, body)

        @block.gpsimd
        def _(pool):
            def body(i, last):
                for s in range(2):
                    nf.norm_gpsimd(pool, 2 * i + s, s)
                    nf.finish_gpsimd(pool, 2 * i + s, s)

            nf.open_gpsimd(pool)
            program(pool, body)

        @block.vector
        def _(dve):
            def split(i, s, r):
                h = head(i, s, r)
                dve.wait_ge(o_hi.sem, o_hi.done(h))
                dve.tensor_tensor(oo[1][:, s, r], oraw[:, r % 2], f32(oo[0][:, s, r]), ALU.subtract).then_inc(o_lo.sem, 1)
                dve.wait_ge(w_hi.sem, w_hi.done(h))
                dve.tensor_tensor(ww[1][:, s, r], wraw[:, r % 2], f32(ww[0][:, s, r]), ALU.subtract).then_inc(w_lo.sem, 1)

            def body(i, last):
                for s in range(2):
                    nf.max_vector(dve, 2 * i + s, s, i)
                    for k in range(NT):
                        if k % 4 == 0 and s == 0:
                            split(i, 1, k // 4)
                        elif k % 4 == 0 and not last:
                            split(i + 1, 0, k // 4)
                        m = i * (2 * NT) + (s * NT + k)
                        t, n = k // 2, k % 2
                        dve.wait_ge(tiles.sem, tiles.done(m))
                        dve.tensor_tensor(X[:, t, n * 512:(n + 1) * 512], acc[:, k % 4],
                                          X[:, t, n * 512:(n + 1) * 512], ALU.add).then_inc(added.sem, 1)
                        nf.step_vector(dve, 2 * i + s, s, share(NS4, k, NT), i)

            o_lo.open(dve)
            w_lo.open(dve)
            added.open(dve)
            nf.open_vector(dve)
            for r in range(GRP):
                split(0, 0, r)
            program(dve, body)

        @block.tensor
        def _(pe):
            tiles.open(pe)
            with pe.Fori(0, PASSES) as i:
                for s in range(2):
                    h = i * (2 * GRP) + (s * GRP + GRP - 1)
                    pe.wait_ge(o_lo.sem, o_lo.done(h))
                    pe.wait_ge(w_lo.sem, w_lo.done(h))
                    for k in range(NT):
                        t, n = k // 2, k % 2
                        pe.wait_ge(added.sem, added.free(i * (2 * NT) + (s * NT + k), 4))
                        for r in range(GRP):
                            last = split_matmul(pe, acc[:, k % 4], [x[:, s, r, t * P:(t + 1) * P] for x in oo],
                                                [x[:, s, r, n * 512:(n + 1) * 512] for x in ww],
                                                r == 0, r == GRP - 1)
                        last.then_inc(tiles.sem, 1)


def router_stage(nc, X, xn, ident, router_w, router_b, expert_b):
    with ExitStack() as ctx:
        sb, ps, sem, event = make_tools(ctx, nc, "ro")
        rw = sb("rw", [E, D], F32)
        rwT = sb("rwT", [P, DC, E], F32)
        rb = sb("rb", [P, E], F32)
        eb = sb("eb", [E, D], F32)
        xT = sb("xT", [P, 2, DC, P], F32)
        lg = sb("lg", [P, 2, E], F32)
        ex = sb("ex", [P, 2, E], F32)
        rest = sb("rest", [P, 2, E], F32)
        top = sb("top", [P, 2, TOPK], F32)
        sm = sb("sm", [P, 2, 6], F32)
        wT = sb("wT", [E, 2, P], F32)
        tmp = sb("tmp", [P, D], F32)
        t_ps = ps("t", [P, DC, P])
        l_ps = ps("l", [P, 512])
        w_ps = ps("w", [P, 512])
        m_ps = ps("m", [P, 2, D])
        w_in, rw_turned, rw_copied = sem("w_in"), sem("rw_turned"), sem("rw_copied")
        turned, copied, logits, seq, picked = sem("turned"), sem("copied"), sem("logits"), sem("seq"), sem("picked")
        maxed, expd = sem("maxed"), sem("expd")
        w_turned, w_copied, mixed, added = sem("w_turned"), sem("w_copied"), sem("mixed"), sem("added")
        block = ctx.enter_context(nc.Block())

        @block.sync
        def _(sp):
            sp.dma_start(rw[:], router_w).then_inc(w_in, 16)
            sp.dma_start(eb[:], expert_b).then_inc(w_in, 16)
            sp.dma_start(rb[:], router_b.rearrange("(a e) -> a e", a=1).broadcast_to((P, E))).then_inc(w_in, 16)

        @block.tensor
        def _(pe):
            pe.wait_ge(w_in, 48)
            for c in range(DC):
                last = pe.transpose(t_ps[:, c, 0:E], rw[:, c * P:(c + 1) * P], ident[0:E, 0:E])
            last.then_inc(rw_turned, 1)

            def turn(t):
                if t == 0:
                    pe.wait_ge(rw_copied, 1)
                else:
                    pe.wait_ge(copied, t)
                for c in range(DC):
                    last = pe.transpose(t_ps[:, c, :], xn[:, t, c * P:(c + 1) * P], ident[:])
                last.then_inc(turned, 1)

            turn(0)
            for t in range(TT):
                pe.wait_ge(copied, t + 1)
                if t:
                    pe.wait_ge(picked, t)
                for c in range(DC):
                    last = pe.matmul(l_ps[:, 0:E], xT[:, t % 2, c, :], rwT[:, c, :], start=c == 0, stop=c == DC - 1)
                last.then_inc(logits, 1)
                if t + 1 < TT:
                    turn(t + 1)
                pe.wait_ge(picked, t + 1)
                if t:
                    pe.wait_ge(w_copied, t)
                pe.transpose(w_ps[0:E, 0:P], rest[:, t % 2, :], ident[:]).then_inc(w_turned, 1)
                pe.wait_ge(w_copied, t + 1)
                if t >= 2:
                    pe.wait_ge(added, t - 1)
                for n in range(2):
                    last = pe.matmul(m_ps[:, t % 2, n * 512:(n + 1) * 512], wT[:, t % 2, :],
                                     eb[:, n * 512:(n + 1) * 512], start=True, stop=True)
                last.then_inc(mixed, 1)

        @block.scalar
        def _(act):
            act.wait_ge(rw_turned, 1)
            act.activation(rwT[:], t_ps[:, :, 0:E], ACT.Copy).then_inc(rw_copied, 1)
            for t in range(TT):
                act.wait_ge(turned, t + 1)
                if t >= 2:
                    act.wait_ge(logits, t - 1)
                act.activation(xT[:, t % 2], t_ps[:], ACT.Copy).then_inc(copied, 1)
                act.wait_ge(maxed, t + 1)
                act.activation(ex[:, t % 2], lg[:, t % 2], ACT.Exp, bias=sm[:, t % 2, 1:2],
                               accum_out=sm[:, t % 2, 2:3]).then_inc(expd, 1)
                act.wait_ge(w_turned, t + 1)
                if t >= 2:
                    act.wait_ge(mixed, t - 1)
                act.activation(wT[:, t % 2, :], w_ps[0:E, 0:P], ACT.Copy).then_inc(w_copied, 1)

        @block.vector
        def _(dve):
            steps = [0]

            def after(ins):
                steps[0] += 1
                ins.then_inc(seq, 1)
                dve.wait_ge(seq, steps[0])

            dve.wait_ge(w_in, 48)
            for t in range(TT):
                s = t % 2
                col = [sm[:, s, k:k + 1] for k in range(6)]
                dve.wait_ge(logits, t + 1)
                after(dve.tensor_tensor_reduce(lg[:, s], l_ps[:, 0:E], rb[:], 1.0, NEG, ALU.add, ALU.max, col[0]))
                dve.tensor_scalar(col[1], col[0], -1.0, None, ALU.mult).then_inc(maxed, 1)
                dve.wait_ge(expd, t + 1)
                after(dve.reciprocal(col[3], col[2]))
                after(dve.tensor_scalar(ex[:, s], ex[:, s], col[3], None, ALU.mult))
                after(dve.max(top[:, s], ex[:, s]))
                if t >= 2:
                    dve.wait_ge(w_turned, t - 1)
                after(dve.match_replace(rest[:, s], top[:, s], ex[:, s], 0.0))
                after(dve.reduce_sum(col[4], top[:, s], AX.X))
                dve.tensor_tensor(rest[:, s], ex[:, s], rest[:, s], ALU.subtract).then_inc(picked, 1)
                after(dve.scalar_tensor_tensor(tmp[:], xn[:, t], col[4], X[:, t], ALU.mult, ALU.add))
                dve.wait_ge(mixed, t + 1)
                dve.tensor_tensor(X[:, t], m_ps[:, s], tmp[:], ALU.add).then_inc(added, 1)


def quantised_stage(nc, X, xn, ident_bf, context, scales):
    with ExitStack() as ctx:
        sb, ps, sem, event = make_tools(ctx, nc, "qn")
        par = sb("par", [P, 4], F32)
        k = sb("k", [P, 6], F32)
        rows = sb("rows", [P, 3, D], F32)
        work = sb("work", [P, 2, D], F32)
        qa = sb("qa", [P, 2, D], BF16)
        qaT = sb("qaT", [P, TT, DC, P], BF16)
        rowsum = sb("rowsum", [P, 2, TT], F32)
        qb = sb("qb", [P, B, KT, D], BF16)
        ones = sb("ones", [P, P], BF16)
        colsum = sb("colsum", [P, B, D], F32)
        tmp = sb("tmp", [P, 512], F32)
        t_ps = ps("t", [P, 2, DC, P], BF16)
        c_ps = ps("c", [P, D])
        acc = ps("acc", [P, 4, 512])
        par_in, k_ready, ones_made = sem("par_in"), sem("k_ready"), sem("ones_made")
        rows_in = [sem(f"rows_in{r}") for r in range(3)]
        seq, qa_done, qb_done, scaled = sem("seq"), sem("qa_done"), sem("qb_done"), sem("scaled")
        turned, copied, col_done, col_read, tiles, added = (
            sem("turned"), sem("copied"), sem("col_done"), sem("col_read"), sem("tiles"), sem("added"))
        block = ctx.enter_context(nc.Block())

        @block.sync
        def _(sp):
            for j, v in enumerate(scales):
                sp.dma_start(par[:, j:j + 1], v.rearrange("(a b) -> a b", a=1).broadcast_to((P, 1))).then_inc(par_in, 16)
            for n in range(B * KT):
                if n >= 3:
                    sp.wait_ge(scaled, TT + n - 2)
                sp.dma_start(rows[:, n % 3], context[n // KT, (n % KT) * P:(n % KT + 1) * P, :]).then_inc(rows_in[n % 3], 16)

        @block.scalar
        def _(act):
            act.wait_ge(k_ready, 1)
            for n in range(TT + B * KT):
                a = n < TT
                if n >= 2:
                    act.wait_ge(qa_done if n - 2 < TT else qb_done, n - 1 if n - 2 < TT else n - 1 - TT)
                if not a:
                    m = n - TT
                    act.wait_ge(rows_in[m % 3], 16 * (m // 3 + 1))
                src = xn[:, n] if a else rows[:, (n - TT) % 3]
                act.activation(work[:, n % 2], src, ACT.Identity, bias=par[:, 1:2] if a else par[:, 3:4],
                               scale=k[:, 0:1] if a else k[:, 1:2]).then_inc(scaled, 1)
                if a:
                    act.wait_ge(turned, n + 1)
                    act.activation(qaT[:, n], t_ps[:, n % 2], ACT.Copy).then_inc(copied, 1)

        @block.gpsimd
        def _(pool):
            pool.memset(ones[:], 1.0).then_inc(ones_made, 1)

        @block.vector
        def _(dve):
            steps = [0]

            def after(ins):
                steps[0] += 1
                ins.then_inc(seq, 1)
                dve.wait_ge(seq, steps[0])

            dve.wait_ge(par_in, 64)
            dve.reciprocal(k[:, 0:1], par[:, 0:1])
            dve.reciprocal(k[:, 1:2], par[:, 2:3])
            dve.tensor_scalar(k[:, 2:3], par[:, 1:2], -1.0, QMID, ALU.mult, ALU.add)
            dve.tensor_tensor(k[:, 4:5], par[:, 0:1], par[:, 2:3], ALU.mult)
            after(dve.tensor_scalar(k[:, 3:4], par[:, 3:4], -1.0, QMID, ALU.mult, ALU.add))
            dve.tensor_scalar(k[:, 5:6], k[:, 3:4], float(D), None, ALU.mult).then_inc(k_ready, 1)

            def quantise(n, out, done):
                dve.wait_ge(scaled, n + 1)
                after(dve.tensor_scalar(work[:, n % 2], work[:, n % 2], QMAX, 0.0, ALU.min, ALU.max))
                dve.tensor_scalar(out, work[:, n % 2], ROUND, ROUND + QMID, ALU.add, ALU.subtract).then_inc(done, 1)

            for t in range(TT):
                if t >= 2:
                    dve.wait_ge(turned, t - 1)
                quantise(t, qa[:, t % 2], qa_done)
                dve.wait_ge(qa_done, t + 1)
                last = dve.reduce_sum(rowsum[:, 0, t:t + 1], qa[:, t % 2], AX.X)
            after(last)
            after(dve.tensor_scalar(rowsum[:, 1], rowsum[:, 0], k[:, 3:4], None, ALU.mult))

            def finish(b):
                dve.wait_ge(col_done, b + 1)
                dve.tensor_scalar(colsum[:, b], c_ps[:], k[:, 5:6], k[:, 2:3], ALU.add, ALU.mult).then_inc(col_read, 1)
                dve.wait_ge(col_read, b + 1)
                for j in range(2 * QT):
                    n = b * 2 * QT + j
                    t, h = n // 2, n % 2
                    sl = slice(h * 512, (h + 1) * 512)
                    dve.wait_ge(tiles, n + 1)
                    after(dve.scalar_tensor_tensor(tmp[:], acc[:, n % 4], rowsum[:, 1, t:t + 1], colsum[:, b, sl], ALU.add, ALU.add))
                    after(dve.scalar_tensor_tensor(X[:, t, sl], tmp[:], k[:, 4:5], X[:, t, sl], ALU.mult, ALU.add))
                    dve.sem_inc(added, 1)

            for n in range(B * KT):
                quantise(TT + n, qb[:, n // KT, n % KT], qb_done)
            for b in range(B):
                finish(b)

        @block.tensor
        def _(pe):
            for t in range(TT):
                pe.wait_ge(qa_done, t + 1)
                if t >= 2:
                    pe.wait_ge(copied, t - 1)
                for c in range(DC):
                    last = pe.transpose(t_ps[:, t % 2, c, :], qa[:, t % 2, c * P:(c + 1) * P], ident_bf[:])
                last.then_inc(turned, 1)
            pe.wait_ge(copied, TT)
            pe.wait_ge(ones_made, 1)
            for b in range(B):
                pe.wait_ge(qb_done, (b + 1) * KT)
                if b:
                    pe.wait_ge(col_read, b)
                for h in range(2):
                    for c in range(KT):
                        last = pe.matmul(c_ps[:, h * 512:(h + 1) * 512], ones[:], qb[:, b, c, h * 512:(h + 1) * 512],
                                         start=c == 0, stop=c == KT - 1)
                last.then_inc(col_done, 1)
                for j in range(2 * QT):
                    n = b * 2 * QT + j
                    t, h = n // 2, n % 2
                    if n >= 4:
                        pe.wait_ge(added, n - 3)
                    for c in range(DC):
                        last = pe.matmul(acc[:, n % 4], qaT[:, t, c, :], qb[:, b, c, h * 512:(h + 1) * 512],
                                         start=c == 0, stop=c == DC - 1)
                    last.then_inc(tiles, 1)


def ffn_stage(nc, xT, X, ident, dq, dq3, ready, sharp, unit_src, unit_dst, rest_src, rest_dst):
    with ExitStack() as ctx:
        sb, ps, sem, event = tools = make_tools(ctx, nc, "ff")
        raw = sb("raw", [P, 3, D], F32)
        gu = [sb(f"gu{x}", [P, 2, 2, D], F32R) for x in ("h", "l")]
        dn = [sb(f"dn{x}", [P, 2, D], F32R) for x in ("h", "l")]
        act_s = sb("act_s", [P, 2, 512], F32)
        hid = sb("hid", [P, 2, 512], F32)
        hT = [sb(f"h{x}", [P, 2, T], F32R) for x in ("h", "l")]
        t_ps = ps("t", [P, 2, 512])
        g_ps = ps("g", [P, 2, 2, 512])
        y_ps = ps("y", [P, 2, 512])
        nf = Nf4(tools, sharp)
        PAIRS = HC // 2
        NT = TT * 2
        REST = HF - (HC - 1) * P
        w3v = dq3.rearrange("(c p) h -> p c h", p=P)
        raw_in = [sem(f"raw_in{j}") for j in range(3)]
        zeroed = sem("zeroed")
        turned = event("turned")
        w_hi = event("w_hi")
        w_lo = event("w_lo", 2)
        gated = event("gated", 4)
        silu = event("silu")
        gone = event("gone", 2)
        h_hi = event("h_hi")
        h_lo = event("h_lo", 2)
        tiles = event("tiles", NT)
        added = event("added", 2)
        block = ctx.enter_context(nc.Block())

        LEAD = 4

        def turn_no(m, x):
            return m * 6 + (LEAD + x)

        def turned_part(x):
            return (2, x) if x < 2 else ((x - 2) // 2, x % 2)

        UE = 6
        LOOPS = (HC - 1 - ready) * 2 // UE
        UNITS = LOOPS * UE

        def program(eng, body):
            with eng.Fori(0, LOOPS - 1) as i:
                for q in range(2):
                    body(2 * i + q, i, 3 * q, 3)
            for q in range(2):
                body(2 * (LOOPS - 1) + q, LOOPS - 1, 3 * q, 3)
            body(2 * LOOPS, LOOPS, 0, 1)
            for pr in range(2 * LOOPS + 1, PAIRS):
                body(pr, LOOPS, 0, 0)

        def after(i, e):
            return not (isinstance(i, int) and i == LOOPS)

        def is_rest(i, e):
            return isinstance(i, int) and i * UE + e == UNITS

        @block.sync
        def _(sp):
            def load_weight(m, j, start, count=None):
                rows = REST if isinstance(m, int) and m == HC - 1 else P
                if rows < P and j == 0:
                    sp.wait_ge(zeroed, 2)
                if count is not None:
                    sp.wait_ge(turned.sem, count)
                if j < 2:
                    sp.dma_start(raw[0:rows, j], dq[j][bass.ds(start, rows), :]).then_inc(raw_in[j], 16)
                else:
                    sp.dma_start(raw[:, j].rearrange("p (c h) -> p c h", h=P)[:, :, 0:rows],
                                 w3v[:, :, bass.ds(start, rows)]).then_inc(raw_in[j], 16)

            def load_unit(i, e):
                rest = is_rest(i, e)
                nf.load_sync(sp, i * UE + e, e % 2, rest_src if rest else [unit_src(i * 3 + (ready + e // 2), e % 2)])

            def store_unit(i, e):
                rest = is_rest(i, e)
                nf.store_sync(sp, i * UE + e, e % 2, rest_dst if rest else [unit_dst(i * 3 + (ready + e // 2), e % 2)])

            def body(pr, i, first, units):
                for x in range(3):
                    if x < 2:
                        m = pr * 2 + x
                        more = not (isinstance(m, int) and m == HC - 1)
                        start = (m + 1) * P if isinstance(m, int) else (i * 4 + (2 * (first // 3) + x + 1)) * P
                        if more:
                            load_weight(m + 1, 0, (m + 1) * P, m * 6 + 2)
                            load_weight(m + 1, 1, (m + 1) * P, m * 6 + 4)
                    if x < units and after(i, first + x):
                        load_unit(i, first + x + 1)
                    if x < 2 and more:
                        load_weight(m + 1, 2, start, m * 6 + 6)
                    if x < units:
                        store_unit(i, first + x)

            nf.open_sync(sp)
            for j in range(3):
                load_weight(0, j, 0)
            load_unit(0, 0)
            program(sp, body)
            nf.close_sync(sp, [UNITS // 2 + 2, UNITS // 2])

        @block.gpsimd
        def _(pool):
            def body(pr, i, first, units):
                for x in range(units):
                    n = i * UE + (first + x)
                    if after(i, first + x):
                        nf.norm_gpsimd(pool, n + 1, (first + x + 1) % 2)
                    nf.finish_gpsimd(pool, n, (first + x) % 2)

            nf.open_gpsimd(pool)
            nf.norm_gpsimd(pool, 0, 0)
            program(pool, body)
            pool.wait_ge(turned.sem, (HC - 2) * 6 + 4)
            pool.memset(raw[REST:P, 0:2], 0.0).then_inc(zeroed, 1)
            pool.wait_ge(turned.sem, (HC - 2) * 6 + 6)
            pool.wait_ge(zeroed, 1)
            pool.memset(raw[:, 2], 0.0).then_inc(zeroed, 1)

        @block.tensor
        def _(pe):
            def turn(m, x):
                u = turn_no(m, x)
                j, k = turned_part(x)
                if k == 0:
                    pe.wait_ge(raw_in[j], (m if j == 2 else m + 1) * 16 + 16)
                pe.wait_ge(w_lo.sem, w_lo.free(u, 2))
                for c in range(4):
                    o = (4 * k + c) * P
                    last = pe.transpose(t_ps[:, k, c * P:(c + 1) * P], raw[:, j, o:o + P], ident[:])
                last.then_inc(turned.sem, 1)

            TURNS = [(0, 1), (None, 2), (3, 4), (5, None)]

            def gate_up(m, s):
                more = not (isinstance(m, int) and m == HC - 1)
                for tile in range(4):
                    j, u = tile // 2, tile % 2
                    if j == 0:
                        pe.wait_ge(w_lo.sem, m * 6 + (2 * (u + 1) + 2))
                    if u == 0:
                        pe.wait_ge(gone.sem, gone.free(m * 2 + j, 2))
                    for c in range(DC):
                        last = split_matmul(pe, g_ps[:, j, u], [x[:, s, u, c * P:(c + 1) * P] for x in gu],
                                            [x[:, c, j * 512:(j + 1) * 512] for x in xT], c == 0, c == DC - 1)
                        if c == DC - 1:
                            last.then_inc(gated.sem, 1)
                        if c in (DC // 2 - 1, DC - 1):
                            x = TURNS[tile][c == DC - 1]
                            if x is not None and (x < 2 or more):
                                turn(m, x)

            def down(pr):
                for k in range(NT):
                    t, n = k // 2, k % 2
                    if k == 0:
                        pe.wait_ge(w_lo.sem, w_lo.done(turn_no(pr * 2 + 1, 1)))
                    if k % (NT // 2) == 0:
                        pe.wait_ge(h_lo.sem, h_lo.done(pr * 4 + (2 + k // (NT // 2))))
                    pe.wait_ge(added.sem, added.free(pr * NT + k, 2))
                    for s in range(2):
                        last = split_matmul(pe, y_ps[:, k % 2], [x[:, s, t * P:(t + 1) * P] for x in hT],
                                            [x[:, s, n * 512:(n + 1) * 512] for x in dn], s == 0, s == 1)
                    last.then_inc(tiles.sem, 1)

            def body(pr, i, first, units):
                for s in range(2):
                    gate_up(pr * 2 + s, s)
                down(pr)

            gated.open(pe)
            tiles.open(pe)
            for x in range(2, 6):
                turn(-1, x)
            program(pe, body)

        def destination(x, s):
            j, k = turned_part(x)
            sl = slice(k * 512, (k + 1) * 512)
            return [d[:, s, sl] for d in dn] if j == 2 else [g[:, 1 - s, j, sl] for g in gu]

        @block.scalar
        def _(act):
            def high(m, s, x):
                act.wait_ge(turned.sem, turned.done(turn_no(m, x)))
                act.activation(destination(x, s)[0], t_ps[:, x % 2], ACT.Copy).then_inc(w_hi.sem, 1)

            def gate(m, j):
                act.wait_ge(gated.sem, gated.done(m * 4 + 2 * j))
                act.wait_ge(gone.sem, gone.free(m * 2 + j, 2))
                act.activation(act_s[:, j], g_ps[:, j, 0], ACT.Silu).then_inc(silu.sem, 1)

            def hidden(m, s, j):
                act.wait_ge(gone.sem, gone.done(m * 2 + j))
                act.activation(hT[0][:, s, j * 512:(j + 1) * 512], hid[:, j], ACT.Copy).then_inc(h_hi.sem, 1)

            def body(pr, i, first, units):
                for s in range(3):
                    n, slot = i * UE + (first + s), (first + s) % 2
                    if s == 2:
                        if s < units:
                            nf.above_scalar(act, n, slot, range(NS4))
                        continue
                    m = pr * 2 + s
                    more = not (isinstance(m, int) and m == HC - 1)
                    if s == 0:
                        act.wait_ge(tiles.sem, tiles.free(pr * NT + (NT - 1), NT))
                    for p in range(8):
                        if p == 2:
                            act.wait_ge(gated.sem, gated.free(m * 4 + 3, 4))
                        if p in (2, 5):
                            gate(m, p // 5)
                        if p == 3:
                            hidden(m, s, 0)
                        x = (0, 1, 2, None, 3, None, 4, 5)[p]
                        if x is not None and (x < 2 or more):
                            high(m, s, x)
                        if s < units:
                            nf.above_scalar(act, n, slot, share(NS4, p, 8))
                    hidden(m, s, 1)

            for x in range(2, 6):
                high(-1, 1, x)
            program(act, body)

        @block.vector
        def _(dve):
            def low(m, s, x):
                u = turn_no(m, x)
                hi, lo = destination(x, s)
                dve.wait_ge(w_hi.sem, w_hi.done(u))
                dve.tensor_tensor(lo, t_ps[:, x % 2], f32(hi), ALU.subtract).then_inc(w_lo.sem, 1)

            def product(m, j):
                a = m * 2 + j
                dve.wait_ge(gated.sem, gated.done(m * 4 + (2 * j + 1)))
                dve.wait_ge(silu.sem, silu.done(a))
                dve.wait_ge(h_lo.sem, h_lo.free(a, 2))
                dve.tensor_tensor(hid[:, j], g_ps[:, j, 1], act_s[:, j], ALU.mult).then_inc(gone.sem, 1)

            def hidden_low(m, s, j):
                dve.wait_ge(h_hi.sem, h_hi.done(m * 2 + j))
                sl = (slice(None), s, slice(j * 512, (j + 1) * 512))
                dve.tensor_tensor(hT[1][sl], hid[:, j], f32(hT[0][sl]), ALU.subtract).then_inc(h_lo.sem, 1)

            def max_next(i, e):
                if after(i, e):
                    parts = 2 if is_rest(i, e + 1) else 1
                    nf.max_vector(dve, i * UE + (e + 1), (e + 1) % 2, i * 3 + (e + 1) // 2, parts=parts)

            def body(pr, i, first, units):
                for s in range(3):
                    e = first + s
                    n, slot, before = i * UE + e, e % 2, i * 3 + e // 2

                    def steps(which):
                        if s < units:
                            nf.step_vector(dve, n, slot, which, before)

                    if s == 2:
                        for k in range(NT):
                            t, h = k // 2, k % 2
                            sl = slice(h * 512, (h + 1) * 512)
                            dve.wait_ge(tiles.sem, tiles.done(pr * NT + k))
                            dve.tensor_tensor(X[:, t, sl], y_ps[:, k % 2], X[:, t, sl], ALU.add).then_inc(added.sem, 1)
                            steps(share(NS4, k, NT))
                            if s < units and k == NT // 2:
                                max_next(i, e)
                        continue
                    m = pr * 2 + s
                    more = not (isinstance(m, int) and m == HC - 1)
                    for p in range(8):
                        if p == 3:
                            product(m, 0)
                        x = (0, 1, 2, None, 3, None, 4, 5)[p]
                        if x is not None and (x < 2 or more):
                            low(m, s, x)
                        if p == 5 and s < units:
                            max_next(i, e)
                        if p == 7:
                            product(m, 1)
                        steps(share(NS4, p, 8))
                        if p == 3:
                            hidden_low(m, s, 0)
                    hidden_low(m, s, 1)

            w_lo.open(dve)
            gone.open(dve)
            h_lo.open(dve)
            added.open(dve)
            nf.open_vector(dve)
            for x in range(2, 6):
                low(-1, 1, x)
            nf.max_vector(dve, 0, 0, 0)
            program(dve, body)


def store_stage(nc, X, out):
    with ExitStack() as ctx:
        stored = ctx.enter_context(nc.semaphore("out_stored"))
        block = ctx.enter_context(nc.Block())

        @block.sync
        def _(sp):
            sp.dma_start(out.rearrange("b (t p) d -> p (b t) d", p=P), X[:]).then_inc(stored, 16)
            sp.wait_ge(stored, 16)


def build(nc, x, context, mask, wq, wk, wv, wo, router_w, router_b, expert_b, s1, z1, s2, z2,
          w1, w2, w3, cos_q, sin_q, cos_k, sin_k, out):
    def scratch(name, shape):
        return nc.dram_tensor(name, shape, F32, kind="Internal").ap()

    q_d = scratch("q_d", (HQ, DH, T))
    k_d = scratch("k_d", (B, HKV, DH, SK))
    v_d = scratch("v_d", (B, KT, P, D))
    o_d = scratch("o_d", (HQ, DH, T))
    dq = [scratch(f"dq{j + 1}", (HF, D)) for j in range(2)]
    dq3 = scratch("dq3", (D, HF))

    w = [w1, w2]
    w3_rows, dq3_rows = [a.rearrange("d h -> (d h)").rearrange("(r n) -> r n", n=D) for a in (w3, dq3)]
    WHOLE = HF // P

    def unit(a, k):
        return a[bass.ds(k * P, P), :]

    def rest(a):
        return a[WHOLE * P:, :].rearrange("r (a n) -> (r a) n", a=2)

    PQ, PK, PO = HQ // 2, HKV // 2, HQ // GRP // 2
    w3_left = range(PQ + PK, WHOLE)
    assert len(w3_left) == 1
    first_k, first_v, first_o, ready = 1, 1, 1 + PK, 1 + PK + PO
    units_v = [
        [([unit(w3_rows, k)], [unit(dq3_rows, k)], D) for k in w3_left]
        + [([rest(w3_rows)], [rest(dq3_rows)], D // 2)]
        + [([unit(w[j], 0)], [unit(dq[j], 0)], D) for j in range(2)],
        [([unit(w2, first_v + k)], [unit(dq[1], first_v + k)], D) for k in range(PK)]]
    units_k = [
        (lambda k: unit(w3_rows, k + PQ), lambda k: unit(dq3_rows, k + PQ)),
        (lambda k: unit(w1, k + first_k), lambda k: unit(dq[0], k + first_k))]

    spent.clear()
    with ExitStack() as ctx:
        X = ctx.enter_context(nc.sbuf_tensor("X", [P, TT, D], F32))
        ident = ctx.enter_context(nc.sbuf_tensor("ident", [P, P], F32))
        ident_bf = ctx.enter_context(nc.sbuf_tensor("ident_bf", [P, P], BF16))
        sharp = ctx.enter_context(nc.sbuf_tensor("sharp", [P, NS4], F32))
        load_stage(nc, x, X, ident, ident_bf, sharp)
        with ExitStack() as c:
            xT = [c.enter_context(nc.sbuf_tensor(f"xT_{n}", [P, DC, T], F32R)) for n in ("h", "l")]
            norm_stage(nc, "n0", X, ident, xT=xT)
            project_stage(nc, "pq", xT, wq, HQ, lambda h: q_d[bass.ds(h, 1)].rearrange("a p n -> p (a n)"),
                          cos_q, sin_q, [(0, 512), (0, 512)], sharp,
                          lambda k: unit(w3_rows, k), lambda k: unit(dq3_rows, k))
        with ExitStack() as c:
            cT = [c.enter_context(nc.sbuf_tensor(f"cT_{n}", [P, DC, SK], F32R)) for n in ("h", "l")]
            for b in range(B):
                context_stage(nc, f"c{b}", context[b], ident, cT)
                project_stage(nc, f"pk{b}", cT, wk, HKV, lambda h: k_d[b, bass.ds(h, 1)].rearrange("a p n -> p (a n)"),
                              cos_k, sin_k, [(0, 512), (512, 1024)], sharp, *units_k[b])
                value_stage(nc, f"v{b}", cT, wv, lambda t, h: v_d[b, t, :, h * 512:(h + 1) * 512], sharp, units_v[b])
        clear_stage(nc)
        attention_stage(nc, q_d, k_d, v_d, o_d, mask, ident)
        output_stage(nc, o_d, wo, X, sharp, lambda k, j: unit(w[j], k + first_o), lambda k, j: unit(dq[j], k + first_o))
        with ExitStack() as c:
            xn = c.enter_context(nc.sbuf_tensor("xn", [P, TT, D], F32))
            norm_stage(nc, "n1", X, ident, xn_all=xn)
            router_stage(nc, X, xn, ident, router_w, router_b, expert_b)
            norm_stage(nc, "n2", X, ident, xn_all=xn)
            quantised_stage(nc, X, xn, ident_bf, context, (s1, z1, s2, z2))
        clear_stage(nc)
        with ExitStack() as c:
            xT = [c.enter_context(nc.sbuf_tensor(f"yT_{n}", [P, DC, T], F32R)) for n in ("h", "l")]
            norm_stage(nc, "n3", X, ident, xT=xT)
            ffn_stage(nc, xT, X, ident, dq, dq3, ready, sharp, lambda k, j: unit(w[j], k), lambda k, j: unit(dq[j], k),
                      [rest(a) for a in w], [rest(a) for a in dq])
        store_stage(nc, X, out)


_INS = ["x", "ctx_4096", "mask_BxSxS2_ff0", "L0_xattn_wq", "L0_xattn_wk", "L0_xattn_wv", "L0_xattn_wo",
        "L0_ffn_router_weight", "L0_ffn_router_bias", "L0_ffn_expert_bias", "L1_xattn_x1_scale",
        "L1_xattn_x1_zp", "L1_xattn_x2_scale", "L1_xattn_x2_zp", "L1_ffn_w1", "L1_ffn_w2", "L1_ffn_w3"]


def rotary_tables():
    inv = np.float32(1.0) / np.float32(10000.0) ** (np.arange(0, DH, 2, dtype=np.float32) / np.float32(DH))
    ang = inv[:, None] * np.arange(SK, dtype=np.float32)[None, :]
    cos = np.concatenate([np.cos(ang)] * 2).astype(np.float32)
    sin = np.concatenate([np.sin(ang), -np.sin(ang)]).astype(np.float32)
    scale = np.float64(DH) ** -0.5
    return ((cos[:, :SQ] * scale).astype(np.float32), (sin[:, :SQ] * scale).astype(np.float32), cos, sin)


def kernel(**inputs):
    import concourse.bacc as bacc
    from concourse.bass_utils import run_bass_kernel_spmd

    nc = bacc.Bacc("TRN2", target_bir_lowering=False, num_devices=1)
    arrays = {n: np.ascontiguousarray(inputs[n]) for n in _INS}
    arrays.update(zip(("cos_q", "sin_q", "cos_k", "sin_k"), rotary_tables()))
    args = [nc.dram_tensor(f"in_{n}", a.shape, mybir.dt.from_np(a.dtype), kind="ExternalInput").ap()
            for n, a in arrays.items()]
    out = nc.dram_tensor("out_x", (B, SQ, D), F32, kind="ExternalOutput").ap()
    build(nc, *args, out)
    r = run_bass_kernel_spmd(nc, [{f"in_{n}": a for n, a in arrays.items()}], core_ids=[0])
    return r.results[0]["out_x"]
```

```python
from contextlib import ExitStack

import numpy as np
import concourse.bass as bass
from concourse import mybir
from concourse.alu_op_type import AluOpType as ALU

F32 = mybir.dt.float32
F32R = mybir.dt.float32r
BF16 = mybir.dt.bfloat16
ACT = mybir.ActivationFunctionType
AX = mybir.AxisListType

P = 128
B, SQ, SK, D = 2, 512, 1024, 1024
T = B * SQ
TT = T // P
DC = D // P
HQ, HKV, DH = 32, 8, 128
GRP = HQ // HKV
KT = SK // P
QT = SQ // P
E, TOPK = 64, 8
HF = 2752
HC = -(-HF // P)
BLK = 64
EPS = 1e-5
ROUND = 1.5 * 2.0 ** 23
QMAX = 255.0
QMID = 128.0
NEG = -3.0e38

CODE = np.array([-1.0, -0.6961928009986877, -0.5250730514526367, -0.39491748809814453,
                 -0.28444138169288635, -0.18477343022823334, -0.09105003625154495, 0.0,
                 0.07958029955625534, 0.16093020141124725, 0.24611230194568634,
                 0.33791524171829224, 0.44070982933044434, 0.5626170039176941,
                 0.7229568362236023, 1.0], np.float32)
BOUNDS = (CODE[:-1] + CODE[1:]) * np.float32(0.5)


def exact_step(a, b):
    d = np.float32(b - a)
    for c in (d, np.nextafter(d, np.float32(9)), np.nextafter(d, np.float32(-9))):
        if np.float32(a + c) == b:
            return float(c)
    raise AssertionError


STEPS = [exact_step(a, b) for a, b in zip(CODE[:-1], CODE[1:])]
NS4 = len(STEPS)
SHARP = 2.0 ** 40


spent = []


class Event:

    def __init__(self, ctx, nc, name, spare=0):
        self.sem = ctx.enter_context(nc.semaphore(name))
        spent.append(self.sem)
        self.spare = spare

    def open(self, eng):
        eng.sem_inc(self.sem, self.spare)

    def done(self, n):
        return n + 1 + self.spare

    def free(self, n, ring):
        return n + 1 - ring + self.spare


def make_tools(ctx, nc, tag):
    def sb(name, shape, dt):
        return ctx.enter_context(nc.sbuf_tensor(f"{tag}_{name}", shape, dt))

    def ps(name, shape, dt=F32):
        return ctx.enter_context(nc.psum_tensor(f"{tag}_{name}", shape, dt))

    def sem(name):
        spent.append(ctx.enter_context(nc.semaphore(f"{tag}_{name}")))
        return spent[-1]

    def event(name, spare=0):
        return Event(ctx, nc, f"{tag}_{name}", spare)

    return sb, ps, sem, event


def f32(ap):
    return ap.bitcast(F32)


def split_matmul(pe, out, w, x, start, stop):
    pe.matmul(out, w[0], x[0], start=start, stop=False)
    pe.matmul(out, w[0], x[1], start=False, stop=False)
    return pe.matmul(out, w[1], x[0], start=False, stop=stop)


class Nf4:
    NB = D // BLK

    def __init__(self, tools, sharp):
        sb, _, sem, event = tools
        self.sharp = sharp
        self.raw = sb("nf_raw", [P, 2, D], F32)
        self.above = sb("nf_above", [P, 2, D], F32)
        self.val = sb("nf_val", [P, 2, D], F32)
        self.am = sb("nf_am", [P, 2, 3, self.NB], F32)
        self.loaded = [sem("nf_loaded0"), sem("nf_loaded1")]
        self.stored = [sem("nf_stored0"), sem("nf_stored1")]
        self.seq = event("nf_seq")
        self.maxed = event("nf_maxed")
        self.normed = event("nf_normed")
        self.above_done = event("nf_above_done")
        self.stepped = event("nf_stepped", 2 * NS4)
        self.finished = event("nf_finished", 2)

    def blocks(self, ap, width):
        return ap[:, 0:width].rearrange("p (n b) -> p n b", b=BLK)

    def open_sync(self, sp):
        for s in range(2):
            sp.sem_inc(self.stored[s], 16)

    def open_vector(self, dve):
        self.stepped.open(dve)

    def open_gpsimd(self, pool):
        self.finished.open(pool)

    def load_sync(self, sp, n, s, parts, width=D):
        sp.wait_ge(self.finished.sem, self.finished.free(n, 2))
        w = width // len(parts)
        for k, part in enumerate(parts):
            sp.dma_start(self.raw[:, s, k * w:(k + 1) * w], part).then_inc(self.loaded[s], 16)

    def store_sync(self, sp, n, s, parts, width=D):
        sp.wait_ge(self.finished.sem, self.finished.done(n))
        w = width // len(parts)
        for k, part in enumerate(parts):
            sp.dma_start(part, self.val[:, s, k * w:(k + 1) * w]).then_inc(self.stored[s], 16)

    def close_sync(self, sp, counts):
        for s in range(2):
            sp.wait_ge(self.stored[s], 16 * (counts[s] + 1))

    def max_vector(self, dve, n, s, before, width=D, parts=1):
        am = self.am
        dve.wait_ge(self.finished.sem, self.finished.free(n, 2))
        dve.wait_ge(self.loaded[s], before * 16 + 16 * parts)
        dve.tensor_reduce(am[:, s, 0, 0:width // BLK], self.blocks(self.raw[:, s], width), AX.X, ALU.max,
                          apply_absolute_value=True).then_inc(self.seq.sem, 1)
        dve.wait_ge(self.seq.sem, self.seq.done(2 * n))
        w = slice(0, width // BLK)
        dve.scalar_tensor_tensor(am[:, s, 1, w], am[:, s, 0, w], 0.0, am[:, s, 0, w], ALU.is_equal, ALU.add).then_inc(self.seq.sem, 1)
        dve.wait_ge(self.seq.sem, self.seq.done(2 * n + 1))
        dve.reciprocal(am[:, s, 2, w], am[:, s, 1, w]).then_inc(self.maxed.sem, 1)

    def norm_gpsimd(self, pool, n, s, width=D):
        pool.wait_ge(self.maxed.sem, self.maxed.done(n))
        raw = self.blocks(self.raw[:, s], width)
        pool.tensor_tensor(raw, raw, self.am[:, s, 2, 0:width // BLK].unsqueeze(2).broadcast_to((P, width // BLK, BLK)),
                           ALU.mult).then_inc(self.normed.sem, 1)

    def above_scalar(self, act, n, s, steps, width=D):
        for j in steps:
            if j == 0:
                act.wait_ge(self.normed.sem, self.normed.done(n))
            act.wait_ge(self.stepped.sem, n * NS4 + (j - 1 + 2 * NS4))
            act.activation(self.above[:, (s + j) % 2, 0:width], self.raw[:, s, 0:width], ACT.Relu,
                           bias=self.sharp[:, j:j + 1], scale=SHARP).then_inc(self.above_done.sem, 1)

    def step_vector(self, dve, n, s, steps, before, width=D):
        for j in steps:
            v = self.val[:, s, 0:width]
            above = self.above[:, (s + j) % 2, 0:width]
            dve.wait_ge(self.above_done.sem, n * NS4 + (j + 1))
            if j == 0:
                dve.wait_ge(self.stored[s], before * 16 + 16)
                dve.tensor_scalar(v, above, STEPS[0], float(CODE[0]), ALU.min, ALU.add).then_inc(self.stepped.sem, 1)
            else:
                dve.wait_ge(self.stepped.sem, n * NS4 + (j + 2 * NS4))
                dve.scalar_tensor_tensor(v, above, STEPS[j], v, ALU.min, ALU.add).then_inc(self.stepped.sem, 1)

    def finish_gpsimd(self, pool, n, s, width=D):
        pool.wait_ge(self.stepped.sem, n * NS4 + 3 * NS4)
        v = self.blocks(self.val[:, s], width)
        pool.tensor_tensor(v, v, self.am[:, s, 0, 0:width // BLK].unsqueeze(2).broadcast_to((P, width // BLK, BLK)),
                           ALU.mult).then_inc(self.finished.sem, 1)


def share(total, k, n):
    return range(total * k // n, total * (k + 1) // n)


def clear_stage(nc):
    with nc.Block() as block:
        @block.sync
        def _(sp):
            for s in spent:
                sp.sem_clear(s)
    spent.clear()


def constants_stage(nc, ident, ident_bf, sharp):
    with ExitStack() as ctx:
        sb, ps, sem, event = make_tools(ctx, nc, "ld")
        zeroed, made = sem("zeroed"), sem("made")
        block = ctx.enter_context(nc.Block())

        @block.gpsimd
        def _(pool):
            for j in range(NS4):
                pool.memset(sharp[:, j:j + 1], -SHARP * float(BOUNDS[j]))
            pool.memset(ident[:], 0.0).then_inc(zeroed, 1)
            pool.wait_ge(zeroed, 1)
            pool.affine_select(out=ident[:], in_=ident[:], compare_op=ALU.not_equal, fill=1.0,
                               base=0, pattern=[[-1, P]], channel_multiplier=1).then_inc(made, 1)
            pool.wait_ge(made, 1)
            pool.tensor_copy(ident_bf[:], ident[:]).then_inc(made, 1)


def norm_stage(nc, tag, X, ident, xT=None, xn_all=None, x=None):
    with ExitStack() as ctx:
        sb, ps, sem, event = make_tools(ctx, nc, tag)
        st = sb("st", [P, TT, 2, 6], F32)
        mv = sb("mv", [P, TT, 2], F32)
        s = sb("s", [P, 5, TT], F32)
        xn = xn_all if xn_all is not None else sb("xn", [P, 2, D], F32)
        slots = TT if xn_all is not None else 2
        seq, var_ready, root_ready, normed = sem("seq"), sem("var"), sem("root"), sem("normed")
        turned, hi_out, lo_out = sem("turned"), sem("hi"), sem("lo")
        x_in = [sem(f"x_in{t}") for t in range(TT)] if x is not None else None
        if xT is not None:
            tp = ps("tp", [P, 2, DC, P])
        block = ctx.enter_context(nc.Block())

        if x is not None:
            @block.sync
            def _(sp):
                tiles = x.rearrange("b (t p) d -> (b t) p d", p=P)
                for t in range(TT):
                    sp.dma_start(X[:, t, :], tiles[t]).then_inc(x_in[t], 16)

        @block.scalar
        def _(act):
            act.wait_ge(var_ready, 1)
            act.activation(s[:, 1, :], s[:, 0, :], ACT.Sqrt).then_inc(root_ready, 1)
            if xT is not None:
                for t in range(TT):
                    act.wait_ge(turned, t + 1)
                    act.activation(xT[0][:, :, t * P:(t + 1) * P], tp[:, t % 2], ACT.Copy).then_inc(hi_out, 1)

        @block.vector
        def _(dve):
            steps = [0]

            def after(ins):
                steps[0] += 1
                ins.then_inc(seq, 1)
                dve.wait_ge(seq, steps[0])

            for t in range(TT):
                if x is not None:
                    dve.wait_ge(x_in[t], 16)
                for h in range(2):
                    last = dve.bn_stats(st[:, t, h, :], X[:, t, h * 512:(h + 1) * 512])
            after(last)
            for t in range(TT):
                last = dve.bn_aggr(mv[:, t, :], st[:, t, :, :].rearrange("p a b -> p (a b)"))
            after(last)
            dve.tensor_scalar(s[:, 0, :], mv[:, :, 1], EPS, None, ALU.add).then_inc(var_ready, 1)
            dve.wait_ge(root_ready, 1)
            after(dve.reciprocal(s[:, 2, :], s[:, 1, :]))
            after(dve.tensor_tensor(s[:, 3, :], s[:, 0, :], s[:, 2, :], ALU.mult))
            after(dve.tensor_tensor(s[:, 3, :], s[:, 3, :], s[:, 1, :], ALU.add))
            after(dve.tensor_scalar(s[:, 2, :], s[:, 3, :], 0.5, None, ALU.mult))
            after(dve.reciprocal(s[:, 4, :], s[:, 2, :]))

            def norm(t):
                if xT is not None and t >= 2:
                    dve.wait_ge(turned, t - 1)
                dve.tensor_scalar(xn[:, t % slots, :], X[:, t, :], mv[:, t, 0:1], s[:, 4, t:t + 1],
                                  ALU.subtract, ALU.mult).then_inc(normed, 1)

            def low(t):
                dve.wait_ge(hi_out, t + 1)
                sl = slice(t * P, (t + 1) * P)
                dve.tensor_tensor(xT[1][:, :, sl], tp[:, t % 2], f32(xT[0][:, :, sl]), ALU.subtract).then_inc(lo_out, 1)

            norm(0)
            for t in range(TT):
                if t + 1 < TT:
                    norm(t + 1)
                if xT is not None:
                    low(t)

        if xT is not None:
            @block.tensor
            def _(pe):
                for t in range(TT):
                    pe.wait_ge(normed, t + 1)
                    if t >= 2:
                        pe.wait_ge(lo_out, t - 1)
                    for c in range(DC):
                        last = pe.transpose(tp[:, t % 2, c, :], xn[:, t % 2, c * P:(c + 1) * P], ident[:])
                    last.then_inc(turned, 1)


def project_stage(nc, tag, xT, w, heads, store, cos_d, sin_d, rows, sharp, unit_src, unit_dst):
    with ExitStack() as ctx:
        sb, ps, sem, event = tools = make_tools(ctx, nc, tag)
        width = max(stop for _, stop in rows)
        cos = sb("cos", [P, width], F32)
        sin = sb("sin", [P, width], F32)
        raw = sb("raw", [P, 2, DC, DH], F32)
        wh = sb("wh", [P, 2, DC, DH], F32R)
        wl = sb("wl", [P, 2, DC, DH], F32R)
        ta = sb("ta", [P, 2, 512], F32)
        tb = sb("tb", [P, 2, 512], F32)
        res = sb("res", [P, 2, 1024], F32)
        pj = ps("pj", [P, 2, 2, 512])
        nf = Nf4(tools, sharp)
        tab_in = sem("tab_in")
        raw_in = [sem("raw_in0"), sem("raw_in1")]
        stored = [sem("stored0"), sem("stored1")]
        hi_out = event("hi")
        lo_out = event("lo", 2)
        tiles = event("tiles", 4)
        copied = event("copied")
        read = event("read", 4)
        scaled = event("scaled")
        summed = event("summed", 2)
        wv_ = w.rearrange("(c p) n -> p c n", p=P)
        block = ctx.enter_context(nc.Block())
        PASSES = heads // 2

        def program(eng, body):
            with eng.Fori(0, PASSES // 2 - 1) as i:
                for u in range(2):
                    body(2 * i + u, u, i, False)
            for u in range(2):
                body(PASSES - 2 + u, u, PASSES // 2 - 1, u == 1)

        @block.sync
        def _(sp):
            def load_head(h, s):
                sp.wait_ge(lo_out.sem, lo_out.free(h, 2))
                sp.dma_start(raw[:, s], wv_[:, :, bass.ds(h * DH, DH)]).then_inc(raw_in[s], 16)

            def store_head(i, s):
                sp.wait_ge(summed.sem, summed.done(4 * i + 2 * s + 1))
                sp.dma_start(store(2 * i + s), res[:, s, :]).then_inc(stored[s], 16)

            def body(i, u, _, last):
                if not last:
                    load_head(2 * i + 2, 0)
                    nf.load_sync(sp, i + 1, 1 - u, [unit_src(i + 1)])
                    load_head(2 * i + 3, 1)
                for s in range(2):
                    store_head(i, s)
                nf.store_sync(sp, i, u, [unit_dst(i)])

            for s in range(2):
                sp.sem_inc(stored[s], 16)
            nf.open_sync(sp)
            lo_out.open(sp)
            load_head(0, 0)
            nf.load_sync(sp, 0, 0, [unit_src(0)])
            sp.dma_start(cos[:], cos_d).then_inc(tab_in, 16)
            sp.dma_start(sin[:], sin_d).then_inc(tab_in, 16)
            load_head(1, 1)
            program(sp, body)
            for s in range(2):
                sp.wait_ge(stored[s], 16 * (PASSES + 1))
            nf.close_sync(sp, [PASSES // 2] * 2)

        @block.scalar
        def _(act):
            def high(i, s):
                act.wait_ge(raw_in[s], i * 16 + 16)
                act.wait_ge(tiles.sem, tiles.free(4 * i + 2 * s + 1, 4))
                act.activation(wh[:, s], raw[:, s], ACT.Copy).then_inc(hi_out.sem, 1)

            def copy(i, s, j):
                n = 4 * i + 2 * s + j
                act.wait_ge(tiles.sem, tiles.done(n))
                act.wait_ge(summed.sem, summed.free(n, 2))
                act.activation(ta[:, j], pj[:, s, j, :], ACT.Copy).then_inc(copied.sem, 1)

            def body(i, u, _, last):
                high(i, 1)
                for s in range(2):
                    if s and not last:
                        high(i + 1, 0)
                    for j in range(2):
                        nf.above_scalar(act, i, u, share(NS4, 2 * s + j, 4))
                        copy(i, s, j)

            high(0, 0)
            program(act, body)

        @block.vector
        def _(dve):
            def rotate(i, s, j):
                n = 4 * i + 2 * s + j
                a, b = rows[j]
                src = pj[:, s, j, :]
                dve.wait_ge(copied.sem, copied.done(n))
                dve.wait_ge(summed.sem, summed.free(n, 2))
                dve.tensor_tensor(tb[0:64, j], src[64:128], sin[64:128, a:b], ALU.mult)
                dve.tensor_tensor(tb[64:128, j], src[0:64], sin[0:64, a:b], ALU.mult).then_inc(read.sem, 1)

            def body(i, u, before, last):
                for s in range(2):
                    for j in range(2):
                        nf.step_vector(dve, i, u, share(NS4, 2 * s + j, 4), before)
                        rotate(i, s, j)
                        if s == 0 and j == 1 and not last:
                            nf.max_vector(dve, i + 1, 1 - u, before + u)

            read.open(dve)
            nf.open_vector(dve)
            nf.max_vector(dve, 0, 0, 0)
            dve.wait_ge(tab_in, 32)
            program(dve, body)

        @block.gpsimd
        def _(pool):
            def low(i, s):
                pool.wait_ge(hi_out.sem, hi_out.done(2 * i + s))
                pool.tensor_tensor(wl[:, s], raw[:, s], f32(wh[:, s]), ALU.subtract).then_inc(lo_out.sem, 1)

            def body(i, u, before, last):
                for s in range(2):
                    if s == 0:
                        low(i, 1)
                    elif not last:
                        low(i + 1, 0)
                    for j in range(2):
                        n = 4 * i + 2 * s + j
                        if j == 0:
                            pool.wait_ge(stored[s], i * 16 + 16)
                        a, b = rows[j]
                        pool.wait_ge(copied.sem, copied.done(n))
                        pool.tensor_tensor(ta[:, j], ta[:, j], cos[:, a:b], ALU.mult).then_inc(scaled.sem, 1)
                        pool.wait_ge(scaled.sem, scaled.done(n))
                        pool.wait_ge(read.sem, read.done(n))
                        pool.tensor_tensor(res[:, s, j * 512:(j + 1) * 512], ta[:, j], tb[:, j],
                                           ALU.add).then_inc(summed.sem, 1)
                        if s == 0 and j == 1 and not last:
                            nf.norm_gpsimd(pool, i + 1, 1 - u)
                nf.finish_gpsimd(pool, i, u)

            summed.open(pool)
            nf.open_gpsimd(pool)
            low(0, 0)
            nf.norm_gpsimd(pool, 0, 0)
            pool.wait_ge(tab_in, 32)
            program(pool, body)

        @block.tensor
        def _(pe):
            tiles.open(pe)
            with pe.Fori(0, PASSES) as i:
                for s in range(2):
                    pe.wait_ge(lo_out.sem, lo_out.done(2 * i + s))
                    for j in range(2):
                        pe.wait_ge(read.sem, read.free(4 * i + 2 * s + j, 4))
                        for c in range(DC):
                            last = split_matmul(pe, pj[:, s, j, :], (wh[:, s, c, :], wl[:, s, c, :]),
                                                [x[:, c, j * 512:(j + 1) * 512] for x in xT],
                                                c == 0, c == DC - 1)
                        last.then_inc(tiles.sem, 1)


def context_stage(nc, tag, ctx_b, ident, cT):
    with ExitStack() as ctx:
        sb, ps, sem, event = make_tools(ctx, nc, tag)
        rows = sb("rows", [P, 3, D], F32)
        tp = ps("tp", [P, 2, DC, P])
        rows_in = [sem(f"rows_in{k}") for k in range(3)]
        turned, hi_out, lo_out = sem("turned"), sem("hi"), sem("lo")
        block = ctx.enter_context(nc.Block())

        @block.sync
        def _(sp):
            for t in range(KT):
                if t >= 3:
                    sp.wait_ge(turned, t - 2)
                sp.dma_start(rows[:, t % 3], ctx_b[t * P:(t + 1) * P, :]).then_inc(rows_in[t % 3], 16)

        @block.tensor
        def _(pe):
            for t in range(KT):
                pe.wait_ge(rows_in[t % 3], 16 * (t // 3 + 1))
                if t >= 2:
                    pe.wait_ge(lo_out, t - 1)
                for c in range(DC):
                    last = pe.transpose(tp[:, t % 2, c, :], rows[:, t % 3, c * P:(c + 1) * P], ident[:])
                last.then_inc(turned, 1)

        @block.scalar
        def _(act):
            for t in range(KT):
                act.wait_ge(turned, t + 1)
                act.activation(cT[0][:, :, t * P:(t + 1) * P], tp[:, t % 2], ACT.Copy).then_inc(hi_out, 1)

        @block.vector
        def _(dve):
            for t in range(KT):
                sl = slice(t * P, (t + 1) * P)
                dve.wait_ge(hi_out, t + 1)
                dve.tensor_tensor(cT[1][:, :, sl], tp[:, t % 2], f32(cT[0][:, :, sl]), ALU.subtract).then_inc(lo_out, 1)


def value_stage(nc, tag, cT, w, store, sharp, units, ident, ctx_next=None):
    with ExitStack() as ctx:
        sb, ps, sem, event = tools = make_tools(ctx, nc, tag)
        raw = sb("raw", [P, 2, 2, 512], F32)
        wh = sb("wh", [P, 2, DC, 512], F32R)
        wl = sb("wl", [P, 2, DC, 512], F32R)
        res = sb("res", [P, 2, 512], F32)
        acc = ps("acc", [P, 2, 512])
        nf = Nf4(tools, sharp)
        if ctx_next is not None:
            rows = sb("rows", [P, 2, D], F32)
            tp = ps("tp", [P, 2, DC, P])
            rows_in = [sem("rows_in0"), sem("rows_in1")]
            turned, turned_hi, turned_lo = sem("turned"), sem("turned_hi"), sem("turned_lo")
        raw_in = [sem("raw_in0"), sem("raw_in1")]
        hi_out, lo_out, tiles, copied = sem("hi"), sem("lo"), sem("tiles"), sem("copied")
        stored = [sem("stored0"), sem("stored1")]
        block = ctx.enter_context(nc.Block())
        halves = D // 512
        CP = DC // 2
        wv_ = w.rearrange("(q c p) n -> q p c n", p=P, c=2)

        @block.sync
        def _(sp):
            def load_weights(m):
                h, q = m // CP, m % CP
                if m >= 2:
                    sp.wait_ge(lo_out, m - 1)
                sp.dma_start(raw[:, m % 2], wv_[q][:, :, h * 512:(h + 1) * 512]).then_inc(raw_in[m % 2], 16)

            def finish_unit(u):
                nf.store_sync(sp, u, u % 2, units[u][1], units[u][2])

            def load_context(t):
                if t >= 2:
                    sp.wait_ge(turned, t - 1)
                sp.dma_start(rows[:, t % 2], ctx_next[t * P:(t + 1) * P, :]).then_inc(rows_in[t % 2], 16)

            nf.open_sync(sp)
            for m in range(CP):
                load_weights(m)
                if m < 2:
                    nf.load_sync(sp, m, m, units[m][0], units[m][2])
            for m in range(CP, halves * CP):
                load_weights(m)
            for h in range(halves):
                for t in range(KT):
                    n = h * KT + t
                    sp.wait_ge(copied, n + 1)
                    sp.dma_start(store(t, h), res[:, n % 2]).then_inc(stored[n % 2], 16)
                    if ctx_next is not None and n >= KT - 2 and n - KT + 2 < KT:
                        load_context(n - KT + 2)
                    if n % 4 == 0 and n:
                        u = n // 4 - 1
                        finish_unit(u)
                        if u + 2 < len(units):
                            nf.load_sync(sp, u + 2, u % 2, units[u + 2][0], units[u + 2][2])
            finish_unit(len(units) - 1)
            nf.close_sync(sp, [sum(len(u[0]) for u in units[s::2]) for s in range(2)])
            for s in range(2):
                sp.wait_ge(stored[s], 16 * (halves * KT // 2))

        @block.scalar
        def _(act):
            def high(m):
                h, q = m // CP, m % CP
                act.wait_ge(raw_in[m % 2], 16 * (m // 2 + 1))
                act.activation(wh[:, h, 2 * q:2 * q + 2], raw[:, m % 2], ACT.Copy).then_inc(hi_out, 1)

            for m in range(CP):
                high(m)
            for h in range(halves):
                for t in range(KT):
                    n = h * KT + t
                    nf.above_scalar(act, n // 4, n // 4 % 2, share(NS4, n % 4, 4), units[n // 4][2])
                    act.wait_ge(tiles, n + 1)
                    if n >= 2:
                        act.wait_ge(stored[n % 2], 16 * (n // 2))
                    act.activation(res[:, n % 2], acc[:, n % 2], ACT.Copy).then_inc(copied, 1)
                    if n < CP:
                        high(CP + n)
                    if ctx_next is not None and h == halves - 1:
                        act.wait_ge(turned, t + 1)
                        act.activation(cT[0][:, :, t * P:(t + 1) * P], tp[:, t % 2], ACT.Copy).then_inc(turned_hi, 1)

        @block.gpsimd
        def _(pool):
            nf.open_gpsimd(pool)
            nf.norm_gpsimd(pool, 0, 0, units[0][2])
            for u in range(len(units)):
                if u + 1 < len(units):
                    nf.norm_gpsimd(pool, u + 1, (u + 1) % 2, units[u + 1][2])
                nf.finish_gpsimd(pool, u, u % 2, units[u][2])

        @block.vector
        def _(dve):
            def low(m):
                h, q = m // CP, m % CP
                dve.wait_ge(hi_out, m + 1)
                dve.tensor_tensor(wl[:, h, 2 * q:2 * q + 2], raw[:, m % 2], f32(wh[:, h, 2 * q:2 * q + 2]), ALU.subtract).then_inc(lo_out, 1)

            nf.open_vector(dve)
            for m in range(CP):
                low(m)
            nf.max_vector(dve, 0, 0, 0, units[0][2], len(units[0][0]))
            parts = [0, 0]
            for n in range(halves * KT):
                u = n // 4
                nf.step_vector(dve, u, u % 2, share(NS4, n % 4, 4), parts[u % 2], units[u][2])
                if n < CP:
                    low(CP + n)
                if ctx_next is not None and n >= KT:
                    t = n - KT
                    sl = slice(t * P, (t + 1) * P)
                    dve.wait_ge(turned_hi, t + 1)
                    dve.tensor_tensor(cT[1][:, :, sl], tp[:, t % 2], f32(cT[0][:, :, sl]), ALU.subtract).then_inc(turned_lo, 1)
                if n % 4 == 2 and u + 1 < len(units):
                    v = u + 1
                    nf.max_vector(dve, v, v % 2, parts[v % 2], units[v][2], len(units[v][0]))
                if n % 4 == 3:
                    parts[u % 2] += len(units[u][0])

        @block.tensor
        def _(pe):
            for h in range(halves):
                for t in range(KT):
                    n = h * KT + t
                    if n >= 2:
                        pe.wait_ge(copied, n - 1)
                    for c in range(DC):
                        if t == 0 and c % 2 == 0:
                            pe.wait_ge(lo_out, h * CP + c // 2 + 1)
                        last = split_matmul(pe, acc[:, n % 2], [x[:, c, t * P:(t + 1) * P] for x in cT],
                                            (wh[:, h, c, :], wl[:, h, c, :]), c == 0, c == DC - 1)
                    last.then_inc(tiles, 1)
                    if ctx_next is not None and h == halves - 1:
                        pe.wait_ge(rows_in[t % 2], 16 * (t // 2 + 1))
                        if t >= 2:
                            pe.wait_ge(turned_lo, t - 1)
                        for c in range(DC):
                            last = pe.transpose(tp[:, t % 2, c, :], rows[:, t % 2, c * P:(c + 1) * P], ident[:])
                        last.then_inc(turned, 1)


def attention_stage(nc, q_d, k_d, v_d, o_d, mask, ident):
    with ExitStack() as ctx:
        sb, ps, sem, event = make_tools(ctx, nc, "at")
        KG = 2
        HP = KG * GRP
        NS = HP * QT
        PASSES = HKV // KG
        HALF = KT // 2

        mk = sb("mk", [P, B * QT, SK], F32)
        kraw = sb("kraw", [P, SK], F32)
        vraw = sb("vraw", [P, KT, DH], F32)
        kk = [sb(f"k{x}", [P, KG, SK], F32R) for x in ("h", "l")]
        vv = [sb(f"v{x}", [P, KG, KT, DH], F32R) for x in ("h", "l")]
        qraw = sb("qraw", [P, 2, SQ], F32)
        qq = [sb(f"q{x}", [P, 2, SQ], F32R) for x in ("h", "l")]
        sc = sb("sc", [P, 2, SK], F32)
        pr = sb("pr", [P, 2, SK], F32)
        pt = [sb(f"pt{x}", [P, 2, KT, SQ], F32R) for x in ("h", "l")]
        ot = sb("ot", [P, 2, SQ], F32)
        sm = sb("sm", [P, 2, 4], F32)
        turnstile = sb("turnstile", [P, 1], F32)
        s_ps = ps("s", [P, 2, SK])
        t_ps = ps("t", [P, 2, HALF, P])
        o_ps = ps("o", [P, 2, SQ])

        mask_in, k_in, v_in = sem("mask_in"), sem("k_in"), sem("v_in")
        q_in = [sem("q_in0"), sem("q_in1")]
        o_st = [sem("o_st0"), sem("o_st1")]
        k_hi, v_hi, q_hi = event("k_hi"), event("v_hi"), event("q_hi")
        k_lo, v_lo = event("k_lo", 1), event("v_lo", 1)
        q_lo = event("q_lo", 2)
        scored = event("scored", NS)
        masked = event("masked", 2)
        maxed = event("maxed")
        expd = event("expd", 2)
        recipd = event("recipd")
        normed = event("normed")
        turned = event("turned", 4)
        t_hi = event("t_hi")
        t_lo = event("t_lo", 2)
        mixed = event("mixed", HP)
        copied = event("copied", 2)
        block = ctx.enter_context(nc.Block())

        def group(b, i, g):
            return i * KG + (b * HKV + g)

        def head(b, i, h):
            return i * HP + (b * HQ + h)

        def step(b, i, n):
            return i * NS + (b * HQ * QT + n)

        def at(b, i, h):
            if isinstance(i, int):
                return b + (i * HP + h) // HQ, (i * HP + h) % HQ
            return b, i * HP + h

        MIX_LAG = QT + 2
        COPY_LAG = MIX_LAG + QT
        STORE_LAG = COPY_LAG + 1
        LEAD = STORE_LAG + 1

        def exists(b, i, n):
            return n >= 0 and not (isinstance(i, int) and step(b, i, n) >= B * HQ * QT)

        def program(eng, do_step):
            for n in range(LEAD):
                do_step(0, 0, n)
            for b in range(B):
                with eng.Fori(0, PASSES - 1) as i:
                    for n in range(LEAD, NS + LEAD):
                        do_step(b, i, n)
                for n in range(LEAD, NS + LEAD):
                    do_step(b, PASSES - 1, n)

        FIRST = [("k", 0), ("q", 0), ("v", 0)]

        def fetches(b, i, n):
            out = [("q", h) for h in [(n + 3) // QT] if h and h * QT - 3 == n]
            out += [("k", g) for g in [(n + 8) // (GRP * QT)] if g and g * GRP * QT - 8 == n]
            out += [("v", g) for g in [(n + 6) // (GRP * QT)] if g and g * GRP * QT - 6 == n]
            return [(kind, x) for kind, x in out if exists(b, i, x * QT * (1 if kind == "q" else GRP))]

        @block.sync
        def _(sp):
            def fetch(b, i, kind, x):
                if kind == "k":
                    bb, h = at(b, i, x * GRP)
                    g = h // GRP if isinstance(i, int) else i * KG + x
                    sp.wait_ge(k_lo.sem, k_lo.free(group(b, i, x), 1))
                    sp.dma_start(kraw[:], k_d[bb, bass.ds(g, 1)].rearrange("a p n -> p (a n)")).then_inc(k_in, 16)
                elif kind == "v":
                    bb, h = at(b, i, x * GRP)
                    start = h // GRP * DH if isinstance(i, int) else i * (KG * DH) + x * DH
                    sp.wait_ge(v_lo.sem, v_lo.free(group(b, i, x), 1))
                    sp.dma_start(vraw[:], v_d[bb].rearrange("t p n -> p t n")[:, :, bass.ds(start, DH)]).then_inc(v_in, 16)
                else:
                    bb, h = at(b, i, x)
                    sp.wait_ge(q_lo.sem, q_lo.free(head(b, i, x), 2))
                    sp.dma_start(qraw[:, x % 2], q_d[bass.ds(h, 1)].rearrange("a p n -> p (a n)")[:, bb * SQ:(bb + 1) * SQ]).then_inc(q_in[x % 2], 16)

            def do_step(b, i, n):
                for kind, x in fetches(b, i, n):
                    fetch(b, i, kind, x)

            for kind, x in FIRST:
                fetch(0, 0, kind, x)
            sp.dma_start(mk[:], mask.rearrange("b (t p) k -> p (b t) k", p=P)).then_inc(mask_in, 16)
            program(sp, do_step)

        @block.gpsimd
        def _(pool):
            def fetch(b, i, kind, x):
                if kind == "k":
                    pool.wait_ge(k_hi.sem, k_hi.done(group(b, i, x)))
                    pool.tensor_tensor(kk[1][:, x % KG], kraw[:], f32(kk[0][:, x % KG]), ALU.subtract).then_inc(k_lo.sem, 1)
                elif kind == "v":
                    pool.wait_ge(v_hi.sem, v_hi.done(group(b, i, x)))
                    pool.tensor_tensor(vv[1][:, x % KG], vraw[:], f32(vv[0][:, x % KG]), ALU.subtract).then_inc(v_lo.sem, 1)
                else:
                    pool.wait_ge(q_hi.sem, q_hi.done(head(b, i, x)))
                    pool.tensor_tensor(qq[1][:, x % 2], qraw[:, x % 2], f32(qq[0][:, x % 2]), ALU.subtract).then_inc(q_lo.sem, 1)

            def do_step(b, i, n):
                for kind, x in fetches(b, i, n):
                    fetch(b, i, kind, x)

            k_lo.open(pool)
            v_lo.open(pool)
            q_lo.open(pool)
            for kind, x in FIRST:
                fetch(0, 0, kind, x)
            program(pool, do_step)

        @block.scalar
        def _(act):
            def fetch(b, i, kind, x):
                if kind == "k":
                    act.wait_ge(k_in, group(b, i, x) * 16 + 16)
                    act.wait_ge(scored.sem, scored.free(step(b, i, (x + 1) * GRP * QT - 1), NS))
                    act.activation(kk[0][:, x % KG], kraw[:], ACT.Copy).then_inc(k_hi.sem, 1)
                elif kind == "v":
                    act.wait_ge(v_in, group(b, i, x) * 16 + 16)
                    act.wait_ge(mixed.sem, mixed.free(head(b, i, (x + 1) * GRP - 1), HP))
                    act.activation(vv[0][:, x % KG], vraw[:], ACT.Copy).then_inc(v_hi.sem, 1)
                else:
                    act.wait_ge(q_in[x % 2], i * (16 * HP // 2) + 16 * (b * HQ // 2 + x // 2 + 1))
                    act.wait_ge(scored.sem, scored.free(step(b, i, QT * (x + 1) - 1), 2 * QT))
                    act.activation(qq[0][:, x % 2], qraw[:, x % 2], ACT.Copy).then_inc(q_hi.sem, 1)

            def exponentials(b, i, n):
                act.wait_ge(maxed.sem, maxed.done(step(b, i, n)))
                act.wait_ge(turned.sem, turned.free(2 * step(b, i, n) + 1, 4))
                act.activation(pr[:, n % 2], sc[:, n % 2], ACT.Exp, bias=sm[:, n % 2, 1:2],
                               accum_out=sm[:, n % 2, 2:3]).then_inc(expd.sem, 1)

            def turn_high(b, i, n):
                h = n // QT
                if n % QT == 0:
                    act.wait_ge(mixed.sem, mixed.free(head(b, i, h), 2))
                for j in range(2):
                    act.wait_ge(turned.sem, turned.done(2 * step(b, i, n) + j))
                    act.activation(pt[0][:, h % 2, j * HALF:(j + 1) * HALF, (n % QT) * P:(n % QT + 1) * P],
                                   t_ps[:, j], ACT.Copy).then_inc(t_hi.sem, 1)

            def copy_out(b, i, h):
                act.wait_ge(mixed.sem, mixed.done(head(b, i, h)))
                act.wait_ge(o_st[h % 2], i * (16 * HP // 2) + 16 * (b * HQ // 2 + h // 2 + 1))
                act.activation(ot[:, h % 2], o_ps[:, h % 2], ACT.Copy).then_inc(copied.sem, 1)

            def store_out(b, i, h):
                bb, hh = at(b, i, h)
                act.wait_ge(copied.sem, copied.done(head(b, i, h)))
                act.dma_start(o_d[bass.ds(hh, 1)].rearrange("a p n -> p (a n)")[:, bb * SQ:(bb + 1) * SQ],
                              ot[:, h % 2]).then_inc(o_st[h % 2], 16)

            def do_step(b, i, n):
                for kind, x in fetches(b, i, n):
                    fetch(b, i, kind, x)
                if exists(b, i, n - 2):
                    turn_high(b, i, n - 2)
                if exists(b, i, n):
                    exponentials(b, i, n)
                for lag, act_on in ((COPY_LAG, copy_out), (STORE_LAG, store_out)):
                    if (n - lag) % QT == 0 and exists(b, i, n - lag):
                        act_on(b, i, (n - lag) // QT)

            expd.open(act)
            copied.open(act)
            for s in range(2):
                act.sem_inc(o_st[s], 16)
            for kind, x in FIRST:
                fetch(0, 0, kind, x)
            program(act, do_step)
            for s in range(2):
                act.wait_ge(o_st[s], 16 * (B * HQ // 2 + 1))

        @block.vector
        def _(dve):
            def mask_and_max(b, i, n):
                bb = at(b, i, n // QT)[0]
                dve.wait_ge(scored.sem, scored.done(step(b, i, n)))
                dve.wait_ge(expd.sem, expd.free(step(b, i, n), 2))
                dve.memset(turnstile[:], 0.0)
                dve.tensor_tensor_reduce(sc[:, n % 2], s_ps[:, n % 2], mk[:, bb * QT + n % QT], 1.0, NEG,
                                         ALU.add, ALU.max, sm[:, n % 2, 0:1]).then_inc(masked.sem, 1)
                dve.wait_ge(masked.sem, masked.done(step(b, i, n)))
                dve.tensor_scalar(sm[:, n % 2, 1:2], sm[:, n % 2, 0:1], -1.0, None, ALU.mult).then_inc(maxed.sem, 1)

            def normalise(b, i, n):
                dve.wait_ge(expd.sem, expd.done(step(b, i, n)))
                dve.reciprocal(sm[:, n % 2, 3:4], sm[:, n % 2, 2:3]).then_inc(recipd.sem, 1)
                dve.wait_ge(recipd.sem, recipd.done(step(b, i, n)))
                dve.tensor_scalar(pr[:, n % 2], pr[:, n % 2], sm[:, n % 2, 3:4], None, ALU.mult).then_inc(normed.sem, 1)

            def turn_low(b, i, n):
                h = n // QT
                for j in range(2):
                    sl = (slice(None), h % 2, slice(j * HALF, (j + 1) * HALF), slice((n % QT) * P, (n % QT + 1) * P))
                    dve.wait_ge(t_hi.sem, t_hi.done(2 * step(b, i, n) + j))
                    dve.tensor_tensor(pt[1][sl], t_ps[:, j], f32(pt[0][sl]), ALU.subtract).then_inc(t_lo.sem, 1)

            def do_step(b, i, n):
                for lag, act_on in ((0, mask_and_max), (1, normalise), (2, turn_low)):
                    if exists(b, i, n - lag):
                        act_on(b, i, n - lag)

            masked.open(dve)
            t_lo.open(dve)
            dve.wait_ge(mask_in, 16)
            program(dve, do_step)

        @block.tensor
        def _(pe):
            def scores(b, i, n):
                h = n // QT
                g = h // GRP
                if n % (QT * GRP) == 0:
                    pe.wait_ge(k_lo.sem, k_lo.done(group(b, i, g)))
                if n % QT == 0:
                    pe.wait_ge(q_lo.sem, q_lo.done(head(b, i, h)))
                pe.wait_ge(masked.sem, masked.free(step(b, i, n), 2))
                for j in range(SK // 512):
                    last = split_matmul(pe, s_ps[:, n % 2, j * 512:(j + 1) * 512],
                                        [x[:, h % 2, (n % QT) * P:(n % QT + 1) * P] for x in qq],
                                        [x[:, g % KG, j * 512:(j + 1) * 512] for x in kk], True, True)
                last.then_inc(scored.sem, 1)

            def turn(b, i, n):
                pe.wait_ge(normed.sem, normed.done(step(b, i, n)))
                for j in range(2):
                    pe.wait_ge(t_lo.sem, t_lo.free(2 * step(b, i, n) + j, 2))
                    for c in range(HALF):
                        k = j * HALF + c
                        last = pe.transpose(t_ps[:, j, c, :], pr[:, n % 2, k * P:(k + 1) * P], ident[:])
                    last.then_inc(turned.sem, 1)

            def mix(b, i, n):
                h, quarter = n // QT, n % QT
                g = h // GRP
                if h % GRP == 0 and quarter == 0:
                    pe.wait_ge(v_lo.sem, v_lo.done(group(b, i, g)))
                if quarter == 0:
                    pe.wait_ge(t_lo.sem, t_lo.done(2 * step(b, i, QT * (h + 1) - 1) + 1))
                    pe.wait_ge(copied.sem, copied.free(head(b, i, h), 2))
                for c in share(KT, quarter, QT):
                    last = split_matmul(pe, o_ps[:, h % 2], [x[:, g % KG, c, :] for x in vv],
                                        [x[:, h % 2, c, :] for x in pt], c == 0, c == KT - 1)
                if quarter == QT - 1:
                    last.then_inc(mixed.sem, 1)

            def do_step(b, i, n):
                for lag, act_on in ((0, scores), (2, turn), (MIX_LAG, mix)):
                    if exists(b, i, n - lag):
                        act_on(b, i, n - lag)

            scored.open(pe)
            turned.open(pe)
            mixed.open(pe)
            program(pe, do_step)


def output_stage(nc, o_d, wo, X, sharp, unit_src, unit_dst):
    with ExitStack() as ctx:
        sb, ps, sem, event = tools = make_tools(ctx, nc, "ou")
        oraw = sb("oraw", [P, 2, T], F32)
        wraw = sb("wraw", [P, 2, D], F32)
        oo = [sb(f"o{x}", [P, 2, GRP, T], F32R) for x in ("h", "l")]
        ww = [sb(f"w{x}", [P, 2, GRP, D], F32R) for x in ("h", "l")]
        acc = ps("acc", [P, 4, 512])
        nf = Nf4(tools, sharp)
        NT = TT * (D // 512)
        o_in = [sem(f"o_in{r}") for r in range(2)]
        w_in = [sem(f"w_in{r}") for r in range(2)]
        o_hi, w_hi = event("o_hi"), event("w_hi")
        o_lo, w_lo = event("o_lo", 2), event("w_lo", 2)
        tiles = event("tiles", 2 * NT)
        added = event("added", 4)
        block = ctx.enter_context(nc.Block())
        PASSES = HQ // GRP // 2
        UE = 4

        def program(eng, body):
            with eng.Fori(0, PASSES - 1) as i:
                body(i, False)
            body(PASSES - 1, True)

        def head(i, s, r):
            return i * (2 * GRP) + (s * GRP + r)

        @block.sync
        def _(sp):
            def load(i, s, r):
                h = head(i, s, r)
                sp.wait_ge(o_lo.sem, o_lo.free(h, 2))
                sp.dma_start(oraw[:, r % 2], o_d[bass.ds(h, 1)].rearrange("a p n -> p (a n)")).then_inc(o_in[r % 2], 16)
                sp.wait_ge(w_lo.sem, w_lo.free(h, 2))
                sp.dma_start(wraw[:, r % 2], wo[bass.ds(h * DH, DH), :]).then_inc(w_in[r % 2], 16)

            def body(i, last):
                for e in range(UE):
                    s, odd = e // 2, e % 2
                    ahead = s + 1 + odd
                    if ahead < 2 or not last:
                        for r in (0, 1) if odd else (2, 3):
                            load(i + ahead // 2, ahead % 2, r)
                    nf.store_sync(sp, i * UE + e, odd, [unit_dst(i, e)])
                    if e + 2 < UE:
                        nf.load_sync(sp, i * UE + (e + 2), odd, [unit_src(i, e + 2)])
                    elif not last:
                        nf.load_sync(sp, i * UE + (e + 2), odd, [unit_src(i + 1, e + 2 - UE)])

            nf.open_sync(sp)
            for r in range(2):
                load(0, 0, r)
            nf.load_sync(sp, 0, 0, [unit_src(0, 0)])
            for r in range(2, GRP):
                load(0, 0, r)
            nf.load_sync(sp, 1, 1, [unit_src(0, 1)])
            for r in range(2):
                load(0, 1, r)
            program(sp, body)
            nf.close_sync(sp, [PASSES * UE // 2] * 2)

        @block.scalar
        def _(act):
            def high(i, s, r):
                h = head(i, s, r)
                if r == 0:
                    act.wait_ge(tiles.sem, tiles.free(i * (2 * NT) + ((s + 1) * NT - 1), 2 * NT))
                act.wait_ge(o_in[r % 2], i * 64 + (32 * s + 16 * (r // 2 + 1)))
                act.activation(oo[0][:, s, r], oraw[:, r % 2], ACT.Copy).then_inc(o_hi.sem, 1)
                act.wait_ge(w_in[r % 2], i * 64 + (32 * s + 16 * (r // 2 + 1)))
                act.activation(ww[0][:, s, r], wraw[:, r % 2], ACT.Copy).then_inc(w_hi.sem, 1)

            def body(i, last):
                for s in range(2):
                    for r in range(GRP):
                        if s == 0:
                            high(i, 1, r)
                        elif not last:
                            high(i + 1, 0, r)
                        for k in share(2 * NS4, r, GRP):
                            e = 2 * s + k // NS4
                            nf.above_scalar(act, i * UE + e, e % 2, [k % NS4])

            for r in range(GRP):
                high(0, 0, r)
            program(act, body)

        @block.gpsimd
        def _(pool):
            def split(i, s, r):
                h = head(i, s, r)
                pool.wait_ge(o_hi.sem, o_hi.done(h))
                pool.tensor_tensor(oo[1][:, s, r], oraw[:, r % 2], f32(oo[0][:, s, r]), ALU.subtract).then_inc(o_lo.sem, 1)
                pool.wait_ge(w_hi.sem, w_hi.done(h))
                pool.tensor_tensor(ww[1][:, s, r], wraw[:, r % 2], f32(ww[0][:, s, r]), ALU.subtract).then_inc(w_lo.sem, 1)

            def body(i, last):
                for e in range(UE):
                    s = e // 2
                    for r in (0, 1) if e % 2 == 0 else (2, 3):
                        if s == 0:
                            split(i, 1, r)
                        elif not last:
                            split(i + 1, 0, r)
                    if e < UE - 1 or not last:
                        nf.norm_gpsimd(pool, i * UE + (e + 1), (e + 1) % 2)
                    nf.finish_gpsimd(pool, i * UE + e, e % 2)

            nf.open_gpsimd(pool)
            nf.norm_gpsimd(pool, 0, 0)
            pool.wait_ge(o_lo.sem, o_lo.done(GRP - 1))
            pool.wait_ge(w_lo.sem, w_lo.done(GRP - 1))
            program(pool, body)

        @block.vector
        def _(dve):
            def split(i, s, r):
                h = head(i, s, r)
                dve.wait_ge(o_hi.sem, o_hi.done(h))
                dve.tensor_tensor(oo[1][:, s, r], oraw[:, r % 2], f32(oo[0][:, s, r]), ALU.subtract).then_inc(o_lo.sem, 1)
                dve.wait_ge(w_hi.sem, w_hi.done(h))
                dve.tensor_tensor(ww[1][:, s, r], wraw[:, r % 2], f32(ww[0][:, s, r]), ALU.subtract).then_inc(w_lo.sem, 1)

            def body(i, last):
                for s in range(2):
                    for k in range(NT):
                        m = i * (2 * NT) + (s * NT + k)
                        t, n = k // 2, k % 2
                        dve.wait_ge(tiles.sem, tiles.done(m))
                        dve.tensor_tensor(X[:, t, n * 512:(n + 1) * 512], acc[:, k % 4],
                                          X[:, t, n * 512:(n + 1) * 512], ALU.add).then_inc(added.sem, 1)
                        for j in share(2 * NS4, k, NT):
                            e = 2 * s + j // NS4
                            nf.step_vector(dve, i * UE + e, e % 2, [j % NS4], i * (UE // 2) + e // 2)
                            if j % NS4 == NS4 // 4 + 1 and (e < UE - 1 or not last):
                                nf.max_vector(dve, i * UE + (e + 1), (e + 1) % 2, i * (UE // 2) + (e + 1) // 2)

            o_lo.open(dve)
            w_lo.open(dve)
            added.open(dve)
            nf.open_vector(dve)
            for r in range(GRP):
                split(0, 0, r)
                if r == 1:
                    nf.max_vector(dve, 0, 0, 0)
            program(dve, body)

        @block.tensor
        def _(pe):
            tiles.open(pe)
            with pe.Fori(0, PASSES) as i:
                for s in range(2):
                    for k in range(NT):
                        t, n = k // 2, k % 2
                        pe.wait_ge(added.sem, added.free(i * (2 * NT) + (s * NT + k), 4))
                        for r in range(GRP):
                            if k == 0:
                                pe.wait_ge(o_lo.sem, o_lo.done(head(i, s, r)))
                                pe.wait_ge(w_lo.sem, w_lo.done(head(i, s, r)))
                            last = split_matmul(pe, acc[:, k % 4], [x[:, s, r, t * P:(t + 1) * P] for x in oo],
                                                [x[:, s, r, n * 512:(n + 1) * 512] for x in ww],
                                                r == 0, r == GRP - 1)
                        last.then_inc(tiles.sem, 1)


def router_stage(nc, X, xn, ident, router_w, router_b, expert_b):
    with ExitStack() as ctx:
        sb, ps, sem, event = make_tools(ctx, nc, "ro")
        rw = sb("rw", [E, D], F32)
        rwT = sb("rwT", [P, DC, E], F32)
        rb = sb("rb", [P, E], F32)
        eb = sb("eb", [E, D], F32)
        xT = sb("xT", [P, 2, DC, P], F32)
        lg = sb("lg", [P, 2, E], F32)
        ex = sb("ex", [P, 2, E], F32)
        rest = sb("rest", [P, 2, E], F32)
        top = sb("top", [P, 2, TOPK], F32)
        sm = sb("sm", [P, 2, 6], F32)
        wT = sb("wT", [E, 2, P], F32)
        tmp = sb("tmp", [P, D], F32)
        t_ps = ps("t", [P, DC, P])
        l_ps = ps("l", [P, 2, 512])
        w_ps = ps("w", [P, 512])
        m_ps = ps("m", [P, D])
        w_in, rw_turned, rw_copied = sem("w_in"), sem("rw_turned"), sem("rw_copied")
        turned, copied, logits, seq, picked = sem("turned"), sem("copied"), sem("logits"), sem("seq"), sem("picked")
        maxed, expd = sem("maxed"), sem("expd")
        w_turned, w_copied, mixed, added = sem("w_turned"), sem("w_copied"), sem("mixed"), sem("added")
        block = ctx.enter_context(nc.Block())

        @block.sync
        def _(sp):
            sp.dma_start(rw[:], router_w).then_inc(w_in, 16)
            sp.dma_start(eb[:], expert_b).then_inc(w_in, 16)
            sp.dma_start(rb[:], router_b.rearrange("(a e) -> a e", a=1).broadcast_to((P, E))).then_inc(w_in, 16)

        @block.tensor
        def _(pe):
            pe.wait_ge(w_in, 48)
            for c in range(DC):
                last = pe.transpose(t_ps[:, c, 0:E], rw[:, c * P:(c + 1) * P], ident[0:E, 0:E])
            last.then_inc(rw_turned, 1)

            def turn(t):
                if t == 0:
                    pe.wait_ge(rw_copied, 1)
                else:
                    pe.wait_ge(copied, t)
                for c in range(DC):
                    last = pe.transpose(t_ps[:, c, :], xn[:, t, c * P:(c + 1) * P], ident[:])
                last.then_inc(turned, 1)

            def score(t):
                pe.wait_ge(copied, t + 1)
                if t >= 2:
                    pe.wait_ge(picked, t - 1)
                for c in range(DC):
                    last = pe.matmul(l_ps[:, t % 2, 0:E], xT[:, t % 2, c, :], rwT[:, c, :], start=c == 0, stop=c == DC - 1)
                last.then_inc(logits, 1)

            turn(0)
            turn(1)
            score(0)
            for t in range(TT):
                if t + 2 < TT:
                    turn(t + 2)
                if t + 1 < TT:
                    score(t + 1)
                pe.wait_ge(picked, t + 1)
                if t:
                    pe.wait_ge(w_copied, t)
                pe.transpose(w_ps[0:E, 0:P], rest[:, t % 2, :], ident[:]).then_inc(w_turned, 1)
                pe.wait_ge(w_copied, t + 1)
                if t:
                    pe.wait_ge(added, t)
                for n in range(2):
                    last = pe.matmul(m_ps[:, n * 512:(n + 1) * 512], wT[:, t % 2, :],
                                     eb[:, n * 512:(n + 1) * 512], start=True, stop=True)
                last.then_inc(mixed, 1)

        @block.scalar
        def _(act):
            act.wait_ge(rw_turned, 1)
            act.activation(rwT[:], t_ps[:, :, 0:E], ACT.Copy).then_inc(rw_copied, 1)

            def copy(t):
                act.wait_ge(turned, t + 1)
                if t >= 2:
                    act.wait_ge(logits, t - 1)
                act.activation(xT[:, t % 2], t_ps[:], ACT.Copy).then_inc(copied, 1)

            copy(0)
            copy(1)
            for t in range(TT):
                act.wait_ge(maxed, t + 1)
                act.activation(ex[:, t % 2], lg[:, t % 2], ACT.Exp, bias=sm[:, t % 2, 1:2],
                               accum_out=sm[:, t % 2, 2:3]).then_inc(expd, 1)
                act.wait_ge(w_turned, t + 1)
                if t >= 2:
                    act.wait_ge(mixed, t - 1)
                act.activation(wT[:, t % 2, :], w_ps[0:E, 0:P], ACT.Copy).then_inc(w_copied, 1)
                if t + 2 < TT:
                    copy(t + 2)

        @block.vector
        def _(dve):
            steps = [0]

            def after(ins):
                steps[0] += 1
                ins.then_inc(seq, 1)
                dve.wait_ge(seq, steps[0])

            dve.wait_ge(w_in, 48)
            for t in range(TT):
                s = t % 2
                col = [sm[:, s, k:k + 1] for k in range(6)]
                dve.wait_ge(logits, t + 1)
                after(dve.tensor_tensor_reduce(lg[:, s], l_ps[:, s, 0:E], rb[:], 1.0, NEG, ALU.add, ALU.max, col[0]))
                dve.tensor_scalar(col[1], col[0], -1.0, None, ALU.mult).then_inc(maxed, 1)
                dve.wait_ge(expd, t + 1)
                after(dve.reciprocal(col[3], col[2]))
                after(dve.tensor_scalar(ex[:, s], ex[:, s], col[3], None, ALU.mult))
                after(dve.max(top[:, s], ex[:, s]))
                if t >= 2:
                    dve.wait_ge(w_turned, t - 1)
                after(dve.match_replace(rest[:, s], top[:, s], ex[:, s], 0.0))
                after(dve.reduce_sum(col[4], top[:, s], AX.X))
                dve.tensor_tensor(rest[:, s], ex[:, s], rest[:, s], ALU.subtract).then_inc(picked, 1)
                after(dve.scalar_tensor_tensor(tmp[:], xn[:, t], col[4], X[:, t], ALU.mult, ALU.add))
                dve.wait_ge(mixed, t + 1)
                dve.tensor_tensor(X[:, t], m_ps[:], tmp[:], ALU.add).then_inc(added, 1)


def quantised_stage(nc, X, xn, ident_bf, context, scales):
    with ExitStack() as ctx:
        sb, ps, sem, event = make_tools(ctx, nc, "qn")
        par = sb("par", [P, 4], F32)
        k = sb("k", [P, 6], F32)
        rows = sb("rows", [P, 3, D], F32)
        work = sb("work", [P, 2, D], F32)
        qa = sb("qa", [P, 2, D], BF16)
        qaT = sb("qaT", [P, TT, DC, P], BF16)
        rowsum = sb("rowsum", [P, 2, TT], F32)
        qb = sb("qb", [P, B, KT, D], BF16)
        ones = sb("ones", [P, P], BF16)
        colsum = sb("colsum", [P, B, D], F32)
        tmp = sb("tmp", [P, 512], F32)
        t_ps = ps("t", [P, 2, DC, P], BF16)
        c_ps = ps("c", [P, D])
        acc = ps("acc", [P, 4, 512])
        par_in, k_ready, ones_made = sem("par_in"), sem("k_ready"), sem("ones_made")
        rows_in = [sem(f"rows_in{r}") for r in range(3)]
        seq, qa_done, qb_done, scaled = sem("seq"), sem("qa_done"), sem("qb_done"), sem("scaled")
        turned, copied, col_done, col_read, tiles, added = (
            sem("turned"), sem("copied"), sem("col_done"), sem("col_read"), sem("tiles"), sem("added"))
        block = ctx.enter_context(nc.Block())

        @block.sync
        def _(sp):
            for j, v in enumerate(scales):
                sp.dma_start(par[:, j:j + 1], v.rearrange("(a b) -> a b", a=1).broadcast_to((P, 1))).then_inc(par_in, 16)
            for n in range(B * KT):
                if n >= 3:
                    sp.wait_ge(scaled, TT + n - 2)
                sp.dma_start(rows[:, n % 3], context[n // KT, (n % KT) * P:(n % KT + 1) * P, :]).then_inc(rows_in[n % 3], 16)

        @block.scalar
        def _(act):
            act.wait_ge(k_ready, 1)
            def scale(n):
                a = n < TT
                if n >= 2:
                    act.wait_ge(qa_done if n - 2 < TT else qb_done, n - 1 if n - 2 < TT else n - 1 - TT)
                if not a:
                    m = n - TT
                    act.wait_ge(rows_in[m % 3], 16 * (m // 3 + 1))
                src = xn[:, n] if a else rows[:, (n - TT) % 3]
                act.activation(work[:, n % 2], src, ACT.Identity, bias=par[:, 1:2] if a else par[:, 3:4],
                               scale=k[:, 0:1] if a else k[:, 1:2]).then_inc(scaled, 1)

            for n in range(2):
                scale(n)
            for n in range(TT + B * KT - 2):
                if n < TT:
                    act.wait_ge(turned, n + 1)
                    act.activation(qaT[:, n], t_ps[:, n % 2], ACT.Copy).then_inc(copied, 1)
                scale(n + 2)

        @block.gpsimd
        def _(pool):
            pool.memset(ones[:], 1.0).then_inc(ones_made, 1)

        @block.vector
        def _(dve):
            steps = [0]

            def after(ins):
                steps[0] += 1
                ins.then_inc(seq, 1)
                dve.wait_ge(seq, steps[0])

            dve.wait_ge(par_in, 64)
            dve.reciprocal(k[:, 0:1], par[:, 0:1])
            dve.reciprocal(k[:, 1:2], par[:, 2:3])
            dve.tensor_scalar(k[:, 2:3], par[:, 1:2], -1.0, QMID, ALU.mult, ALU.add)
            dve.tensor_tensor(k[:, 4:5], par[:, 0:1], par[:, 2:3], ALU.mult)
            after(dve.tensor_scalar(k[:, 3:4], par[:, 3:4], -1.0, QMID, ALU.mult, ALU.add))
            dve.tensor_scalar(k[:, 5:6], k[:, 3:4], float(D), None, ALU.mult).then_inc(k_ready, 1)

            def quantise(n, out, done):
                dve.wait_ge(scaled, n + 1)
                after(dve.tensor_scalar(work[:, n % 2], work[:, n % 2], QMAX, 0.0, ALU.min, ALU.max))
                dve.tensor_scalar(out, work[:, n % 2], ROUND, ROUND + QMID, ALU.add, ALU.subtract).then_inc(done, 1)

            for t in range(TT):
                if t >= 2:
                    dve.wait_ge(turned, t - 1)
                quantise(t, qa[:, t % 2], qa_done)
                dve.wait_ge(qa_done, t + 1)
                last = dve.reduce_sum(rowsum[:, 0, t:t + 1], qa[:, t % 2], AX.X)
            after(last)
            after(dve.tensor_scalar(rowsum[:, 1], rowsum[:, 0], k[:, 3:4], None, ALU.mult))

            def finish_columns(b):
                dve.wait_ge(col_done, b + 1)
                dve.tensor_scalar(colsum[:, b], c_ps[:], k[:, 5:6], k[:, 2:3], ALU.add, ALU.mult).then_inc(col_read, 1)
                dve.wait_ge(col_read, b + 1)

            def finish(b, tiles_of_b):
                for j in tiles_of_b:
                    n = b * 2 * QT + j
                    t, h = n // 2, n % 2
                    sl = slice(h * 512, (h + 1) * 512)
                    dve.wait_ge(tiles, n + 1)
                    after(dve.scalar_tensor_tensor(tmp[:], acc[:, n % 4], rowsum[:, 1, t:t + 1], colsum[:, b, sl], ALU.add, ALU.add))
                    after(dve.scalar_tensor_tensor(X[:, t, sl], tmp[:], k[:, 4:5], X[:, t, sl], ALU.mult, ALU.add))
                    dve.sem_inc(added, 1)

            for n in range(B * KT):
                quantise(TT + n, qb[:, n // KT, n % KT], qb_done)
            for b in range(B - 1):
                finish_columns(b)
                finish(b, range(2 * QT))
            finish_columns(B - 1)
            finish(B - 1, range(2 * QT))

        @block.tensor
        def _(pe):
            for t in range(TT):
                pe.wait_ge(qa_done, t + 1)
                if t >= 2:
                    pe.wait_ge(copied, t - 1)
                for c in range(DC):
                    last = pe.transpose(t_ps[:, t % 2, c, :], qa[:, t % 2, c * P:(c + 1) * P], ident_bf[:])
                last.then_inc(turned, 1)
            pe.wait_ge(copied, TT)
            pe.wait_ge(ones_made, 1)
            for b in range(B):
                pe.wait_ge(qb_done, (b + 1) * KT)
                if b:
                    pe.wait_ge(col_read, b)
                for h in range(2):
                    for c in range(KT):
                        last = pe.matmul(c_ps[:, h * 512:(h + 1) * 512], ones[:], qb[:, b, c, h * 512:(h + 1) * 512],
                                         start=c == 0, stop=c == KT - 1)
                last.then_inc(col_done, 1)
                for j in range(2 * QT):
                    n = b * 2 * QT + j
                    t, h = n // 2, n % 2
                    if n >= 4:
                        pe.wait_ge(added, n - 3)
                    for c in range(DC):
                        last = pe.matmul(acc[:, n % 4], qaT[:, t, c, :], qb[:, b, c, h * 512:(h + 1) * 512],
                                         start=c == 0, stop=c == DC - 1)
                    last.then_inc(tiles, 1)


def ffn_stage(nc, xT, X, ident, dq, dq3, ready, sharp, unit_src, unit_dst, rest_src, rest_dst, out):
    with ExitStack() as ctx:
        sb, ps, sem, event = tools = make_tools(ctx, nc, "ff")
        raw = sb("raw", [P, 3, D], F32)
        gu = [sb(f"gu{x}", [P, 2, 2, D], F32R) for x in ("h", "l")]
        dn = [sb(f"dn{x}", [P, 2, D], F32R) for x in ("h", "l")]
        act_s = sb("act_s", [P, 2, 512], F32)
        hid = sb("hid", [P, 2, 512], F32)
        hT = [sb(f"h{x}", [P, 2, T], F32R) for x in ("h", "l")]
        t_ps = ps("t", [P, 2, 512])
        g_ps = ps("g", [P, 2, 2, 512])
        y_ps = ps("y", [P, 2, 512])
        nf = Nf4(tools, sharp)
        PAIRS = HC // 2
        NT = TT * 2
        REST = HF - (HC - 1) * P
        w3v = dq3.rearrange("(c p) h -> p c h", p=P)
        raw_in = [sem(f"raw_in{j}") for j in range(3)]
        zeroed, out_stored = sem("zeroed"), sem("out_stored")
        turned = event("turned")
        w_hi = event("w_hi")
        w_lo = event("w_lo", 2)
        gated = event("gated", 4)
        silu = event("silu")
        gone = event("gone", 2)
        h_hi = event("h_hi")
        h_lo = event("h_lo", 2)
        tiles = event("tiles", NT)
        added = event("added", 2)
        block = ctx.enter_context(nc.Block())

        LEAD = 4
        ORDER = (2, 3, 4, 5, 0, 1)

        def is_last(m):
            return isinstance(m, int) and m == HC - 1

        def turn_no(m, x):
            if isinstance(m, int) and m < 0:
                return ORDER.index(x)
            return m * 6 + (LEAD + (x if is_last(m) else ORDER.index(x)))

        def turned_part(x):
            return (2, x) if x < 2 else ((x - 2) // 2, x % 2)

        UE = 4
        LOOPS = (HC - 1 - ready) * 2 // UE
        UNITS = LOOPS * UE

        def program(eng, chunk, tail):
            def body(pr, i, q, units):
                chunk(pr, pr * 2 + 1, 1, i, 2 * q, units)
                chunk(pr, pr * 2 + 2, 0, i, 2 * q, units)

            chunk(-1, 0, 0, 0, 0, 0)
            with eng.Fori(0, LOOPS - 1) as i:
                for q in range(2):
                    body(2 * i + q, i, q, 2)
            for q in range(2):
                body(2 * (LOOPS - 1) + q, LOOPS - 1, q, 2)
            body(2 * LOOPS, LOOPS, 0, 1)
            for pr in range(2 * LOOPS + 1, PAIRS - 1):
                body(pr, LOOPS, 0, 0)
            chunk(PAIRS - 1, HC - 1, 1, LOOPS, 0, 0)
            tail(PAIRS - 1)

        def items(s, m, pr):
            def turns(*xs):
                return [("turn", x) for x in xs if x < 2 or not is_last(m)]

            def sums(j):
                if s or isinstance(pr, int) and pr < 0:
                    return []
                return [("sum", k) for k in range(j * NT // 2, (j + 1) * NT // 2)]

            if s == 0:
                return ([("-", 0)] * 2 + sums(0) + [("-", 0)] + turns(2, 3) + [("product", 0), ("hidden", 0)] + turns(4, 5)
                        + sums(1) + [("-", 0)] + turns(0, 1) + [("product", 1), ("hidden", 1)])
            return (turns(2, 3) + [("product", 0), ("hidden", 0)] + turns(4, 5, 0, 1)
                    + [("product", 1), ("hidden", 1)])

        def unit_steps(s, p, count, first, units):
            total = units * NS4
            cut = total * 7 // 30
            some = range(0, cut) if s else range(cut, total)
            return [(first + some[k] // NS4, some[k] % NS4) for k in share(len(some), p, count)]

        def has_next(i, e):
            return not (isinstance(i, int) and i == LOOPS)

        def is_rest(i, e):
            return isinstance(i, int) and i * UE + e == UNITS

        @block.sync
        def _(sp):
            def load_weight(m, j, start, count=None):
                rows = REST if isinstance(m, int) and m == HC - 1 else P
                if rows < P and j != 1:
                    sp.wait_ge(zeroed, 1 + j // 2)
                if count is not None:
                    sp.wait_ge(turned.sem, count)
                if j < 2:
                    sp.dma_start(raw[0:rows, j], dq[j][bass.ds(start, rows), :]).then_inc(raw_in[j], 16)
                else:
                    sp.dma_start(raw[:, j].rearrange("p (c h) -> p c h", h=P)[:, :, 0:rows],
                                 w3v[:, :, bass.ds(start, rows)]).then_inc(raw_in[j], 16)

            def load_w3(m, s, i, first):
                start = (m + 1) * P if isinstance(m, int) else (i * 4 + (2 * (first // 2) + 3 - s)) * P
                load_weight(m + 1, 2, start, turn_no(m, 1) + 1)

            def load_unit(i, e):
                rest = is_rest(i, e)
                nf.load_sync(sp, i * UE + e, e % 2, rest_src if rest else [unit_src(i * (UE // 2) + (ready + e // 2), e % 2)])

            def store_unit(i, e):
                rest = is_rest(i, e)
                nf.store_sync(sp, i * UE + e, e % 2, rest_dst if rest else [unit_dst(i * (UE // 2) + (ready + e // 2), e % 2)])

            def chunk(pr, m, s, i, first, units):
                def load_next():
                    if not (isinstance(m, int) and m + 2 >= HC):
                        for j in range(2):
                            load_weight(m + 2, j, (m + 2) * P, turn_no(m, 2 * j + 3) + 1)

                if s and units:
                    for slot in range(2):
                        sp.wait_ge(nf.stored[slot], (i * (UE // 2) + (first + 1 - slot) // 2 + 1) * 16)
                elif isinstance(m, int) and m == HC - 3:
                    sp.wait_ge(nf.stored[0], (UNITS // 2 + 3) * 16)
                if s == 1 and units and has_next(i, first):
                    load_unit(i, first + 1)
                if s == 0 and units > 1:
                    store_unit(i, first)
                    load_unit(i, first + 2)
                load_next()
                if not is_last(m):
                    load_w3(m, s, i, first)
                if s == 0 and units:
                    store_unit(i, first + units - 1)

            nf.open_sync(sp)
            for j in range(3):
                load_weight(0, j, 0)
            load_unit(0, 0)
            for j in range(2):
                load_weight(1, j, P, turn_no(-1, 2 * j + 3) + 1)
            def store(pr):
                for t in range(TT):
                    sp.wait_ge(added.sem, added.done(pr * NT + 2 * t + 1))
                    sp.dma_start(out.rearrange("b (t p) d -> (b t) p d", p=P)[t], X[:, t, :]).then_inc(out_stored, 16)

            program(sp, chunk, store)
            sp.wait_ge(out_stored, 16 * TT)
            nf.close_sync(sp, [UNITS // 2 + 2, UNITS // 2])

        @block.gpsimd
        def _(pool):
            def chunk(pr, m, s, i, first, units):
                for e in range(first, first + units) if s == 0 else ():
                    if has_next(i, e):
                        nf.norm_gpsimd(pool, i * UE + (e + 1), (e + 1) % 2)
                    nf.finish_gpsimd(pool, i * UE + e, e % 2)

            nf.open_gpsimd(pool)
            nf.norm_gpsimd(pool, 0, 0)
            program(pool, chunk, lambda pr: None)
            pool.wait_ge(nf.finished.sem, nf.finished.done(UNITS))
            pool.wait_ge(turned.sem, turn_no(HC - 3, 5) + 1)
            pool.memset(raw[REST:P, 0:2], 0.0).then_inc(zeroed, 1)
            pool.wait_ge(turned.sem, turn_no(HC - 2, 1) + 1)
            pool.wait_ge(zeroed, 1)
            pool.memset(raw[:, 2], 0.0).then_inc(zeroed, 1)

        @block.tensor
        def _(pe):
            def turn(m, x):
                j, k = turned_part(x)
                if k == 0:
                    pe.wait_ge(raw_in[j], (m if j == 2 else m + 1) * 16 + 16)
                pe.wait_ge(w_lo.sem, w_lo.free(turn_no(m, x), 2))
                for c in range(4):
                    o = (4 * k + c) * P
                    last = pe.transpose(t_ps[:, k, c * P:(c + 1) * P], raw[:, j, o:o + P], ident[:])
                last.then_inc(turned.sem, 1)

            TURNS = [[(None, None), (2, 3), (4, 5), (0, 1)], [(None, 2), (3, None), (4, 5), (0, 1)]]

            def gate_up_tile(m, s, tile):
                j, u = tile // 2, tile % 2
                if j == 0:
                    pe.wait_ge(w_lo.sem, w_lo.done(turn_no(m - 1, 2 * u + 3)))
                if u == 0:
                    pe.wait_ge(gone.sem, gone.free(m * 2 + j, 2))
                for c in range(DC):
                    last = split_matmul(pe, g_ps[:, j, u], [x[:, s, u, c * P:(c + 1) * P] for x in gu],
                                        [x[:, c, j * 512:(j + 1) * 512] for x in xT], c == 0, c == DC - 1)
                    if c == DC - 1:
                        last.then_inc(gated.sem, 1)
                    if c in (DC // 2 - 1, DC - 1):
                        x = TURNS[s][tile][c == DC - 1]
                        if x is not None and (x < 2 or not is_last(m)):
                            turn(m, x)

            def down(pr, j):
                if j == 0:
                    pe.wait_ge(w_lo.sem, w_lo.done(turn_no(pr * 2 + 1, 1)))
                pe.wait_ge(h_lo.sem, h_lo.done(pr * 4 + (2 + j)))
                for k in range(j * NT // 2, (j + 1) * NT // 2):
                    t, n = k // 2, k % 2
                    pe.wait_ge(added.sem, added.free(pr * NT + k, 2))
                    for s in range(2):
                        last = split_matmul(pe, y_ps[:, k % 2], [x[:, s, t * P:(t + 1) * P] for x in hT],
                                            [x[:, s, n * 512:(n + 1) * 512] for x in dn], s == 0, s == 1)
                    last.then_inc(tiles.sem, 1)

            def chunk(pr, m, s, i, first, units):
                for tile in range(4):
                    gate_up_tile(m, s, tile)
                    if s == 0 and tile % 2 == 0 and not (isinstance(pr, int) and pr < 0):
                        down(pr, tile // 2)

            def tail(pr):
                for j in range(2):
                    down(pr, j)

            gated.open(pe)
            tiles.open(pe)
            for x in range(2, 6):
                turn(-1, x)
            program(pe, chunk, tail)

        def destination(x, s):
            j, k = turned_part(x)
            sl = slice(k * 512, (k + 1) * 512)
            return [d[:, s, sl] for d in dn] if j == 2 else [g[:, 1 - s, j, sl] for g in gu]

        @block.scalar
        def _(act):
            def high(m, s, x):
                act.wait_ge(turned.sem, turned.done(turn_no(m, x)))
                act.activation(destination(x, s)[0], t_ps[:, x % 2], ACT.Copy).then_inc(w_hi.sem, 1)

            def gate(m, j):
                act.wait_ge(gated.sem, gated.done(m * 4 + 2 * j))
                act.wait_ge(gone.sem, gone.free(m * 2 + j, 2))
                act.activation(act_s[:, j], g_ps[:, j, 0], ACT.Silu).then_inc(silu.sem, 1)

            def hidden(m, s, j):
                act.wait_ge(gone.sem, gone.done(m * 2 + j))
                act.activation(hT[0][:, s, j * 512:(j + 1) * 512], hid[:, j], ACT.Copy).then_inc(h_hi.sem, 1)

            def chunk(pr, m, s, i, first, units):
                todo = items(s, m, pr)
                for p, (kind, x) in enumerate(todo):
                    if kind == "turn":
                        if x == 2:
                            act.wait_ge(gated.sem, gated.free(m * 4 + 3, 4))
                        if x == 0:
                            act.wait_ge(tiles.sem, tiles.free((pr + 1 - s) * NT + (NT - 1), NT))
                        high(m, s, x)
                    elif kind == "product":
                        gate(m, x)
                    elif kind == "hidden":
                        if s == 0:
                            act.wait_ge(tiles.sem, tiles.free((pr + 1) * NT + ((x + 1) * NT // 2 - 1), NT))
                        hidden(m, s, x)
                    for e, j in unit_steps(s, p, len(todo), first, units):
                        nf.above_scalar(act, i * UE + e, e % 2, [j])

            for x in range(2, 6):
                high(-1, 1, x)
            program(act, chunk, lambda pr: None)

        @block.vector
        def _(dve):
            def low(m, s, x):
                hi, lo = destination(x, s)
                dve.wait_ge(w_hi.sem, w_hi.done(turn_no(m, x)))
                dve.tensor_tensor(lo, t_ps[:, x % 2], f32(hi), ALU.subtract).then_inc(w_lo.sem, 1)

            def product(m, j):
                a = m * 2 + j
                dve.wait_ge(gated.sem, gated.done(m * 4 + (2 * j + 1)))
                dve.wait_ge(silu.sem, silu.done(a))
                dve.wait_ge(h_lo.sem, h_lo.free(a, 2))
                dve.tensor_tensor(hid[:, j], g_ps[:, j, 1], act_s[:, j], ALU.mult).then_inc(gone.sem, 1)

            def hidden_low(m, s, j):
                dve.wait_ge(h_hi.sem, h_hi.done(m * 2 + j))
                sl = (slice(None), s, slice(j * 512, (j + 1) * 512))
                dve.tensor_tensor(hT[1][sl], hid[:, j], f32(hT[0][sl]), ALU.subtract).then_inc(h_lo.sem, 1)

            def add(pr, k):
                t, h = k // 2, k % 2
                sl = slice(h * 512, (h + 1) * 512)
                dve.wait_ge(tiles.sem, tiles.done(pr * NT + k))
                dve.tensor_tensor(X[:, t, sl], y_ps[:, k % 2], X[:, t, sl], ALU.add).then_inc(added.sem, 1)

            def chunk(pr, m, s, i, first, units):
                todo = items(s, m, pr)
                for p, (kind, x) in enumerate(todo):
                    if kind == "turn":
                        low(m, s, x)
                    elif kind == "product":
                        product(m, x)
                    elif kind == "hidden":
                        hidden_low(m, s, x)
                    elif kind == "sum":
                        add(pr, x)
                    for e, j in unit_steps(s, p, len(todo), first, units):
                        nf.step_vector(dve, i * UE + e, e % 2, [j], i * (UE // 2) + e // 2)
                        if j == NS4 - 2 and has_next(i, e):
                            nf.max_vector(dve, i * UE + (e + 1), (e + 1) % 2, i * (UE // 2) + (e + 1) // 2,
                                          parts=2 if is_rest(i, e + 1) else 1)

            def tail(pr):
                for k in range(NT):
                    add(pr, k)

            w_lo.open(dve)
            gone.open(dve)
            h_lo.open(dve)
            added.open(dve)
            nf.open_vector(dve)
            for x in range(2, 6):
                low(-1, 1, x)
            nf.max_vector(dve, 0, 0, 0)
            program(dve, chunk, tail)


def build(nc, x, context, mask, wq, wk, wv, wo, router_w, router_b, expert_b, s1, z1, s2, z2,
          w1, w2, w3, cos_q, sin_q, cos_k, sin_k, out):
    def scratch(name, shape):
        return nc.dram_tensor(name, shape, F32, kind="Internal").ap()

    q_d = scratch("q_d", (HQ, DH, T))
    k_d = scratch("k_d", (B, HKV, DH, SK))
    v_d = scratch("v_d", (B, KT, P, D))
    o_d = scratch("o_d", (HQ, DH, T))
    dq = [scratch(f"dq{j + 1}", (HF, D)) for j in range(2)]
    dq3 = scratch("dq3", (D, HF))

    w = [w1, w2]
    w3_rows, dq3_rows = [a.rearrange("d h -> (d h)").rearrange("(r n) -> r n", n=D) for a in (w3, dq3)]
    WHOLE = HF // P

    def unit(a, k):
        return a[bass.ds(k * P, P), :]

    def rest(a):
        return a[WHOLE * P:, :].rearrange("r (a n) -> (r a) n", a=2)

    PQ, PK, PO = HQ // 2, HKV // 2, HQ // GRP // 2
    w3_left = range(PQ + PK, WHOLE)
    assert len(w3_left) == 1
    first_k, first_v, first_o, ready = 1, 1, 1 + PK, 1 + PK + 2 * PO
    units_v = [
        [([unit(w3_rows, k)], [unit(dq3_rows, k)], D) for k in w3_left]
        + [([rest(w3_rows)], [rest(dq3_rows)], D // 2)]
        + [([unit(w[j], 0)], [unit(dq[j], 0)], D) for j in range(2)],
        [([unit(w2, first_v + k)], [unit(dq[1], first_v + k)], D) for k in range(PK)]]
    units_k = [
        (lambda k: unit(w3_rows, k + PQ), lambda k: unit(dq3_rows, k + PQ)),
        (lambda k: unit(w1, k + first_k), lambda k: unit(dq[0], k + first_k))]

    spent.clear()
    with ExitStack() as ctx:
        X = ctx.enter_context(nc.sbuf_tensor("X", [P, TT, D], F32))
        ident = ctx.enter_context(nc.sbuf_tensor("ident", [P, P], F32))
        ident_bf = ctx.enter_context(nc.sbuf_tensor("ident_bf", [P, P], BF16))
        sharp = ctx.enter_context(nc.sbuf_tensor("sharp", [P, NS4], F32))
        constants_stage(nc, ident, ident_bf, sharp)
        with ExitStack() as c:
            xT = [c.enter_context(nc.sbuf_tensor(f"xT_{n}", [P, DC, T], F32R)) for n in ("h", "l")]
            norm_stage(nc, "n0", X, ident, xT=xT, x=x)
            project_stage(nc, "pq", xT, wq, HQ, lambda h: q_d[bass.ds(h, 1)].rearrange("a p n -> p (a n)"),
                          cos_q, sin_q, [(0, 512), (0, 512)], sharp,
                          lambda k: unit(w3_rows, k), lambda k: unit(dq3_rows, k))
        with ExitStack() as c:
            cT = [c.enter_context(nc.sbuf_tensor(f"cT_{n}", [P, DC, SK], F32R)) for n in ("h", "l")]
            for b in range(B):
                if b == 0:
                    context_stage(nc, f"c{b}", context[b], ident, cT)
                project_stage(nc, f"pk{b}", cT, wk, HKV, lambda h: k_d[b, bass.ds(h, 1)].rearrange("a p n -> p (a n)"),
                              cos_k, sin_k, [(0, 512), (512, 1024)], sharp, *units_k[b])
                value_stage(nc, f"v{b}", cT, wv, lambda t, h: v_d[b, t, :, h * 512:(h + 1) * 512], sharp, units_v[b],
                            ident, context[b + 1] if b + 1 < B else None)
        clear_stage(nc)
        attention_stage(nc, q_d, k_d, v_d, o_d, mask, ident)
        output_stage(nc, o_d, wo, X, sharp, lambda k, e: unit(w[e % 2], k * 2 + (first_o + e // 2)),
                     lambda k, e: unit(dq[e % 2], k * 2 + (first_o + e // 2)))
        with ExitStack() as c:
            xn = c.enter_context(nc.sbuf_tensor("xn", [P, TT, D], F32))
            norm_stage(nc, "n1", X, ident, xn_all=xn)
            router_stage(nc, X, xn, ident, router_w, router_b, expert_b)
            norm_stage(nc, "n2", X, ident, xn_all=xn)
            quantised_stage(nc, X, xn, ident_bf, context, (s1, z1, s2, z2))
        clear_stage(nc)
        with ExitStack() as c:
            xT = [c.enter_context(nc.sbuf_tensor(f"yT_{n}", [P, DC, T], F32R)) for n in ("h", "l")]
            norm_stage(nc, "n3", X, ident, xT=xT)
            ffn_stage(nc, xT, X, ident, dq, dq3, ready, sharp, lambda k, j: unit(w[j], k), lambda k, j: unit(dq[j], k),
                      [rest(a) for a in w], [rest(a) for a in dq], out)


_INS = ["x", "ctx_4096", "mask_BxSxS2_ff0", "L0_xattn_wq", "L0_xattn_wk", "L0_xattn_wv", "L0_xattn_wo",
        "L0_ffn_router_weight", "L0_ffn_router_bias", "L0_ffn_expert_bias", "L1_xattn_x1_scale",
        "L1_xattn_x1_zp", "L1_xattn_x2_scale", "L1_xattn_x2_zp", "L1_ffn_w1", "L1_ffn_w2", "L1_ffn_w3"]


def rotary_tables():
    inv = np.float32(1.0) / np.float32(10000.0) ** (np.arange(0, DH, 2, dtype=np.float32) / np.float32(DH))
    ang = inv[:, None] * np.arange(SK, dtype=np.float32)[None, :]
    cos = np.concatenate([np.cos(ang)] * 2).astype(np.float32)
    sin = np.concatenate([np.sin(ang), -np.sin(ang)]).astype(np.float32)
    scale = np.float64(DH) ** -0.5
    return ((cos[:, :SQ] * scale).astype(np.float32), (sin[:, :SQ] * scale).astype(np.float32), cos, sin)


def kernel(**inputs):
    import concourse.bacc as bacc
    from concourse.bass_utils import run_bass_kernel_spmd

    nc = bacc.Bacc("TRN2", target_bir_lowering=False, num_devices=1)
    arrays = {n: np.ascontiguousarray(inputs[n]) for n in _INS}
    arrays.update(zip(("cos_q", "sin_q", "cos_k", "sin_k"), rotary_tables()))
    args = [nc.dram_tensor(f"in_{n}", a.shape, mybir.dt.from_np(a.dtype), kind="ExternalInput").ap()
            for n, a in arrays.items()]
    out = nc.dram_tensor("out_x", (B, SQ, D), F32, kind="ExternalOutput").ap()
    build(nc, *args, out)
    r = run_bass_kernel_spmd(nc, [{f"in_{n}": a for n, a in arrays.items()}], core_ids=[0])
    return r.results[0]["out_x"]
```
